# Optimizing a Trainium2 kernel written in Bass

```python
import numpy as np
import jax
import jax.numpy as jnp

def _softmax(x, axis=-1):
    return jax.nn.softmax(x, axis=axis)

def _gelu(x):
    return jax.nn.gelu(x, approximate=True)

def _silu(x):
    return jax.nn.silu(x)

def _sigmoid(x):
    return jax.nn.sigmoid(x)

def _layernorm(x, axis=-1, eps=1e-05):
    m = jnp.mean(x, axis=axis, keepdims=True)
    v = jnp.var(x, axis=axis, keepdims=True)
    return (x - m) / jnp.sqrt(v + eps)

def _scatter_add(tgt, idx, src, axis=0):
    return tgt.at[idx].add(src)

def _segment_sum(src, seg, n):
    return jax.ops.segment_sum(src, seg, n)
kernel_name = 'mk_decoder_postln_d1_seqx_r2_0cd444'

def setup_inputs(seed: int=0):
    np.random.seed(seed)
    _w = jnp.asarray

    def _rec_inputs():
        import jax
        import jax.numpy as jnp
        _rk = jax.random.key(seed)
        x = -0.0002928 + 1 * jax.random.normal(jax.random.fold_in(_rk, 1), (8, 512, 512), jnp.float32)
        _lenS = 512 - jax.random.randint(jax.random.fold_in(_rk, 7), (8,), 0, max(1, 512 // 4) + 1, jnp.int32)
        _lenS2 = 512 - jax.random.randint(jax.random.fold_in(_rk, 8), (8,), 0, max(1, 512 // 4) + 1, jnp.int32)
        _ctx_1024P = jax.random.normal(jax.random.fold_in(_rk, 11), (8, 16, 512), jnp.float32)
        _ctx_1024c = jax.random.dirichlet(jax.random.fold_in(_rk, 511), 0.3 * jnp.ones((16,), jnp.float32), (8, 512))
        _ctx_1024t = jnp.einsum('bsk,bkd->bsd', _ctx_1024c, _ctx_1024P)
        _ctx_1024t = _ctx_1024t * jax.lax.rsqrt(jnp.mean(jnp.square(_ctx_1024t)) + 1e-12) * 0.953939
        ctx_1024 = -1.39393e-06 + 0.999914 * (_ctx_1024t + 0.3 * jax.random.normal(jax.random.fold_in(_rk, 611), (8, 512, 512), jnp.float32))
        return (x, ctx_1024)
    x, ctx_1024 = _rec_inputs()

    def _L0_attn_setup():
        import jax, jax.numpy as jnp
        import numpy as np
        B, S, D_MODEL, D_K = (4, 1024, 512, 1)
        D_QKV = D_MODEL * D_K
        MASK_NEG = -9000000000000000.0

        def _scaled_dot_product_attention(q, k, v):
            d_k = k.shape[-1]
            scores = jnp.einsum('bqd,bkd->bqk', q, k) / jnp.sqrt(jnp.float32(d_k))
            scores = jnp.triu(scores, k=0)
            scores = jnp.where(scores == 0, MASK_NEG, scores)
            attn = jax.nn.softmax(scores, axis=-1)
            return jnp.einsum('bqk,bkd->bqd', attn, v)
        key = jax.random.key(seed)
        kx, kw = jax.random.split(key)
        x = jax.random.normal(kx, (B, S, D_MODEL), dtype=jnp.float32)
        W = jax.random.normal(kw, (D_MODEL, 3 * D_QKV), dtype=jnp.float32) * (1.0 / np.sqrt(D_MODEL))
        return {'x': x, 'W': W}
    _L0_attn_all = _L0_attn_setup()
    _L0_attn_in = {k: v for k, v in _L0_attn_all.items() if k in ('W',)}
    del _L0_attn_all

    def _L0_xattn_setup():
        import jax, jax.numpy as jnp
        import numpy as np
        DIM_MODEL = 512
        DIM_K = 64
        DIM_V = 64
        H = 16
        B = 2
        S = 1024
        key = jax.random.key(seed)
        ks = jax.random.split(key, 11)
        s = 0.02
        return {'Q': jax.random.normal(ks[0], (B, S, DIM_MODEL), jnp.float32), 'K': jax.random.normal(ks[1], (B, S, DIM_MODEL), jnp.float32), 'V': jax.random.normal(ks[2], (B, S, DIM_MODEL), jnp.float32), 'Wq': jax.random.normal(ks[3], (DIM_MODEL, H * DIM_K), jnp.float32) * s, 'bq': jnp.zeros((H * DIM_K,), jnp.float32), 'Wk': jax.random.normal(ks[4], (DIM_MODEL, H * DIM_K), jnp.float32) * s, 'bk': jnp.zeros((H * DIM_K,), jnp.float32), 'Wv': jax.random.normal(ks[5], (DIM_MODEL, H * DIM_V), jnp.float32) * s, 'bv': jnp.zeros((H * DIM_V,), jnp.float32), 'Wo': jax.random.normal(ks[6], (H * DIM_V, DIM_MODEL), jnp.float32) * s, 'bo': jnp.zeros((DIM_MODEL,), jnp.float32)}
    _L0_xattn_all = _L0_xattn_setup()
    _L0_xattn_in = {k: v for k, v in _L0_xattn_all.items() if k in ('Wq', 'bq', 'Wk', 'bk', 'Wv', 'bv', 'Wo', 'bo')}
    del _L0_xattn_all

    def _L0_ffn_setup():
        import jax, jax.numpy as jnp
        import numpy as np
        E = 8
        K = 2
        D = 512
        B, N = (4, 2048)
        DC = 256
        key = jax.random.key(seed)
        ks = jax.random.split(key, 6)
        x = jax.random.normal(ks[0], (B, N, D), jnp.float32)
        cond = jax.random.normal(ks[1], (B, N, DC), jnp.float32)
        mask = jnp.ones((B, N), jnp.float32)
        W_shared = jax.random.normal(ks[2], (D, D), jnp.float32) * 0.02
        W_expert = jax.random.normal(ks[3], (D, D), jnp.float32) * 0.02
        W_gate = jax.random.normal(ks[4], (D, E - 1), jnp.float32) * 0.02
        bias = jnp.zeros((D,), jnp.float32)
        return dict(x=x, cond=cond, mask=mask, W_shared=W_shared, W_expert=W_expert, W_gate=W_gate, bias=bias)
    _L0_ffn_all = _L0_ffn_setup()
    _L0_ffn_in = {k: v for k, v in _L0_ffn_all.items() if k in ('cond', 'mask', 'W_shared', 'W_expert', 'W_gate', 'bias')}
    del _L0_ffn_all
    return {'x': x, 'ctx_1024': ctx_1024, 'L0_attn_W': _L0_attn_in['W'], 'L0_xattn_Wq': _L0_xattn_in['Wq'], 'L0_xattn_bq': _L0_xattn_in['bq'], 'L0_xattn_Wk': _L0_xattn_in['Wk'], 'L0_xattn_bk': _L0_xattn_in['bk'], 'L0_xattn_Wv': _L0_xattn_in['Wv'], 'L0_xattn_bv': _L0_xattn_in['bv'], 'L0_xattn_Wo': _L0_xattn_in['Wo'], 'L0_xattn_bo': _L0_xattn_in['bo'], 'L0_ffn_cond': _L0_ffn_in['cond'], 'L0_ffn_mask': _L0_ffn_in['mask'], 'L0_ffn_W_shared': _L0_ffn_in['W_shared'], 'L0_ffn_W_expert': _L0_ffn_in['W_expert'], 'L0_ffn_W_gate': _L0_ffn_in['W_gate'], 'L0_ffn_bias': _L0_ffn_in['bias']}

def reference(x, ctx_1024, L0_attn_W, L0_xattn_Wq, L0_xattn_bq, L0_xattn_Wk, L0_xattn_bk, L0_xattn_Wv, L0_xattn_bv, L0_xattn_Wo, L0_xattn_bo, L0_ffn_cond, L0_ffn_mask, L0_ffn_W_shared, L0_ffn_W_expert, L0_ffn_W_gate, L0_ffn_bias):
    import jax
    import jax.numpy as jnp

    def _L0_attn_ref(x, W):
        import jax, jax.numpy as jnp
        import numpy as np
        B, S, D_MODEL, D_K = (4, 1024, 512, 1)
        D_QKV = D_MODEL * D_K
        MASK_NEG = -9000000000000000.0

        def _scaled_dot_product_attention(q, k, v):
            d_k = k.shape[-1]
            scores = jnp.einsum('bqd,bkd->bqk', q, k) / jnp.sqrt(jnp.float32(d_k))
            scores = jnp.triu(scores, k=0)
            scores = jnp.where(scores == 0, MASK_NEG, scores)
            attn = jax.nn.softmax(scores, axis=-1)
            return jnp.einsum('bqk,bkd->bqd', attn, v)
        qkv = jnp.einsum('bsd,df->bsf', x, W)
        q, k, v = jnp.split(qkv, 3, axis=-1)
        return _scaled_dot_product_attention(q, k, v)

    def _L0_xattn_ref(Q, K, V, Wq, bq, Wk, bk, Wv, bv, Wo, bo):
        import jax, jax.numpy as jnp
        import numpy as np
        DIM_MODEL = 512
        DIM_K = 64
        DIM_V = 64
        H = 16
        B = 2
        S = 1024
        b, len_q = (Q.shape[0], Q.shape[1])
        q = (Q @ Wq + bq).reshape(b, len_q, H, DIM_K).transpose(0, 2, 1, 3)
        k = (K @ Wk + bk).reshape(b, K.shape[1], H, DIM_K).transpose(0, 2, 1, 3)
        v = (V @ Wv + bv).reshape(b, V.shape[1], H, DIM_V).transpose(0, 2, 1, 3)
        scale = 1.0 / np.sqrt(b).astype(np.float32)
        att = jnp.einsum('bhqd,bhkd->bhqk', q * scale, k)
        att = jax.nn.softmax(att, axis=-1)
        out = jnp.einsum('bhqk,bhkd->bhqd', att, v)
        out = out.transpose(0, 2, 1, 3).reshape(b, len_q, H * DIM_V)
        return out @ Wo + bo

    def _L0_ffn_ref(x, cond, mask, W_shared, W_expert, W_gate, bias):
        import jax, jax.numpy as jnp
        import numpy as np
        E = 8
        K = 2
        D = 512
        B, N = (4, 2048)
        DC = 256
        b, n, d = x.shape
        T = b * n
        xf = x.reshape(T, d)
        scores = jax.nn.softmax(xf @ W_gate, axis=-1)
        expert_weights, _ = jax.lax.top_k(scores, K)
        expert_weights = expert_weights / expert_weights.sum(-1, keepdims=True)
        expert_indices = (jnp.arange(T * K) % E).reshape(T, K)
        te = expert_indices.reshape(-1)
        w = expert_weights.reshape(-1)
        capacity = K * T // E
        order = jnp.argsort(te, stable=True)
        sorted_e = te[order]
        hist = jnp.bincount(te, length=E)
        starts = jnp.concatenate([jnp.zeros((1,), hist.dtype), jnp.cumsum(hist)[:-1]])
        pos = jnp.arange(T * K) - starts[sorted_e]
        valid = pos < capacity
        dest = jnp.where(valid, sorted_e * capacity + pos, E * capacity)
        tok = order // K
        gathered = jnp.zeros((E * capacity + 1, d), x.dtype).at[dest].set(xf[tok])
        gathered = gathered[:-1]
        y = gathered @ W_expert.T
        contrib = w[order][:, None] * y[jnp.minimum(dest, E * capacity - 1)]
        moe_out = jnp.zeros((T, d), x.dtype).at[tok].add(jnp.where(valid[:, None], contrib, 0.0))
        shared = xf @ W_shared.T
        out = (shared + moe_out + bias).reshape(b, n, d)
        return out
    x = _layernorm(x + _L0_attn_ref(x, L0_attn_W), axis=-1)
    x = _layernorm(x + _L0_xattn_ref(x, ctx_1024, ctx_1024, L0_xattn_Wq, L0_xattn_bq, L0_xattn_Wk, L0_xattn_bk, L0_xattn_Wv, L0_xattn_bv, L0_xattn_Wo, L0_xattn_bo), axis=-1)
    x = _layernorm(x + _L0_ffn_ref(x, L0_ffn_cond, L0_ffn_mask, L0_ffn_W_shared, L0_ffn_W_expert, L0_ffn_W_gate, L0_ffn_bias), axis=-1)
    return x

_drawn_inputs = setup_inputs


def setup_inputs(seed=0):
    import zlib

    import numpy as np

    out = dict(_drawn_inputs(seed))
    spreads = {'L0_xattn_bq': (0.0, 0.8),
     'L0_xattn_bk': (0.0, 0.8),
     'L0_xattn_bv': (0.0, 0.1),
     'L0_xattn_bo': (0.0, 0.1),
     'L0_ffn_bias': (0.0, 0.1)}
    factors = {'L0_ffn_W_gate': 8.0}
    for name, (base, spread) in spreads.items():
        noise = np.random.default_rng([zlib.crc32(name.encode()), seed]).standard_normal(out[name].shape)
        drawn = base * np.exp(spread * noise) if base else spread * noise
        out[name] = jnp.asarray(drawn.astype(out[name].dtype))
    for name, factor in factors.items():
        out[name] = (out[name] * factor).astype(out[name].dtype)
    return out
```

```python
from contextlib import ExitStack

import concourse.bass as bass
from concourse import mybir

F32 = mybir.dt.float32
F32R = mybir.dt.float32r
ALU = mybir.AluOpType
ACT = mybir.ActivationFunctionType
AX = mybir.AxisListType

P = 128
HI, LO = 0, 1
EPS = 1e-5
NEG = 9000000000000000.0
TERMS = ((HI, HI), (HI, LO), (LO, HI))


class Scope:

    def __init__(self, nc, ctx, stage):
        self.nc, self.ctx, self.stage = nc, ctx, stage

    def sb(self, name, shape, dt=F32):
        return self.ctx.enter_context(self.nc.sbuf_tensor(f"{self.stage}_{name}", shape, dt))

    def ps(self, name, shape):
        return self.ctx.enter_context(self.nc.psum_tensor(f"{self.stage}_{name}", shape, F32))

    def sem(self, name):
        return self.ctx.enter_context(self.nc.semaphore(f"{self.stage}_{name}"))


def as_f32(ap):
    return ap.bitcast(F32)


def three_pass(nc, out, stationary, moving, depth):
    last = (depth - 1, TERMS[-1])
    for k in range(depth):
        for s, m in TERMS:
            ins = nc.tensor.matmul(out, stationary(s, k), moving(m, k), start=(k == 0 and s == m == HI),
                                   stop=((k, (s, m)) == last))
    return ins


class Norm:

    def __init__(self, sc, T, D, name="norm", credit=0):
        self.T, self.D, self.credit = T, D, credit
        self.stat = sc.sb(f"{name}_stat", [P, T, 6])
        self.mean, self.var, self.std = (sc.sb(f"{name}_{n}", [P, T]) for n in ("mean", "variance", "std"))
        self.r, self.t, self.u = (sc.sb(f"{name}_{n}", [P, T]) for n in ("r", "t", "u"))
        self.summed, self.have_stat, self.step, self.have_var, self.have_std, self.normed = (
            sc.sem(f"{name}_{n}") for n in ("summed", "have_stat", "step", "have_var", "have_std", "normed"))

    def link(self, nc, count, ins):
        count[0] = count[0] + 1
        ins.then_inc(self.step, 1)
        nc.vector.wait_ge(self.step, count[0])

    VARIANCE_STEPS, STEPS = 6, 11

    def stats(self, nc, b, i, y):
        nc.vector.wait_ge(self.summed, self.T * b + i + 1 + self.credit)
        nc.vector.bn_stats(self.stat[:, i, :], y[:, i, :]).then_inc(self.have_stat, 1)

    def variance(self, nc, b):
        v, st, n = nc.vector, self.stat, [self.STEPS * b]
        v.wait_ge(self.have_stat, self.T * b + self.T)
        self.link(nc, n, v.tensor_tensor(self.mean[:, :], st[:, :, 1], st[:, :, 4], ALU.add))
        self.link(nc, n, v.tensor_scalar(self.mean[:, :], self.mean[:, :], 0.5, None, ALU.mult))
        self.link(nc, n, v.tensor_tensor(self.t[:, :], st[:, :, 1], st[:, :, 4], ALU.subtract))
        self.link(nc, n, v.tensor_tensor(self.t[:, :], self.t[:, :], self.t[:, :], ALU.mult))
        self.link(nc, n, v.tensor_tensor(self.u[:, :], st[:, :, 2], st[:, :, 5], ALU.add))
        self.link(nc, n, v.tensor_scalar(self.u[:, :], self.u[:, :], 1.0 / self.D, EPS, ALU.mult, ALU.add))
        v.scalar_tensor_tensor(out=self.var[:, :], in0=self.t[:, :], scalar=0.25, in1=self.u[:, :], op0=ALU.mult,
                               op1=ALU.add).then_inc(self.have_var, 1)

    def root(self, nc, b):
        nc.scalar.wait_ge(self.have_var, b + 1)
        nc.scalar.activation(self.std[:, :], self.var[:, :], ACT.Sqrt).then_inc(self.have_std, 1)

    def scale(self, nc, b, out, y):
        v, n = nc.vector, [self.STEPS * b + self.VARIANCE_STEPS]
        v.wait_ge(self.have_std, b + 1)
        self.link(nc, n, v.reciprocal(self.r[:, :], self.std[:, :]))
        self.link(nc, n, v.tensor_tensor(self.t[:, :], self.r[:, :], self.r[:, :], ALU.mult))
        self.link(nc, n, v.tensor_tensor(self.t[:, :], self.t[:, :], self.var[:, :], ALU.mult))
        self.link(nc, n, v.tensor_scalar(self.t[:, :], self.t[:, :], -0.5, 1.5, ALU.mult, ALU.add))
        self.link(nc, n, v.tensor_tensor(self.r[:, :], self.r[:, :], self.t[:, :], ALU.mult))
        for i in range(self.T):
            v.tensor_scalar(out[:, i, :], y[:, i, :], self.mean[:, i:i + 1], self.r[:, i:i + 1], ALU.subtract,
                            ALU.mult).then_inc(self.normed, 1)


def load_weights(nc, wqT, wkT, wv, A, WV, D):
    T = D // P
    with ExitStack() as ctx:
        sc = Scope(nc, ctx, "w")
        raw = sc.sb("raw", [P, 3, T, D])
        part = sc.sb("part", [P, 2, 2, T, D], F32R)
        pa = sc.ps("a", [P, T, D])
        loaded = [sc.sem(f"loaded{n}") for n in range(3)]
        hi_done, lo_done, a_mm, a_hi, a_lo = (sc.sem(n) for n in ("hi_done", "lo_done", "a_mm", "a_hi", "a_lo"))

        def dest(w, h):
            return WV[:, h, :, :] if w == 2 else part[:, w, h, :, :]

        with nc.Block() as block:

            @block.sync
            def _(sp):
                for w, src in enumerate((wqT, wkT, wv)):
                    sp.dma_start(raw[:, w, :, :], src.rearrange("(k p) n -> p k n", p=P)).then_inc(loaded[w], 16)

            @block.scalar
            def _(act):
                for w in range(3):
                    act.wait_ge(loaded[w], 16)
                    for k in range(T):
                        nc.scalar.copy(dest(w, HI)[:, k, :], raw[:, w, k, :]).then_inc(hi_done, 1)
                for m in range(T):
                    act.wait_ge(a_mm, m + 1)
                    nc.scalar.activation(A[:, HI, m, :], pa[:, m, :], ACT.Copy,
                                         scale=float(D) ** -0.5).then_inc(a_hi, 1)

            @block.vector
            def _(dve):
                for w in range(3):
                    for k in range(T):
                        dve.wait_ge(hi_done, T * w + k + 1)
                        nc.vector.tensor_tensor(dest(w, LO)[:, k, :], raw[:, w, k, :], as_f32(dest(w, HI)[:, k, :]),
                                                ALU.subtract).then_inc(lo_done, 1)
                for m in range(T):
                    dve.wait_ge(a_hi, m + 1)
                    nc.vector.scalar_tensor_tensor(out=A[:, LO, m, :], in0=pa[:, m, :], scalar=float(D) ** -0.5,
                                                   in1=as_f32(A[:, HI, m, :]), op0=ALU.mult,
                                                   op1=ALU.subtract).then_inc(a_lo, 1)

            @block.tensor
            def _(pe):
                pe.wait_ge(lo_done, 2 * T)
                for m in range(T):
                    three_pass(nc, pa[:, m, :], lambda h, k: part[:, 0, h, k, m * P:(m + 1) * P],
                               lambda h, k: part[:, 1, h, k, :], T).then_inc(a_mm, 1)


def self_attention(nc, x, xT, wpair, A, WV, ident, x1, x1T, wparts, NB, S, D, QSCALE):
    T, K = S // P, D // P
    with ExitStack() as ctx:
        sc = Scope(nc, ctx, "s")
        xraw = sc.sb("xraw", [P, K, S])
        xp = sc.sb("xp", [P, 2, K, S], F32R)
        qp = sc.sb("qp", [P, 2, K, S], F32R)
        vp = sc.sb("vp", [P, 2, T, D], F32R)
        y = sc.sb("y", [P, T, D])
        x1t = sc.sb("x1t", [P, K, S])
        strip = sc.sb("strip", [P, (2 * T - 1) * P])
        upper = sc.sb("upper", [P, T, S])
        ms = sc.sb("ms", [P, T, S])
        gone = sc.sb("gone", [P, T, S])
        prob = sc.sb("prob", [P, T, S])
        pt = sc.sb("pt", [P, 2, T, S], F32R)
        negmax, den, rden = sc.sb("negmax", [P, T]), sc.sb("den", [P, T]), sc.sb("rden", [P, T])
        NWP = 4
        wraw, wtmp = sc.sb("wraw", [P, NWP, D]), sc.sb("wtmp", [P, NWP, D])
        wsp = sc.sb("wsp", [P, NWP, 2, D], F32R)
        proj, spsum = sc.ps("proj", [P, 2, 512]), sc.ps("score", [P, 2, 512])
        tpsum, opsum = sc.ps("turned", [P, 2, 512]), sc.ps("av", [P, 2, 512])
        norm = Norm(sc, T, D)
        passed = sc.sem("passed")

        (xT_loaded, x_loaded, x_hi, x_lo, q_mm, q_hi, q_lo, s_mm, v_mm, v_hi, v_lo, t_mm, pt_hi, pt_lo, av_mm,
         x1t_mm, x1t_out, strip_step, cut, is_zero, masked, prob_exp, have_rden, prob_ready, y_stored,
         x1t_stored, base, w_loaded, w_tmp, w_hi, w_lo, w_stored) = (sc.sem(n) for n in (
             "xT_loaded", "x_loaded", "x_hi", "x_lo", "q_mm", "q_hi", "q_lo", "s_mm", "v_mm", "v_hi", "v_lo",
             "t_mm", "pt_hi", "pt_lo", "av_mm", "x1t_mm", "x1t_out", "strip_step", "cut", "is_zero", "masked",
             "prob_exp", "have_rden", "prob_ready", "y_stored", "x1t_stored", "base", "w_loaded", "w_tmp", "w_hi",
             "w_lo", "w_stored"))

        def batches(eng, body):
            body(0, True, False)
            with eng.Fori(1, NB - 1) as b:
                body(b, False, False)
            body(NB - 1, False, True)

        with nc.Block() as block:

            @block.sync
            def _(sp):
                def load_xT(b):
                    sp.dma_start(xraw[:, :, :], xT[b].rearrange("(k p) n -> p k n", p=P)).then_inc(xT_loaded, 16)

                def store_x1T(b):
                    sp.wait_ge(x1t_out, K * b + K)
                    sp.dma_start(x1T[b], x1t[:, :, :]).then_inc(x1t_stored, 16)

                def body(b, first, last):
                    if first:
                        load_xT(b)
                    if not last:
                        sp.wait_ge(x_lo, K * b + K)
                        load_xT(b + 1)
                    if not first:
                        sp.wait_ge(w_tmp, NWP * b)
                        sp.wait_ge(w_lo, NWP * b)
                    sp.dma_start(wraw[:, :, :], wpair[b].rearrange("w p n -> p w n")).then_inc(w_loaded, 16)
                    if not first:
                        store_x1T(b - 1)
                        sp.wait_ge(y_stored, 16 * b)
                        sp.wait_ge(x1t_mm, K * b)
                    sp.dma_start(y[:, :, :], x[b].rearrange("(t p) d -> p t d", p=P)).then_inc(x_loaded, 16)
                    sp.wait_ge(w_lo, NWP * b + NWP)
                    for w, dst in enumerate(wparts):
                        sp.dma_start(dst[b], as_f32(wsp[:, w, :, :])).then_inc(w_stored, 16)
                    sp.wait_ge(norm.normed, T * b + T)
                    sp.dma_start(x1[b].rearrange("(t p) d -> p t d", p=P), y[:, :, :]).then_inc(y_stored, 16)

                batches(sp, body)
                store_x1T(NB - 1)
                sp.wait_ge(y_stored, 16 * NB)
                sp.wait_ge(x1t_stored, 16 * NB + 16)
                sp.wait_ge(w_stored, 16 * NWP * NB)

            @block.gpsimd
            def _(pool):
                nc.gpsimd.memset(strip[:, :(T - 1) * P], 0.0).then_inc(strip_step, 1)
                nc.gpsimd.memset(strip[:, (T - 1) * P:], 1.0).then_inc(strip_step, 1)
                pool.wait_ge(strip_step, 2)
                tri = strip[:, (T - 1) * P:T * P]
                nc.gpsimd.affine_select(out=tri, in_=tri, compare_op=ALU.is_ge, fill=0.0, base=0, pattern=[[1, P]],
                                        channel_multiplier=-1).then_inc(strip_step, 1)

                def body(b, first, last):
                    for i in range(T):
                        pool.wait_ge(have_rden, T * b + i + 1)
                        pool.sem_inc(passed, 1)
                        nc.gpsimd.tensor_scalar(prob[:, i, :], prob[:, i, :], rden[:, i:i + 1], 1.0, ALU.mult,
                                                ALU.mult).then_inc(prob_ready, 1)
                    pool.wait_ge(w_loaded, 16 * b + 16)
                    if not first:
                        pool.wait_ge(w_lo, NWP * b)
                    pool.sem_inc(passed, 1)
                    for w, scale in enumerate((QSCALE, 1.0, 1.0, 1.0)):
                        nc.gpsimd.tensor_scalar(wtmp[:, w, :], wraw[:, w, :], scale, 1.0, ALU.mult,
                                                ALU.mult).then_inc(w_tmp, 1)
                    if not first:
                        pool.wait_ge(w_stored, 16 * NWP * b)
                    for w in range(NWP):
                        pool.wait_ge(w_tmp, NWP * b + w + 1)
                        pool.sem_inc(passed, 1)
                        nc.gpsimd.tensor_scalar(wsp[:, w, HI, :], wtmp[:, w, :], 1.0, 1.0, ALU.mult,
                                                ALU.mult).then_inc(w_hi, 1)
                        pool.wait_ge(w_hi, NWP * b + w + 1)
                        nc.gpsimd.tensor_tensor(wsp[:, w, LO, :], wtmp[:, w, :], as_f32(wsp[:, w, HI, :]),
                                                ALU.subtract).then_inc(w_lo, 1)

                batches(pool, body)

            @block.scalar
            def _(act):
                def split_x(b, first):
                    act.wait_ge(xT_loaded, 16 * b + 16)
                    if not first:
                        act.wait_ge(s_mm, T * b)
                        act.wait_ge(v_mm, T * b)
                    for k in range(K):
                        nc.scalar.copy(xp[:, HI, k, :], xraw[:, k, :]).then_inc(x_hi, 1)

                def body(b, first, last):
                    if first:
                        split_x(b, True)
                    for m in range(K):
                        act.wait_ge(q_mm, K * b + m + 1)
                        nc.scalar.copy(qp[:, HI, m, :], proj[:, m % 2, :]).then_inc(q_hi, 1)
                    for i in range(T):
                        act.wait_ge(masked, T * b + i + 1)
                        if not first:
                            act.wait_ge(t_mm, T * b)
                        nc.scalar.activation(prob[:, i, :], ms[:, i, :], ACT.Exp, bias=negmax[:, i:i + 1], scale=-1.0,
                                             accum_out=den[:, i:i + 1]).then_inc(prob_exp, 1)
                    for i in range(T):
                        act.wait_ge(v_mm, T * b + i + 1)
                        if not first:
                            act.wait_ge(av_mm, T * b)
                        nc.scalar.copy(vp[:, HI, i, :], proj[:, i % 2, :]).then_inc(v_hi, 1)
                    for k in range(T):
                        act.wait_ge(t_mm, T * b + k + 1)
                        nc.scalar.copy(pt[:, HI, k, :], tpsum[:, k % 2, :]).then_inc(pt_hi, 1)
                    if not last:
                        split_x(b + 1, False)
                    norm.root(nc, b)

                batches(act, body)

            @block.vector
            def _(dve):
                dve.sem_inc(x1t_stored, 16)
                for i in range(1, T):
                    nc.vector.memset(ms[:, i, :i * P], NEG).then_inc(base, 1)

                def split_x(b):
                    for k in range(K):
                        dve.wait_ge(x_hi, K * b + k + 1)
                        nc.vector.tensor_tensor(xp[:, LO, k, :], xraw[:, k, :], as_f32(xp[:, HI, k, :]),
                                                ALU.subtract).then_inc(x_lo, 1)

                def turn_x1(b):
                    for k in range(K):
                        dve.wait_ge(x1t_mm, K * b + k + 1)
                        nc.vector.tensor_copy(x1t[:, k, :], tpsum[:, k % 2, :]).then_inc(x1t_out, 1)

                def cut_tile(b, i, first):
                    dve.wait_ge(s_mm, T * b + i + 1)
                    if first:
                        dve.wait_ge(strip_step, 3)
                    else:
                        dve.wait_ge(masked, T * b - T + i + 1)
                        dve.wait_ge(prob_exp, T * b - T + i + 1)
                    nc.vector.tensor_tensor(upper[:, i, i * P:], spsum[:, i % 2, i * P:],
                                            strip[:, (T - 1) * P:(2 * T - 1 - i) * P], ALU.mult).then_inc(cut, 1)

                def recip(b, i):
                    dve.wait_ge(prob_exp, T * b + i + 1)
                    nc.vector.reciprocal(rden[:, i:i + 1], den[:, i:i + 1]).then_inc(have_rden, 1)

                def body(b, first, last):
                    if first:
                        split_x(b)
                    for m in range(K):
                        dve.wait_ge(q_hi, K * b + m + 1)
                        nc.vector.tensor_tensor(qp[:, LO, m, :], proj[:, m % 2, :], as_f32(qp[:, HI, m, :]),
                                                ALU.subtract).then_inc(q_lo, 1)
                    if not first:
                        dve.wait_ge(x1t_stored, 16 * b)
                        turn_x1(b - 1)
                    for i in range(T):
                        if i == 0:
                            cut_tile(b, 0, first)
                        dve.wait_ge(cut, T * b + i + 1)
                        nc.vector.tensor_scalar(gone[:, i, i * P:], upper[:, i, i * P:], 0.0, -NEG, ALU.is_equal,
                                                ALU.mult).then_inc(is_zero, 1)
                        dve.wait_ge(is_zero, T * b + i + 1)
                        if i + 1 < T:
                            cut_tile(b, i + 1, first)
                        else:
                            recip(b, i - 1)
                        if first and i == 0:
                            dve.wait_ge(base, T - 1)
                        nc.vector.tensor_tensor_reduce(ms[:, i, i * P:], upper[:, i, i * P:], gone[:, i, i * P:], -1.0,
                                                       NEG, ALU.add, ALU.min, negmax[:, i:i + 1]).then_inc(masked, 1)
                        if 0 < i < T - 1:
                            recip(b, i - 1)
                    recip(b, T - 1)
                    for i in range(T):
                        dve.wait_ge(v_hi, T * b + i + 1)
                        nc.vector.tensor_tensor(vp[:, LO, i, :], proj[:, i % 2, :], as_f32(vp[:, HI, i, :]),
                                                ALU.subtract).then_inc(v_lo, 1)
                    for k in range(T):
                        dve.wait_ge(pt_hi, T * b + k + 1)
                        nc.vector.tensor_tensor(pt[:, LO, k, :], tpsum[:, k % 2, :], as_f32(pt[:, HI, k, :]),
                                                ALU.subtract).then_inc(pt_lo, 1)
                    if not last:
                        split_x(b + 1)
                    dve.wait_ge(x_loaded, 16 * b + 16)
                    for i in range(T):
                        dve.wait_ge(av_mm, T * b + i + 1)
                        nc.vector.tensor_tensor(y[:, i, :], opsum[:, i % 2, :], y[:, i, :],
                                                ALU.add).then_inc(norm.summed, 1)
                        norm.stats(nc, b, i, y)
                    norm.variance(nc, b)
                    norm.scale(nc, b, y, y)

                batches(dve, body)
                dve.wait_ge(x1t_stored, 16 * NB)
                turn_x1(NB - 1)

            @block.tensor
            def _(pe):
                def turn_x1(b, first=False):
                    pe.wait_ge(norm.normed, T * b + T)
                    for k in range(K):
                        if k < 2:
                            pe.wait_ge(pt_lo, T * b + T)
                        else:
                            pe.wait_ge(x1t_out, K * b + k - 1)
                        for i in range(T):
                            t = nc.tensor.transpose(tpsum[:, k % 2, i * P:(i + 1) * P], y[:, i, k * P:(k + 1) * P],
                                                    ident[:, :])
                        t.then_inc(x1t_mm, 1)

                def body(b, first, last):
                    pe.wait_ge(x_lo, K * b + K)
                    for m in range(K):
                        if m < 2 and not first:
                            pe.wait_ge(v_lo, T * b - 2 + m + 1)
                        if m >= 2:
                            pe.wait_ge(q_lo, K * b + m - 1)
                        three_pass(nc, proj[:, m % 2, :], lambda h, k: A[:, h, k, m * P:(m + 1) * P],
                                   lambda h, k: xp[:, h, k, :], K).then_inc(q_mm, 1)
                    if not first:
                        turn_x1(b - 1)
                    pe.wait_ge(q_lo, K * b + K)
                    for i in range(T):
                        if i < 2:
                            if not first:
                                pe.wait_ge(cut, T * b - 2 + i + 1)
                        else:
                            pe.wait_ge(cut, T * b + i - 1)
                        three_pass(nc, spsum[:, i % 2, i * P:], lambda h, k: qp[:, h, k, i * P:(i + 1) * P],
                                   lambda h, k: xp[:, h, k, i * P:], K).then_inc(s_mm, 1)
                    for i in range(T):
                        if i >= 2:
                            pe.wait_ge(v_lo, T * b + i - 1)
                        three_pass(nc, proj[:, i % 2, :], lambda h, k: xp[:, h, k, i * P:(i + 1) * P],
                                   lambda h, k: WV[:, h, k, :], K).then_inc(v_mm, 1)
                    for k in range(T):
                        if k < 2:
                            if not first:
                                pe.wait_ge(x1t_out, K * b)
                        else:
                            pe.wait_ge(pt_lo, T * b + k - 1)
                        for i in range(T):
                            if k == 0:
                                pe.wait_ge(prob_ready, T * b + i + 1)
                            t = nc.tensor.transpose(tpsum[:, k % 2, i * P:(i + 1) * P],
                                                    prob[:, i, k * P:(k + 1) * P], ident[:, :])
                        t.then_inc(t_mm, 1)
                    pe.wait_ge(v_lo, T * b + T)
                    pe.wait_ge(pt_lo, T * b + T)
                    for i in range(T):
                        if i < 2:
                            if not first:
                                pe.wait_ge(norm.summed, T * b - 2 + i + 1)
                        else:
                            pe.wait_ge(norm.summed, T * b + i - 1)
                        three_pass(nc, opsum[:, i % 2, :], lambda h, k: pt[:, h, k, i * P:(i + 1) * P],
                                   lambda h, k: vp[:, h, k, :], T).then_inc(av_mm, 1)

                batches(pe, body)
                turn_x1(NB - 1)


def cross_attention(nc, y_steps, x1T, ctxT, wqparts, wkparts, wvparts, woparts, bq, bk, bv, ident, NB, S, D, H, DK):
    T, K = S // P, D // P
    HALVES, HH = 2, H // 2
    PAIRS = HH // 2
    CH = HH * DK
    assert 2 * DK == P and CH == 512 and S == 512 and PAIRS % 2 == 0
    with ExitStack() as ctx:
        sc = Scope(nc, ctx, "c")
        WV = sc.sb("WV", [P, 2, K, H * DK], F32R)
        WO = sc.sb("WO", [P, 2, H // 2, D], F32R)
        xp = sc.sb("xp", [P, 2, K, S], F32R)
        cp = sc.sb("cp", [P, 2, K, S], F32R)
        wk, wq = sc.sb("wk", [P, 2, K, P], F32R), sc.sb("wq", [P, 2, K, P], F32R)
        qs = sc.sb("qs", [P, 2, 2, S], F32R)
        ks = sc.sb("ks", [P, 2, 2, 2, S], F32R)
        vs = sc.sb("vs", [P, T, HH, 2 * DK], F32R)
        prob = sc.sb("prob", [P, 2, T, S])
        pt = sc.sb("pt", [P, 2, 2, S], F32R)
        opart, osum = sc.sb("opart", [P, S]), sc.sb("osum", [P, S])
        op = sc.sb("op", [P, 2, PAIRS, S], F32R)
        y = sc.sb("y", [P, T, D])
        negmax, den, rden = sc.sb("negmax", [P, 2, T]), sc.sb("den", [P, 2, T]), sc.sb("rden", [P, 2, T])
        bq_raw = sc.sb("bq_raw", [P, H // 2])
        bqs, bks, bvs = sc.sb("bq", [P, H // 2]), sc.sb("bk", [P, H // 2]), sc.sb("bv", [DK, H])
        projp, spsum = sc.ps("proj", [P, 2, 512]), sc.ps("score", [P, 2, 512])
        tpsum, opsum = sc.ps("turned", [P, 2, 512]), sc.ps("av", [P, 2, 512])
        wo_bank = [spsum[:, 0, :], spsum[:, 1, :], tpsum[:, 0, :], tpsum[:, 1, :]]

        (consts, bias_ready, ctx_loaded, x_loaded, raw_hi, raw_lo, wk_loaded, wq_loaded, proj_mm, proj_hi, proj_lo,
         s_mm, smax, p_exp, have_rden, p_ready, t_mm, pt_hi, pt_lo, av_mm, o_part, o_sum, op_hi, op_lo, wo_mm,
         wo_out, y_loaded, y_stored) = (sc.sem(n) for n in (
             "consts", "bias_ready", "ctx_loaded", "x_loaded", "raw_hi", "raw_lo", "wk_loaded", "wq_loaded", "proj_mm",
             "proj_hi", "proj_lo", "s_mm", "smax", "p_exp", "have_rden", "p_ready", "t_mm", "pt_hi", "pt_lo",
             "av_mm", "o_part", "o_sum", "op_hi", "op_lo", "wo_mm", "wo_out", "y_loaded", "y_stored"))
        passed = sc.sem("passed")
        k_doubled = [sc.sem(f"k_doubled{n}") for n in range(2)]
        wv_loaded = [sc.sem(f"wv_loaded{n}") for n in range(HALVES)]
        wo_loaded = sc.sem("wo_loaded")

        CREDIT = 16
        credited = {"pe": (s_mm, t_mm, av_mm, wo_mm, proj_mm), "act": (p_exp,), "dve": (pt_lo, o_sum, wo_out, proj_lo),
                    "pool": (op_lo,)}

        def done(n):
            return n + CREDIT

        ORDER = ["K0", "Q0", "V0", "V1", "K1", "V2", "Q1", "V3", "K2", "Q2", "K3", "Q3"]
        assert PAIRS == 4 and T == 4
        NPROJ = len(ORDER)
        STEPS = [1 if name[0] == "V" else 2 for name in ORDER]
        NSTEP = sum(STEPS)

        def use(name):
            return ORDER.index(name)

        def step(name, head=1):
            n = use(name)
            return sum(STEPS[:n + 1]) - (1 - head if name[0] != "V" else 0)

        def groups(eng, body):
            with eng.Fori(0, HALVES) as h:
                with eng.Fori(0, NB - 1) as b:
                    body(h * NB + b, h, b, b + 1, h)
                body(h * NB + NB - 1, h, NB - 1, 0, h * -1 + 1)

        TILES, LEAD = T * HH, 5
        OPENING = ["K0", "Q0", "V0", "V1", 0, 1, "K1", 2, "V2", 3, "Q1", 4, "V3"]
        LATER = ["K2", "Q2", "K3", "Q3"]
        THIRDS = 3
        assert [o for o in OPENING if isinstance(o, str)] + LATER == ORDER
        assert [o for o in OPENING if isinstance(o, int)] == list(range(LEAD))

        def schedule(split_proj, maximum, recip, exponential, pt_tile, o_half):
            for o in OPENING:
                if isinstance(o, str):
                    split_proj(o)
                else:
                    maximum(o)
                    exponential(o)
                    if o:
                        recip(o - 1)
            for t in range(TILES):
                n, i = divmod(t, T)
                if t + LEAD < TILES:
                    maximum(t + LEAD)
                if t + LEAD <= TILES:
                    recip(t + LEAD - 1)
                pt_tile(t)
                if t + LEAD < TILES:
                    exponential(t + LEAD)
                if n and i == 0:
                    o_half(n - 1)
                if n < len(LATER) and i == THIRDS:
                    split_proj(LATER[n])
            o_half(HH - 1)

        def none(*_):
            pass

        with nc.Block() as block:

            @block.sync
            def _(sp):
                def load_ctx(g, b):
                    sp.wait_ge(t_mm, done(T * HH * g - T))
                    sp.dma_start(prob[:, 0, :, :], ctxT[b].rearrange("(k p) n -> p k n", p=P)).then_inc(ctx_loaded, 16)

                def load_x(g, b):
                    sp.wait_ge(t_mm, done(T * HH * g))
                    sp.dma_start(prob[:, 1, :, :], x1T[b].rearrange("p (k n) -> p k n", k=K)).then_inc(x_loaded, 16)

                def load_wk(h, j, pair):
                    sp.wait_ge(proj_mm, done(pair))
                    sp.dma_start(as_f32(wk[:, :, :, :]), wkparts[h * PAIRS + j]).then_inc(wk_loaded, 16)

                def load_wq(h, j, pair):
                    sp.wait_ge(proj_mm, done(pair))
                    sp.dma_start(as_f32(wq[:, :, :, :]), wqparts[h * PAIRS + j]).then_inc(wq_loaded, 16)

                def double_k(g, j):
                    for e, (own, other) in enumerate(((slice(0, DK), slice(DK, P)), (slice(DK, P), slice(0, DK)))):
                        sp.wait_ge(proj_lo, done(NSTEP * g + step(f"K{j}", e)))
                        sp.dma_start(as_f32(ks[other, j % 2, e, :, :]),
                                     as_f32(ks[own, j % 2, e, :, :])).then_inc(k_doubled[e], 16)

                load_ctx(0, 0)
                load_wk(0, 0, 0)
                for h in range(HALVES):
                    for k in range(K):
                        sp.dma_start(as_f32(WV[:, :, k, h * CH:(h + 1) * CH]),
                                     wvparts[h * K + k].rearrange("p (a n) -> p a n", a=2)).then_inc(wv_loaded[h], 16)
                    if h == 0:
                        load_x(0, 0)
                        load_wq(0, 0, 0)
                        for dst, src in ((bq_raw, bq), (bks, bk), (bvs, bv)):
                            sp.dma_start(dst[:, :], src).then_inc(consts, 16)
                for j in range(H // 2):
                    sp.dma_start(as_f32(WO[:, :, j, :]),
                                 woparts[j].rearrange("p (a n) -> p a n", a=2)).then_inc(wo_loaded, 16)
                sp.dma_start(y[:, :, :], y_steps[0].rearrange("(t p) d -> p t d", p=P)).then_inc(y_loaded, 16)

                def body(g, h, b, nb, nh):
                    n = NPROJ * g
                    double_k(g, 0)
                    load_wk(h, 1, n + use("K0") + 1)
                    double_k(g, 1)
                    load_wq(h, 1, n + use("Q0") + 1)
                    load_wk(h, 2, n + use("K1") + 1)
                    load_wq(h, 2, n + use("Q1") + 1)
                    double_k(g, 2)
                    load_wk(h, 3, n + use("K2") + 1)
                    load_wq(h, 3, n + use("Q2") + 1)
                    double_k(g, 3)
                    load_wk(nh, 0, n + use("K3") + 1)
                    load_wq(nh, 0, n + use("Q3") + 1)
                    load_ctx(g + 1, nb)
                    load_x(g + 1, nb)
                    sp.wait_ge(wo_out, done(T * g + T))
                    sp.dma_start(y_steps[g + NB].rearrange("(t p) d -> p t d", p=P), y[:, :, :]).then_inc(y_stored, 16)
                    sp.wait_ge(y_stored, 16 * g + 16)
                    sp.dma_start(y[:, :, :], y_steps[g + 1].rearrange("(t p) d -> p t d", p=P)).then_inc(y_loaded, 16)

                groups(sp, body)
                sp.wait_ge(y_loaded, 16 * (HALVES * NB + 1))

            @block.gpsimd
            def _(pool):
                for s in credited["pool"]:
                    pool.sem_inc(s, CREDIT)

                def body(g, h, b, nb, nh):
                    def norm_tile(t):
                        n, i = divmod(t, T)
                        pool.wait_ge(have_rden, TILES * g + t + 1)
                        pool.sem_inc(passed, 1)
                        nc.gpsimd.tensor_scalar(prob[:, n % 2, i, :], prob[:, n % 2, i, :], rden[:, n % 2, i:i + 1], 1.0,
                                                ALU.mult, ALU.mult).then_inc(p_ready, 1)

                    def split_hi(j):
                        pool.wait_ge(o_sum, done(HH * g + 2 * j + 2))
                        if j == 0:
                            pool.wait_ge(wo_mm, done(T * g))
                        pool.sem_inc(passed, 1)
                        nc.gpsimd.tensor_scalar(op[:, HI, j, :], osum[:, :], 1.0, 1.0, ALU.mult,
                                                ALU.mult).then_inc(op_hi, 1)

                    def split_lo(j):
                        pool.wait_ge(op_hi, PAIRS * g + j + 1)
                        nc.gpsimd.tensor_tensor(op[:, LO, j, :], osum[:, :], as_f32(op[:, HI, j, :]),
                                                ALU.subtract).then_inc(op_lo, 1)

                    for t in range(LEAD - 1):
                        norm_tile(t)
                    for t in range(TILES):
                        n, i = divmod(t, T)
                        if t + LEAD <= TILES:
                            norm_tile(t + LEAD - 1)
                        if n and n % 2 == 0 and i == 2:
                            split_hi(n // 2 - 1)
                        if n and n % 2 == 0 and i == 3:
                            split_lo(n // 2 - 1)
                    split_hi(PAIRS - 1)
                    split_lo(PAIRS - 1)

                groups(pool, body)

            @block.scalar
            def _(act):
                for s in credited["act"]:
                    act.sem_inc(s, CREDIT)

                def split_piece(g, k):
                    if k == 0:
                        act.wait_ge(ctx_loaded, 16 * g + 16)
                        act.wait_ge(proj_mm, done(NPROJ * g))
                    if k == K:
                        act.wait_ge(x_loaded, 16 * g + 16)
                    dst = cp if k < K else xp
                    nc.scalar.copy(dst[:, HI, k % K, :], prob[:, k // K, k % K, :]).then_inc(raw_hi, 1)

                for k in range(2 * K):
                    split_piece(0, k)
                act.wait_ge(bias_ready, 1)

                def body(g, h, b, nb, nh):
                    def exp_tile(t):
                        n, i = divmod(t, T)
                        head = HH * g + n
                        act.wait_ge(smax, T * head + i + 1)
                        if i == 0:
                            act.wait_ge(t_mm, done(T * head - T))
                            if n < 2:
                                act.wait_ge(raw_lo, 2 * K * g + 2 * K)
                        nc.scalar.activation(prob[:, n % 2, i, :], spsum[:, i % 2, :], ACT.Exp,
                                             bias=negmax[:, n % 2, i:i + 1], scale=1.0,
                                             accum_out=den[:, n % 2, i:i + 1]).then_inc(p_exp, 1)

                    def split_proj(name):
                        u, j = use(name), int(name[1])
                        bank = projp[:, u % 2, :]
                        act.wait_ge(proj_mm, done(NPROJ * g + u + 1))
                        if name[0] == "V":
                            if j == 0:
                                act.wait_ge(av_mm, done(T * HH * g))
                            nc.scalar.copy(vs[:, j, :, 0:DK], bank.rearrange("p (h d) -> p h d", d=DK)).then_inc(proj_hi, 1)
                            return
                        bias = bks if name[0] == "K" else bqs
                        act.wait_ge(s_mm, done(T * (HH * g + 2 * j - 2)))
                        for e, rows in enumerate((slice(0, DK), slice(DK, P))):
                            dst = ks[rows, j % 2, e, HI, :] if name[0] == "K" else qs[rows, j % 2, e, :]
                            nc.scalar.activation(dst, bank[rows, :], ACT.Identity,
                                                 bias=bias[rows, ds(h * PAIRS + j)], scale=1.0).then_inc(proj_hi, 1)

                    def ds(i):
                        return bass.ds(i, 1)

                    def pt_tile(t):
                        act.wait_ge(t_mm, done(TILES * g + t + 1))
                        act.wait_ge(av_mm, done(TILES * g + t - 1))
                        nc.scalar.copy(pt[:, t % 2, HI, :], tpsum[:, t % 2, :]).then_inc(pt_hi, 1)

                    def o_first(n):
                        head = HH * g + n
                        act.wait_ge(av_mm, done(T * head + T))
                        act.wait_ge(o_sum, done(head - 1))
                        rows = slice(0, DK) if n % 2 == 0 else slice(DK, P)
                        nc.scalar.activation(opart[rows, :], opsum[0:DK, n % 2, :], ACT.Identity,
                                             bias=bvs[:, ds(h * HH + n)], scale=1.0).then_inc(o_part, 1)

                    schedule(split_proj, none, none, exp_tile, pt_tile, o_first)
                    for k in range(2 * K):
                        split_piece(g + 1, k)

                groups(act, body)

            @block.vector
            def _(dve):
                for s in credited["dve"]:
                    dve.sem_inc(s, CREDIT)

                def split_piece(g, k):
                    dst = cp if k < K else xp
                    dve.wait_ge(raw_hi, 2 * K * g + k + 1)
                    nc.vector.tensor_tensor(dst[:, LO, k % K, :], prob[:, k // K, k % K, :],
                                            as_f32(dst[:, HI, k % K, :]), ALU.subtract).then_inc(raw_lo, 1)

                for k in range(2 * K):
                    split_piece(0, k)
                dve.wait_ge(consts, 48)
                nc.vector.tensor_scalar(bqs[:, :], bq_raw[:, :], float(NB) ** -0.5, None, ALU.mult).then_inc(bias_ready, 1)
                dve.wait_ge(bias_ready, 1)

                def body(g, h, b, nb, nh):
                    def ds(i):
                        return bass.ds(i, 1)

                    def max_tile(t):
                        n, i = divmod(t, T)
                        dve.wait_ge(s_mm, done(TILES * g + t + 1))
                        nc.vector.tensor_reduce(negmax[:, n % 2, i:i + 1], spsum[:, i % 2, :], AX.X, ALU.max,
                                                negate=True).then_inc(smax, 1)

                    def recip(t):
                        n, i = divmod(t, T)
                        dve.wait_ge(p_exp, done(TILES * g + t + 1))
                        nc.vector.reciprocal(rden[:, n % 2, i:i + 1], den[:, n % 2, i:i + 1]).then_inc(have_rden, 1)

                    def split_proj(name):
                        u, j = use(name), int(name[1])
                        bank = projp[:, u % 2, :]
                        if name[0] == "V":
                            dve.wait_ge(proj_hi, NSTEP * g + step(name))
                            nc.vector.tensor_tensor(vs[:, j, :, DK:], bank.rearrange("p (h d) -> p h d", d=DK),
                                                    as_f32(vs[:, j, :, 0:DK]), ALU.subtract).then_inc(proj_lo, 1)
                            return
                        bias = bks if name[0] == "K" else bqs
                        for e, rows in enumerate((slice(0, DK), slice(DK, P))):
                            dve.wait_ge(proj_hi, NSTEP * g + step(name, e))
                            if name[0] == "K":
                                hi, lo = ks[rows, j % 2, e, HI, :], ks[rows, j % 2, e, LO, :]
                            else:
                                hi, lo = qs[rows, j % 2, e, :], qs[slice(DK, P) if e == 0 else slice(0, DK), j % 2, e, :]
                            nc.vector.scalar_tensor_tensor(out=lo, in0=bank[rows, :], scalar=bias[rows, ds(h * PAIRS + j)],
                                                           in1=as_f32(hi), op0=ALU.add,
                                                           op1=ALU.subtract).then_inc(proj_lo, 1)

                    def pt_tile(t):
                        dve.wait_ge(pt_hi, TILES * g + t + 1)
                        nc.vector.tensor_tensor(pt[:, t % 2, LO, :], tpsum[:, t % 2, :], as_f32(pt[:, t % 2, HI, :]),
                                                ALU.subtract).then_inc(pt_lo, 1)

                    def o_second(n):
                        head = HH * g + n
                        dve.wait_ge(o_part, head + 1)
                        if n % 2 == 0:
                            dve.wait_ge(op_lo, done(PAIRS * g + n // 2))
                        rows = slice(0, DK) if n % 2 == 0 else slice(DK, P)
                        nc.vector.tensor_tensor(osum[rows, :], opsum[DK:P, n % 2, :], opart[rows, :],
                                                ALU.add).then_inc(o_sum, 1)

                    schedule(split_proj, max_tile, recip, none, pt_tile, o_second)
                    for k in range(2 * K):
                        split_piece(g + 1, k)
                    dve.wait_ge(y_loaded, 16 * g + 16)
                    for i in range(T):
                        dve.wait_ge(wo_mm, done(T * g + i + 1))
                        nc.vector.tensor_tensor(y[:, i, :], wo_bank[i], y[:, i, :], ALU.add).then_inc(wo_out, 1)

                groups(dve, body)

            @block.tensor
            def _(pe):
                for s in credited["pe"]:
                    pe.sem_inc(s, CREDIT)

                def body(g, h, b, nb, nh):
                    def proj_tile(name, part=0, parts=1):
                        u, j = use(name), int(name[1])
                        out = projp[:, u % 2, :]
                        mms = [(k, s, m) for k in range(K) for s, m in TERMS]
                        if part == 0:
                            before = NSTEP * g + (sum(STEPS[:u - 1]) if u else -STEPS[-1])
                            pe.wait_ge(proj_lo, done(before))
                            if name[0] == "K":
                                pe.wait_ge(wk_loaded, 16 * (PAIRS * g + j + 1))
                            if name[0] == "Q":
                                pe.wait_ge(wq_loaded, 16 * (PAIRS * g + j + 1))
                        lo, hi = part * len(mms) // parts, (part + 1) * len(mms) // parts
                        for n, (k, s, m) in enumerate(mms[lo:hi], lo):
                            if name[0] == "K":
                                l, r = wk[:, s, k, :], cp[:, m, k, :]
                            elif name[0] == "Q":
                                l, r = wq[:, s, k, :], xp[:, m, k, :]
                            else:
                                l, r = cp[:, s, k, j * P:(j + 1) * P], WV[:, m, k, bass.ds(h * CH, CH)]
                            ins = nc.tensor.matmul(out, l, r, start=(n == 0), stop=(n == len(mms) - 1))
                        if part == parts - 1:
                            ins.then_inc(proj_mm, 1)

                    def scores(t):
                        n, i = divmod(t, T)
                        head, j, e = HH * g + n, n // 2, n % 2
                        if i == 0:
                            if e == 0:
                                pe.wait_ge(proj_lo, done(NSTEP * g + step(f"Q{j}")))
                                pe.wait_ge(proj_lo, done(NSTEP * g + step(f"K{j}")))
                            pe.wait_ge(k_doubled[e], 16 * (PAIRS * g + j + 1))
                        pe.wait_ge(p_exp, done(T * head + i - 1))
                        if n == 0 and i == 0:
                            pe.wait_ge(wo_out, done(T * g))
                        for m in (HI, LO):
                            ins = nc.tensor.matmul(spsum[:, i % 2, :], qs[:, j % 2, e, i * P:(i + 1) * P],
                                                   ks[:, j % 2, e, m, :], start=(m == HI), stop=(m == LO))
                        ins.then_inc(s_mm, 1)

                    def turn(n, k):
                        head = HH * g + n
                        pe.wait_ge(pt_lo, done(T * head + k - 1))
                        for i in range(T):
                            if k == 0:
                                pe.wait_ge(p_ready, T * head + i + 1)
                            ins = nc.tensor.transpose(tpsum[:, k % 2, i * P:(i + 1) * P],
                                                      prob[:, n % 2, i, k * P:(k + 1) * P], ident[:, :])
                        ins.then_inc(t_mm, 1)

                    def values(n, k):
                        head = HH * g + n
                        if k == 0:
                            pe.wait_ge(o_sum, done(head - 1))
                            if n == 0:
                                pe.wait_ge(proj_lo, done(NSTEP * g + step("V3")))
                        pe.wait_ge(pt_lo, done(T * head + k + 1))
                        for m in (HI, LO):
                            ins = nc.tensor.matmul(opsum[:, n % 2, :], vs[:, k, n, :], pt[:, k % 2, m, :],
                                                   start=(k == 0 and m == HI), stop=(k == T - 1 and m == LO))
                        ins.then_inc(av_mm, 1)

                    def out_tile(i, pairs):
                        for j in pairs:
                            pe.wait_ge(op_lo, done(PAIRS * g + j + 1))
                            for s, m in TERMS:
                                ins = nc.tensor.matmul(wo_bank[i], op[:, s, j, i * P:(i + 1) * P],
                                                       WO[:, m, bass.ds(h * PAIRS + j, 1), :].rearrange("p a n -> p (a n)"),
                                                       start=(j == 0 and s == m == HI),
                                                       stop=(j == PAIRS - 1 and (s, m) == TERMS[-1]))
                        return ins

                    pe.wait_ge(raw_lo, 2 * K * g + K)
                    for o in OPENING:
                        if o == "Q0":
                            pe.wait_ge(raw_lo, 2 * K * g + 2 * K)
                        if o == "V0":
                            for loaded in wv_loaded:
                                pe.wait_ge(loaded, 16 * K)
                        if isinstance(o, str):
                            proj_tile(o)
                        else:
                            scores(o)
                    for t in range(TILES):
                        n, i = divmod(t, T)
                        if t + LEAD < TILES:
                            scores(t + LEAD)
                        if n < len(LATER) and i < THIRDS:
                            proj_tile(LATER[n], i, THIRDS)
                        turn(n, i)
                        if i:
                            values(n, i - 1)
                        elif n:
                            values(n - 1, T - 1)
                    values(HH - 1, T - 1)
                    pe.wait_ge(wo_loaded, 16 * (H // 2))
                    pe.wait_ge(p_exp, done(T * HH * g + T * HH))
                    for i in range(T):
                        if i == 2:
                            pe.wait_ge(pt_lo, done(T * HH * g + T * HH))
                        out_tile(i, range(PAIRS - 1))
                    for i in range(T):
                        out_tile(i, [PAIRS - 1]).then_inc(wo_mm, 1)

                groups(pe, body)


def feed_forward(nc, y_in, WsT, WeT, Wg, bo, bias, ident, out, NB, S, D, NG):
    T, K, RING = S // P, D // P, 2
    SHARED, EXPERT = 0, 1
    PAD = 8
    assert NB % RING == 0 and T == 4 and K == 4 and NG < PAD
    with ExitStack() as ctx:
        sc = Scope(nc, ctx, "f")
        raw = sc.sb("raw", [P, 2, K, D])
        W = sc.sb("W", [P, 2, 2, K, D], F32R)
        graw, G = sc.sb("graw", [P, K, P]), sc.sb("G", [P, 2, K, P], F32R)
        bo_all, bias_all = sc.sb("bo", [P, D]), sc.sb("bias", [P, D])
        x2 = sc.sb("x2", [P, RING, T, D])
        x2T = sc.sb("x2T", [P, RING, 2, K, S], F32R)
        z = sc.sb("z", [P, RING, T, D])
        logitT = sc.sb("logitT", [P, S])
        e = sc.sb("e", [P, T, PAD])
        gneg, den = sc.sb("gneg", [P, T]), sc.sb("den", [P, T])
        best = sc.sb("best", [P, T, PAD])
        total, route, weight = sc.sb("total", [P, T]), sc.sb("route", [P, 2, T]), sc.sb("weight", [P, T])
        prod = sc.ps("prod", [P, RING, 2, D])
        turned = sc.ps("turned", [P, 2, S])
        gateT, logit = sc.ps("gateT", [P, S]), sc.ps("logit", [P, T, P])

        (g_zero, g_loaded, w_hi, w_lo, b_loaded, xb_made, t_mm, x2_hi, x2_lo, gate_mm, gate_out, lt_mm,
         g_max, e_done, e_pad, w_step, w_done, prod_mm, z_mid) = (sc.sem(n) for n in (
             "g_zero", "g_loaded", "w_hi", "w_lo", "b_loaded", "xb_made", "t_mm", "x2_hi", "x2_lo", "gate_mm",
             "gate_out", "lt_mm", "g_max", "e_done", "e_pad", "w_step", "w_done", "prod_mm", "z_mid"))
        ranked, passed = sc.sem("ranked"), sc.sem("passed")
        w_loaded = [sc.sem(f"w_loaded{n}") for n in range(2)]
        y_loaded, z_stored = ([sc.sem(f"{n}{u}") for u in range(RING)] for n in ("y_loaded", "z_stored"))
        WEIGHT_STEPS = 1 + T + 4
        CREDIT = 16
        norm2, norm3 = Norm(sc, T, D, "norm2"), Norm(sc, T, D, "norm3", credit=CREDIT)

        def done(n):
            return n + CREDIT

        def batches(eng, step):
            if NB > RING:
                with eng.Fori(0, NB // RING - 1) as c:
                    for u in range(RING):
                        step(c * RING + u, u, c, RING)
            for u in range(RING):
                step(NB - RING + u, u, NB // RING - 1, RING - 1 - u)

        with nc.Block() as block:

            @block.sync
            def _(sp):
                def load(u, b):
                    sp.dma_start(x2[:, u, :, :], y_in[b].rearrange("(t p) d -> p t d", p=P)).then_inc(y_loaded[u], 16)

                load(0, 0)
                sp.dma_start(bo_all[:, :], bo.partition_broadcast(P)).then_inc(b_loaded, 16)
                sp.wait_ge(g_zero, 1)
                sp.dma_start(graw[:, :, :NG], Wg.rearrange("(k p) n -> p k n", p=P)).then_inc(g_loaded, 16)
                sp.dma_start(bias_all[:, :], bias.partition_broadcast(P)).then_inc(b_loaded, 16)
                for w, src in enumerate((WsT, WeT)):
                    sp.dma_start(raw[:, w, :, :], src.rearrange("(k p) n -> p k n", p=P)).then_inc(w_loaded[w], 16)
                load(1, 1)

                def step(b, u, c, more):
                    if more == RING:
                        sp.wait_ge(t_mm, K * b + K)
                        sp.wait_ge(xb_made, T * b + T)
                        load(u, b + RING)
                    sp.wait_ge(norm3.normed, T * b + T)
                    sp.dma_start(out[b].rearrange("(t p) d -> p t d", p=P), z[:, u, :, :]).then_inc(z_stored[u], 16)

                batches(sp, step)
                for u in range(RING):
                    sp.wait_ge(z_stored[u], done(16 * NB // RING))

            @block.gpsimd
            def _(pool):
                nc.gpsimd.memset(graw[:, :, :], 0.0).then_inc(g_zero, 1)
                for u in range(RING):
                    pool.sem_inc(z_stored[u], CREDIT)

                def add_bo(u, c):
                    pool.wait_ge(y_loaded[u], 16 * c + 16)
                    for i in range(T):
                        nc.gpsimd.tensor_tensor(x2[:, u, i, :], x2[:, u, i, :], bo_all[:, :],
                                                ALU.add).then_inc(norm2.summed, 1)

                def add_bias(b, u, c):
                    pool.wait_ge(norm2.normed, T * b + T)
                    pool.wait_ge(z_stored[u], 16 * c + CREDIT)
                    for i in range(T):
                        nc.gpsimd.tensor_tensor(z[:, u, i, :], x2[:, u, i, :], bias_all[:, :],
                                                ALU.add).then_inc(xb_made, 1)

                pool.wait_ge(b_loaded, 32)
                add_bo(0, 0)
                add_bias(0, 0, 0)
                add_bo(1, 0)

                def step(b, u, c, more):
                    if more:
                        add_bias(b + 1, (u + 1) % RING, c + (u + 1) // RING)
                    if more == RING:
                        add_bo(u, c + 1)

                batches(pool, step)

            @block.scalar
            def _(act):
                act.sem_inc(e_done, CREDIT)
                act.sem_inc(gate_out, CREDIT)

                def turn_hi(b, u):
                    for k in range(K):
                        act.wait_ge(t_mm, K * b + k + 1)
                        act.wait_ge(prod_mm, done(T * b - T))
                        nc.scalar.copy(x2T[:, u, HI, k, :], turned[:, k % 2, :]).then_inc(x2_hi, 1)

                def gate_copy(b):
                    act.wait_ge(gate_mm, b + 1)
                    act.wait_ge(lt_mm, done(b))
                    nc.scalar.copy(logitT[:, :], gateT[:, :]).then_inc(gate_out, 1)

                for w in range(2):
                    act.wait_ge(w_loaded[w], 16)
                    for k in range(K):
                        nc.scalar.copy(W[:, w, HI, k, :], raw[:, w, k, :]).then_inc(w_hi, 1)
                    if w == 0:
                        act.wait_ge(g_loaded, 16)
                        nc.scalar.copy(G[:, HI, :, :], graw[:, :, :]).then_inc(w_hi, 1)
                norm2.root(nc, 0)
                turn_hi(0, 0)
                gate_copy(0)

                def step(b, u, c, more):
                    act.wait_ge(g_max, b + 1)
                    act.wait_ge(w_done, done(b))
                    for i in range(T):
                        nc.scalar.activation(e[:, i, :NG], logit[:, i, :NG], ACT.Exp, bias=gneg[:, i:i + 1], scale=1.0,
                                             accum_out=den[:, i:i + 1]).then_inc(e_done, 1)
                    if more:
                        norm2.root(nc, b + 1)
                        turn_hi(b + 1, (u + 1) % RING)
                        gate_copy(b + 1)
                    norm3.root(nc, b)

                batches(act, step)

            @block.vector
            def _(dve):
                for s in (x2_lo, w_done, norm3.summed):
                    dve.sem_inc(s, CREDIT)
                nc.vector.memset(e[:, :, :], 0.0).then_inc(e_pad, 1)
                dve.wait_ge(e_pad, 1)
                v = nc.vector

                def turn_lo(b, u):
                    for k in range(K):
                        dve.wait_ge(x2_hi, K * b + k + 1)
                        v.tensor_tensor(x2T[:, u, LO, k, :], turned[:, k % 2, :], as_f32(x2T[:, u, HI, k, :]),
                                        ALU.subtract).then_inc(x2_lo, 1)

                def gate_max(b):
                    dve.wait_ge(lt_mm, done(b + 1))
                    v.tensor_reduce(gneg[:, :], logit[:, :, :NG], AX.X, ALU.max, negate=True).then_inc(g_max, 1)

                def route_weights(b):
                    count = [WEIGHT_STEPS * b]

                    def link(ins):
                        count[0] = count[0] + 1
                        ins.then_inc(w_step, 1)
                        dve.wait_ge(w_step, count[0])

                    dve.wait_ge(e_done, done(T * b + T))
                    link(v.reciprocal(den[:, :], den[:, :]))
                    for i in range(T):
                        link(v.tensor_scalar(e[:, i, :NG], e[:, i, :NG], den[:, i:i + 1], None, ALU.mult))
                    dve.sem_inc(passed, 1)
                    for i in range(T):
                        v.max(best[:, i, :], e[:, i, :]).then_inc(ranked, 1)
                    dve.wait_ge(ranked, T * b + T)
                    link(v.tensor_tensor(total[:, :], best[:, :, 0], best[:, :, 1], ALU.add))
                    link(v.reciprocal(total[:, :], total[:, :]))
                    for r in range(2):
                        link(v.tensor_tensor(route[:, r, :], best[:, :, r], total[:, :], ALU.mult))
                    v.tensor_tensor(weight[:, :], route[:, 0, :], route[:, 1, :], ALU.add).then_inc(w_done, 1)

                def finish_tile(b, u, i):
                    dve.wait_ge(prod_mm, done(T * b + i + 1))
                    dve.wait_ge(xb_made, T * b + i + 1)
                    if i == 0:
                        dve.wait_ge(w_done, done(b + 1))
                    v.scalar_tensor_tensor(out=z[:, u, i, :], in0=prod[:, i % RING, EXPERT, :], scalar=weight[:, i:i + 1],
                                           in1=z[:, u, i, :], op0=ALU.mult, op1=ALU.add).then_inc(z_mid, 1)
                    dve.wait_ge(z_mid, T * b + i + 1)
                    v.tensor_tensor(z[:, u, i, :], prod[:, i % RING, SHARED, :], z[:, u, i, :],
                                    ALU.add).then_inc(norm3.summed, 1)
                    norm3.stats(nc, b, i, z[:, u])

                for i in range(T):
                    norm2.stats(nc, 0, i, x2[:, 0])
                norm2.variance(nc, 0)
                for n in range(2):
                    for k in range(K):
                        dve.wait_ge(w_hi, (K + 1) * n + k + 1)
                        v.tensor_tensor(W[:, n, LO, k, :], raw[:, n, k, :], as_f32(W[:, n, HI, k, :]),
                                        ALU.subtract).then_inc(w_lo, 1)
                    if n == 0:
                        dve.wait_ge(w_hi, K + 1)
                        v.tensor_tensor(G[:, LO, :, :], graw[:, :, :], as_f32(G[:, HI, :, :]),
                                        ALU.subtract).then_inc(w_lo, 1)
                norm2.scale(nc, 0, x2[:, 0], x2[:, 0])
                turn_lo(0, 0)

                def step(b, u, c, more):
                    nu = (u + 1) % RING
                    if more:
                        for i in range(T):
                            norm2.stats(nc, b + 1, i, x2[:, nu])
                    gate_max(b)
                    if more:
                        norm2.variance(nc, b + 1)
                    route_weights(b)
                    finish_tile(b, u, 0)
                    if more:
                        norm2.scale(nc, b + 1, x2[:, nu], x2[:, nu])
                    finish_tile(b, u, 1)
                    finish_tile(b, u, 2)
                    if more:
                        turn_lo(b + 1, nu)
                    finish_tile(b, u, 3)
                    norm3.variance(nc, b)
                    norm3.scale(nc, b, z[:, u], z[:, u])

                batches(dve, step)

            @block.tensor
            def _(pe):
                pe.sem_inc(lt_mm, CREDIT)
                pe.sem_inc(prod_mm, CREDIT)

                def turn(b, u, ks):
                    pe.wait_ge(norm2.normed, T * b + T)
                    for k in ks:
                        pe.wait_ge(x2_lo, done(K * b + k - 1))
                        for i in range(T):
                            t = nc.tensor.transpose(turned[:, k % 2, i * P:(i + 1) * P], x2[:, u, i, k * P:(k + 1) * P],
                                                    ident[:, :])
                        t.then_inc(t_mm, 1)

                def gate(b, u):
                    pe.wait_ge(x2_lo, done(K * b + K))
                    pe.wait_ge(gate_out, done(b))
                    three_pass(nc, gateT[:, :], lambda s, k: G[:, s, k, :], lambda m, k: x2T[:, u, m, k, :],
                               K).then_inc(gate_mm, 1)

                def turn_logits(b):
                    pe.wait_ge(gate_out, done(b + 1))
                    pe.wait_ge(e_done, done(T * b))
                    for i in range(T):
                        t = nc.tensor.transpose(logit[:, i, :], logitT[:, i * P:(i + 1) * P], ident[:, :])
                    t.then_inc(lt_mm, 1)

                def product(b, u, i, which):
                    if which == SHARED:
                        pe.wait_ge(norm3.summed, done(T * b + i - 1))
                    return three_pass(nc, prod[:, i % RING, which, :], lambda s, k: x2T[:, u, s, k, i * P:(i + 1) * P],
                                      lambda m, k: W[:, which, m, k, :], K)

                turn(0, 0, range(K))
                pe.wait_ge(w_lo, 2 * K + 1)
                gate(0, 0)

                def step(b, u, c, more):
                    nu = (u + 1) % RING
                    product(b, u, 0, SHARED)
                    turn_logits(b)
                    product(b, u, 0, EXPERT).then_inc(prod_mm, 1)
                    for i in (1, 2):
                        product(b, u, i, SHARED)
                        product(b, u, i, EXPERT).then_inc(prod_mm, 1)
                    if more:
                        turn(b + 1, nu, range(0, 2))
                    product(b, u, 3, SHARED)
                    if more:
                        turn(b + 1, nu, range(2, K))
                    product(b, u, 3, EXPERT).then_inc(prod_mm, 1)
                    if more:
                        gate(b + 1, nu)

                batches(pe, step)


def decoder_layer(nc, x, xT, ctxT, wqT, wkT, wv, wpair, bq, bk, bv, bo, WsT, WeT, Wg, bias, out):
    NB, S, D = x.shape
    NPAIR, (DK, H) = wpair.shape[0], bv.shape
    y_steps = nc.dram_tensor("y_steps_scratch", [3 * NB, S, D], F32).ap()
    x1T = nc.dram_tensor("x1T_scratch", [NB, P, (D // P) * S], F32).ap()
    wparts = [nc.dram_tensor(f"{n}_scratch", [NPAIR, P, 2 * D], F32).ap() for n in ("wq", "wk", "wv", "wo")]
    with ExitStack() as ctx:
        sc = Scope(nc, ctx, "all")
        ident = sc.sb("ident", [P, P])
        made = sc.sem("ident_made")
        with nc.Block() as block:
            @block.gpsimd
            def _(pool):
                nc.gpsimd.memset(ident[:, :], 0.0).then_inc(made, 1)
                pool.wait_ge(made, 1)
                nc.gpsimd.affine_select(out=ident[:, :], in_=ident[:, :], compare_op=ALU.not_equal, fill=1.0, base=0,
                                        pattern=[[-1, P]], channel_multiplier=1).then_inc(made, 1)
        with ExitStack() as first_half:
            sa = Scope(nc, first_half, "sw")
            A, WV = sa.sb("A", [P, 2, D // P, D], F32R), sa.sb("WV", [P, 2, D // P, D], F32R)
            load_weights(nc, wqT, wkT, wv, A, WV, D)
            self_attention(nc, x, xT, wpair, A, WV, ident, y_steps, x1T, wparts, NB, S, D, float(NB) ** -0.5)
        cross_attention(nc, y_steps, x1T, ctxT, *wparts, bq, bk, bv, ident, NB, S, D, H, DK)
        feed_forward(nc, y_steps[2 * NB:3 * NB], WsT, WeT, Wg, bo, bias, ident, out, NB, S, D, Wg.shape[1])


def kernel(x, ctx_1024, L0_attn_W, L0_xattn_Wq, L0_xattn_bq, L0_xattn_Wk, L0_xattn_bk, L0_xattn_Wv, L0_xattn_bv,
           L0_xattn_Wo, L0_xattn_bo, L0_ffn_cond, L0_ffn_mask, L0_ffn_W_shared, L0_ffn_W_expert, L0_ffn_W_gate,
           L0_ffn_bias):
    import numpy as np
    import concourse.bacc as bacc
    from concourse.bass_utils import run_bass_kernel_spmd

    D, H, DK = x.shape[2], 16, 64
    K, PAIRS = D // P, H * DK // P

    def pair_columns(w):
        return w.reshape(K, P, PAIRS, P).transpose(2, 1, 0, 3).reshape(PAIRS, P, K * P)

    W, Wq, Wk, Wv, Wo = (np.asarray(a) for a in (L0_attn_W, L0_xattn_Wq, L0_xattn_Wk, L0_xattn_Wv, L0_xattn_Wo))
    halves = Wv.reshape(K, P, 2, Wv.shape[1] // 2).transpose(2, 0, 1, 3).reshape(PAIRS, P, Wv.shape[1] // 2)
    arrays = {
        "x": np.asarray(x), "xT": np.asarray(x).transpose(0, 2, 1), "ctxT": np.asarray(ctx_1024).transpose(0, 2, 1),
        "wqT": W[:, :D].T, "wkT": W[:, D:2 * D].T, "wv": W[:, 2 * D:],
        "wpair": np.stack([pair_columns(Wq), pair_columns(Wk), halves, Wo.reshape(PAIRS, P, D)], axis=1),
        "bq": np.asarray(L0_xattn_bq).reshape(PAIRS, P).T, "bk": np.asarray(L0_xattn_bk).reshape(PAIRS, P).T,
        "bv": np.asarray(L0_xattn_bv).reshape(H, DK).T, "bo": np.asarray(L0_xattn_bo).reshape(1, D),
        "WsT": np.asarray(L0_ffn_W_shared).T, "WeT": np.asarray(L0_ffn_W_expert).T,
        "Wg": np.asarray(L0_ffn_W_gate), "bias": np.asarray(L0_ffn_bias).reshape(1, D)}
    arrays = {f"in_{name}": np.ascontiguousarray(a) for name, a in arrays.items()}
    nc = bacc.Bacc("TRN2", target_bir_lowering=False, num_devices=1)
    args = [nc.dram_tensor(name, a.shape, mybir.dt.from_np(a.dtype), kind="ExternalInput").ap()
            for name, a in arrays.items()]
    args.append(nc.dram_tensor("out", x.shape, F32, kind="ExternalOutput").ap())
    decoder_layer(nc, *args)
    return run_bass_kernel_spmd(nc, [arrays], core_ids=[0]).results[0]["out"]
```

```python
from contextlib import ExitStack

import concourse.bass as bass
from concourse import mybir

F32 = mybir.dt.float32
F32R = mybir.dt.float32r
ALU = mybir.AluOpType
ACT = mybir.ActivationFunctionType
AX = mybir.AxisListType

P = 128
HI, LO = 0, 1
EPS = 1e-5
NEG = 9000000000000000.0
TERMS = ((HI, HI), (HI, LO), (LO, HI))


class Scope:

    def __init__(self, nc, ctx, stage):
        self.nc, self.ctx, self.stage = nc, ctx, stage

    def sb(self, name, shape, dt=F32):
        return self.ctx.enter_context(self.nc.sbuf_tensor(f"{self.stage}_{name}", shape, dt))

    def ps(self, name, shape):
        return self.ctx.enter_context(self.nc.psum_tensor(f"{self.stage}_{name}", shape, F32))

    def sem(self, name):
        return self.ctx.enter_context(self.nc.semaphore(f"{self.stage}_{name}"))


def as_f32(ap):
    return ap.bitcast(F32)


def three_pass(nc, out, stationary, moving, depth):
    last = (depth - 1, TERMS[-1])
    for k in range(depth):
        for s, m in TERMS:
            ins = nc.tensor.matmul(out, stationary(s, k), moving(m, k), start=(k == 0 and s == m == HI),
                                   stop=((k, (s, m)) == last))
    return ins


class Norm:

    def __init__(self, sc, T, D, name="norm", credit=0):
        self.T, self.D, self.credit = T, D, credit
        self.stat = sc.sb(f"{name}_stat", [P, T, 6])
        self.mean, self.var, self.std = (sc.sb(f"{name}_{n}", [P, T]) for n in ("mean", "variance", "std"))
        self.r, self.t, self.u = (sc.sb(f"{name}_{n}", [P, T]) for n in ("r", "t", "u"))
        self.summed, self.have_stat, self.step, self.have_var, self.have_std, self.normed = (
            sc.sem(f"{name}_{n}") for n in ("summed", "have_stat", "step", "have_var", "have_std", "normed"))

    def link(self, nc, count, ins):
        count[0] = count[0] + 1
        ins.then_inc(self.step, 1)
        nc.vector.wait_ge(self.step, count[0])

    VARIANCE_STEPS, STEPS = 6, 11

    def stats(self, nc, b, i, y):
        nc.vector.wait_ge(self.summed, self.T * b + i + 1 + self.credit)
        nc.vector.bn_stats(self.stat[:, i, :], y[:, i, :]).then_inc(self.have_stat, 1)

    def variance(self, nc, b):
        v, st, n = nc.vector, self.stat, [self.STEPS * b]
        v.wait_ge(self.have_stat, self.T * b + self.T)
        self.link(nc, n, v.tensor_tensor(self.mean[:, :], st[:, :, 1], st[:, :, 4], ALU.add))
        self.link(nc, n, v.tensor_scalar(self.mean[:, :], self.mean[:, :], 0.5, None, ALU.mult))
        self.link(nc, n, v.tensor_tensor(self.t[:, :], st[:, :, 1], st[:, :, 4], ALU.subtract))
        self.link(nc, n, v.tensor_tensor(self.t[:, :], self.t[:, :], self.t[:, :], ALU.mult))
        self.link(nc, n, v.tensor_tensor(self.u[:, :], st[:, :, 2], st[:, :, 5], ALU.add))
        self.link(nc, n, v.tensor_scalar(self.u[:, :], self.u[:, :], 1.0 / self.D, EPS, ALU.mult, ALU.add))
        v.scalar_tensor_tensor(out=self.var[:, :], in0=self.t[:, :], scalar=0.25, in1=self.u[:, :], op0=ALU.mult,
                               op1=ALU.add).then_inc(self.have_var, 1)

    def root(self, nc, b):
        nc.scalar.wait_ge(self.have_var, b + 1)
        nc.scalar.activation(self.std[:, :], self.var[:, :], ACT.Sqrt).then_inc(self.have_std, 1)

    def scale(self, nc, b, out, y):
        v, n = nc.vector, [self.STEPS * b + self.VARIANCE_STEPS]
        v.wait_ge(self.have_std, b + 1)
        self.link(nc, n, v.reciprocal(self.r[:, :], self.std[:, :]))
        self.link(nc, n, v.tensor_tensor(self.t[:, :], self.r[:, :], self.r[:, :], ALU.mult))
        self.link(nc, n, v.tensor_tensor(self.t[:, :], self.t[:, :], self.var[:, :], ALU.mult))
        self.link(nc, n, v.tensor_scalar(self.t[:, :], self.t[:, :], -0.5, 1.5, ALU.mult, ALU.add))
        self.link(nc, n, v.tensor_tensor(self.r[:, :], self.r[:, :], self.t[:, :], ALU.mult))
        for i in range(self.T):
            v.tensor_scalar(out[:, i, :], y[:, i, :], self.mean[:, i:i + 1], self.r[:, i:i + 1], ALU.subtract,
                            ALU.mult).then_inc(self.normed, 1)


def load_weights(nc, wqT, wkT, wv, A, WV, D):
    T = D // P
    with ExitStack() as ctx:
        sc = Scope(nc, ctx, "w")
        raw = sc.sb("raw", [P, 3, T, D])
        part = sc.sb("part", [P, 2, 2, T, D], F32R)
        pa = sc.ps("a", [P, T, D])
        loaded = [sc.sem(f"loaded{n}") for n in range(3)]
        hi_done, lo_done, a_mm, a_hi, a_lo = (sc.sem(n) for n in ("hi_done", "lo_done", "a_mm", "a_hi", "a_lo"))

        def dest(w, h):
            return WV[:, h, :, :] if w == 2 else part[:, w, h, :, :]

        with nc.Block() as block:

            @block.sync
            def _(sp):
                for w, src in enumerate((wqT, wkT, wv)):
                    sp.dma_start(raw[:, w, :, :], src.rearrange("(k p) n -> p k n", p=P)).then_inc(loaded[w], 16)

            @block.scalar
            def _(act):
                for w in range(3):
                    act.wait_ge(loaded[w], 16)
                    for k in range(T):
                        nc.scalar.copy(dest(w, HI)[:, k, :], raw[:, w, k, :]).then_inc(hi_done, 1)
                for m in range(T):
                    act.wait_ge(a_mm, m + 1)
                    nc.scalar.activation(A[:, HI, m, :], pa[:, m, :], ACT.Copy,
                                         scale=float(D) ** -0.5).then_inc(a_hi, 1)

            @block.vector
            def _(dve):
                for w in range(3):
                    for k in range(T):
                        dve.wait_ge(hi_done, T * w + k + 1)
                        nc.vector.tensor_tensor(dest(w, LO)[:, k, :], raw[:, w, k, :], as_f32(dest(w, HI)[:, k, :]),
                                                ALU.subtract).then_inc(lo_done, 1)
                for m in range(T):
                    dve.wait_ge(a_hi, m + 1)
                    nc.vector.scalar_tensor_tensor(out=A[:, LO, m, :], in0=pa[:, m, :], scalar=float(D) ** -0.5,
                                                   in1=as_f32(A[:, HI, m, :]), op0=ALU.mult,
                                                   op1=ALU.subtract).then_inc(a_lo, 1)

            @block.tensor
            def _(pe):
                pe.wait_ge(lo_done, 2 * T)
                for m in range(T):
                    three_pass(nc, pa[:, m, :], lambda h, k: part[:, 0, h, k, m * P:(m + 1) * P],
                               lambda h, k: part[:, 1, h, k, :], T).then_inc(a_mm, 1)


def self_attention(nc, x, xT, ctxT, wpair, A, WV, ident, x1, xparts, cparts, wparts, NB, S, D, QSCALE):
    T, K = S // P, D // P
    with ExitStack() as ctx:
        sc = Scope(nc, ctx, "s")
        xraw = sc.sb("xraw", [P, K, S])
        xp = sc.sb("xp", [P, 2, K, S], F32R)
        qp = sc.sb("qp", [P, 2, K, S], F32R)
        vp = sc.sb("vp", [P, 2, T, D], F32R)
        y = sc.sb("y", [P, T, D])
        x1t = sc.sb("x1t", [P, 2, K, S], F32R)
        strip = sc.sb("strip", [P, (2 * T - 1) * P])
        upper = sc.sb("upper", [P, T, S])
        ms = sc.sb("ms", [P, T, S])
        gone = sc.sb("gone", [P, T, S])
        prob = sc.sb("prob", [P, T, S])
        pt = sc.sb("pt", [P, 2, T, S], F32R)
        negmax, den, rden = sc.sb("negmax", [P, T]), sc.sb("den", [P, T]), sc.sb("rden", [P, T])
        NWP = len(wparts)
        assert K == NWP and D == S
        wraw = sc.sb("wraw", [P, NWP, D])
        wsp = sc.sb("wsp", [P, NWP, 2, D], F32R)
        proj, spsum = sc.ps("proj", [P, 2, 512]), sc.ps("score", [P, 2, 512])
        tpsum, opsum = sc.ps("turned", [P, 2, 512]), sc.ps("av", [P, 2, 512])
        norm = Norm(sc, T, D)
        passed = sc.sem("passed")

        (xT_loaded, x_loaded, x_hi, x_lo, q_mm, q_hi, q_lo, s_mm, v_mm, v_hi, v_lo, t_mm, pt_hi, pt_lo, av_mm,
         x1t_mm, x1t_hi, x1t_out, strip_step, cut, is_zero, masked, prob_exp, have_rden, prob_ready, y_stored,
         x1t_stored, base, w_loaded, w_scaled, w_hi, w_lo, w_stored, c_stored) = (sc.sem(n) for n in (
             "xT_loaded", "x_loaded", "x_hi", "x_lo", "q_mm", "q_hi", "q_lo", "s_mm", "v_mm", "v_hi", "v_lo",
             "t_mm", "pt_hi", "pt_lo", "av_mm", "x1t_mm", "x1t_hi", "x1t_out", "strip_step", "cut", "is_zero", "masked",
             "prob_exp", "have_rden", "prob_ready", "y_stored", "x1t_stored", "base", "w_loaded", "w_scaled",
             "w_hi", "w_lo", "w_stored", "c_stored"))

        def batches(eng, body):
            body(0, True, False)
            with eng.Fori(1, NB - 1) as b:
                body(b, False, False)
            body(NB - 1, False, True)

        with nc.Block() as block:

            @block.sync
            def _(sp):
                def load_xT(b):
                    sp.dma_start(xraw[:, :, :], xT[b].rearrange("(k p) n -> p k n", p=P)).then_inc(xT_loaded, 16)

                def store_x1T(b):
                    sp.wait_ge(x1t_out, K * b + K)
                    sp.dma_start(xparts[b], as_f32(x1t[:, :, :, :])).then_inc(x1t_stored, 16)

                def store_ctx(b):
                    sp.wait_ge(w_lo, NWP * (2 * b + 2))
                    sp.dma_start(cparts[b], as_f32(wsp[:, :, :, :])).then_inc(c_stored, 16)

                def body(b, first, last):
                    if first:
                        load_xT(b)
                    else:
                        store_ctx(b - 1)
                    sp.dma_start(wraw[:, :, :], wpair[b].rearrange("w p n -> p w n")).then_inc(w_loaded, 16)
                    if not last:
                        sp.wait_ge(x_lo, K * b + K)
                        load_xT(b + 1)
                    if not first:
                        store_x1T(b - 1)
                        sp.wait_ge(y_stored, 16 * b)
                        sp.wait_ge(x1t_mm, K * b)
                    sp.dma_start(y[:, :, :], x[b].rearrange("(t p) d -> p t d", p=P)).then_inc(x_loaded, 16)
                    sp.wait_ge(w_lo, NWP * (2 * b + 1))
                    for w, dst in enumerate(wparts):
                        sp.dma_start(dst[b], as_f32(wsp[:, w, :, :])).then_inc(w_stored, 16)
                    sp.dma_start(wraw[:, :, :], ctxT[b].rearrange("(k p) n -> p k n", p=P)).then_inc(w_loaded, 16)
                    sp.wait_ge(norm.normed, T * b + T)
                    sp.dma_start(x1[b].rearrange("(t p) d -> p t d", p=P), y[:, :, :]).then_inc(y_stored, 16)

                batches(sp, body)
                store_ctx(NB - 1)
                store_x1T(NB - 1)
                sp.wait_ge(y_stored, 16 * NB)
                sp.wait_ge(x1t_stored, 16 * NB + 16)
                sp.wait_ge(w_stored, 16 * NWP * NB)
                sp.wait_ge(c_stored, 16 * NB)

            @block.gpsimd
            def _(pool):
                nc.gpsimd.memset(strip[:, :(T - 1) * P], 0.0).then_inc(strip_step, 1)
                nc.gpsimd.memset(strip[:, (T - 1) * P:], 1.0).then_inc(strip_step, 1)
                pool.wait_ge(strip_step, 2)
                tri = strip[:, (T - 1) * P:T * P]
                nc.gpsimd.affine_select(out=tri, in_=tri, compare_op=ALU.is_ge, fill=0.0, base=0, pattern=[[1, P]],
                                        channel_multiplier=-1).then_inc(strip_step, 1)

                def split_round(n, free, stored):
                    if free is not None:
                        pool.wait_ge(stored, free)
                    for w in range(NWP):
                        pool.sem_inc(passed, 1)
                        nc.gpsimd.tensor_scalar(wsp[:, w, HI, :], wraw[:, w, :], 1.0, 1.0, ALU.mult,
                                                ALU.mult).then_inc(w_hi, 1)
                        pool.wait_ge(w_hi, NWP * n + w + 1)
                        nc.gpsimd.tensor_tensor(wsp[:, w, LO, :], wraw[:, w, :], as_f32(wsp[:, w, HI, :]),
                                                ALU.subtract).then_inc(w_lo, 1)

                def body(b, first, last):
                    pool.wait_ge(w_loaded, 32 * b + 16)
                    pool.sem_inc(passed, 1)
                    nc.gpsimd.tensor_scalar(wraw[:, 0, :], wraw[:, 0, :], QSCALE, 1.0, ALU.mult,
                                            ALU.mult).then_inc(w_scaled, 1)
                    pool.wait_ge(w_scaled, b + 1)
                    split_round(b * 2, None if first else 16 * b, c_stored)
                    for i in range(T):
                        pool.wait_ge(have_rden, T * b + i + 1)
                        pool.sem_inc(passed, 1)
                        nc.gpsimd.tensor_scalar(prob[:, i, :], prob[:, i, :], rden[:, i:i + 1], 1.0, ALU.mult,
                                                ALU.mult).then_inc(prob_ready, 1)
                    pool.wait_ge(w_loaded, 32 * b + 32)
                    split_round(b * 2 + 1, 16 * NWP * b + 16 * NWP, w_stored)

                batches(pool, body)

            @block.scalar
            def _(act):
                act.sem_inc(x1t_stored, 16)

                def turn_x1(b):
                    for k in range(K):
                        act.wait_ge(x1t_mm, K * b + k + 1)
                        act.wait_ge(x1t_stored, 16 * b + 16)
                        nc.scalar.copy(x1t[:, HI, k, :], tpsum[:, k % 2, :]).then_inc(x1t_hi, 1)

                def split_x(b, first):
                    act.wait_ge(xT_loaded, 16 * b + 16)
                    if not first:
                        act.wait_ge(s_mm, T * b)
                        act.wait_ge(v_mm, T * b)
                    for k in range(K):
                        nc.scalar.copy(xp[:, HI, k, :], xraw[:, k, :]).then_inc(x_hi, 1)

                def body(b, first, last):
                    if first:
                        split_x(b, True)
                    for m in range(K):
                        act.wait_ge(q_mm, K * b + m + 1)
                        nc.scalar.copy(qp[:, HI, m, :], proj[:, m % 2, :]).then_inc(q_hi, 1)
                    if not first:
                        turn_x1(b - 1)
                    for i in range(T):
                        act.wait_ge(masked, T * b + i + 1)
                        if not first:
                            act.wait_ge(t_mm, T * b)
                        nc.scalar.activation(prob[:, i, :], ms[:, i, :], ACT.Exp, bias=negmax[:, i:i + 1], scale=-1.0,
                                             accum_out=den[:, i:i + 1]).then_inc(prob_exp, 1)
                    for i in range(T):
                        act.wait_ge(v_mm, T * b + i + 1)
                        if not first:
                            act.wait_ge(av_mm, T * b)
                        nc.scalar.copy(vp[:, HI, i, :], proj[:, i % 2, :]).then_inc(v_hi, 1)
                    for k in range(T):
                        act.wait_ge(t_mm, T * b + k + 1)
                        nc.scalar.copy(pt[:, HI, k, :], tpsum[:, k % 2, :]).then_inc(pt_hi, 1)
                    if not last:
                        split_x(b + 1, False)
                    norm.root(nc, b)

                batches(act, body)
                turn_x1(NB - 1)

            @block.vector
            def _(dve):
                for i in range(1, T):
                    nc.vector.memset(ms[:, i, :i * P], NEG).then_inc(base, 1)

                def split_x(b):
                    for k in range(K):
                        dve.wait_ge(x_hi, K * b + k + 1)
                        nc.vector.tensor_tensor(xp[:, LO, k, :], xraw[:, k, :], as_f32(xp[:, HI, k, :]),
                                                ALU.subtract).then_inc(x_lo, 1)

                def turn_x1(b):
                    for k in range(K):
                        dve.wait_ge(x1t_hi, K * b + k + 1)
                        nc.vector.tensor_tensor(x1t[:, LO, k, :], tpsum[:, k % 2, :], as_f32(x1t[:, HI, k, :]),
                                                ALU.subtract).then_inc(x1t_out, 1)

                def cut_tile(b, i, first):
                    dve.wait_ge(s_mm, T * b + i + 1)
                    if first:
                        dve.wait_ge(strip_step, 3)
                    else:
                        dve.wait_ge(masked, T * b - T + i + 1)
                        dve.wait_ge(prob_exp, T * b - T + i + 1)
                    nc.vector.tensor_tensor(upper[:, i, i * P:], spsum[:, i % 2, i * P:],
                                            strip[:, (T - 1) * P:(2 * T - 1 - i) * P], ALU.mult).then_inc(cut, 1)

                def recip(b, i):
                    dve.wait_ge(prob_exp, T * b + i + 1)
                    nc.vector.reciprocal(rden[:, i:i + 1], den[:, i:i + 1]).then_inc(have_rden, 1)

                def body(b, first, last):
                    if first:
                        split_x(b)
                    for m in range(K):
                        dve.wait_ge(q_hi, K * b + m + 1)
                        nc.vector.tensor_tensor(qp[:, LO, m, :], proj[:, m % 2, :], as_f32(qp[:, HI, m, :]),
                                                ALU.subtract).then_inc(q_lo, 1)
                    if not first:
                        turn_x1(b - 1)
                    for i in range(T):
                        if i == 0:
                            cut_tile(b, 0, first)
                        dve.wait_ge(cut, T * b + i + 1)
                        nc.vector.tensor_scalar(gone[:, i, i * P:], upper[:, i, i * P:], 0.0, -NEG, ALU.is_equal,
                                                ALU.mult).then_inc(is_zero, 1)
                        dve.wait_ge(is_zero, T * b + i + 1)
                        if i + 1 < T:
                            cut_tile(b, i + 1, first)
                        else:
                            recip(b, i - 1)
                        if first and i == 0:
                            dve.wait_ge(base, T - 1)
                        nc.vector.tensor_tensor_reduce(ms[:, i, i * P:], upper[:, i, i * P:], gone[:, i, i * P:], -1.0,
                                                       NEG, ALU.add, ALU.min, negmax[:, i:i + 1]).then_inc(masked, 1)
                        if 0 < i < T - 1:
                            recip(b, i - 1)
                    recip(b, T - 1)
                    for i in range(T):
                        dve.wait_ge(v_hi, T * b + i + 1)
                        nc.vector.tensor_tensor(vp[:, LO, i, :], proj[:, i % 2, :], as_f32(vp[:, HI, i, :]),
                                                ALU.subtract).then_inc(v_lo, 1)
                    for k in range(T):
                        dve.wait_ge(pt_hi, T * b + k + 1)
                        nc.vector.tensor_tensor(pt[:, LO, k, :], tpsum[:, k % 2, :], as_f32(pt[:, HI, k, :]),
                                                ALU.subtract).then_inc(pt_lo, 1)
                    if not last:
                        split_x(b + 1)
                    dve.wait_ge(x_loaded, 16 * b + 16)
                    for i in range(T):
                        dve.wait_ge(av_mm, T * b + i + 1)
                        nc.vector.tensor_tensor(y[:, i, :], opsum[:, i % 2, :], y[:, i, :],
                                                ALU.add).then_inc(norm.summed, 1)
                        norm.stats(nc, b, i, y)
                    norm.variance(nc, b)
                    norm.scale(nc, b, y, y)

                batches(dve, body)
                turn_x1(NB - 1)

            @block.tensor
            def _(pe):
                def turn_x1(b, first=False):
                    pe.wait_ge(norm.normed, T * b + T)
                    for k in range(K):
                        if k < 2:
                            pe.wait_ge(pt_lo, T * b + T)
                        else:
                            pe.wait_ge(x1t_out, K * b + k - 1)
                        for i in range(T):
                            t = nc.tensor.transpose(tpsum[:, k % 2, i * P:(i + 1) * P], y[:, i, k * P:(k + 1) * P],
                                                    ident[:, :])
                        t.then_inc(x1t_mm, 1)

                def body(b, first, last):
                    pe.wait_ge(x_lo, K * b + K)
                    for m in range(K):
                        if m < 2 and not first:
                            pe.wait_ge(v_lo, T * b - 2 + m + 1)
                        if m >= 2:
                            pe.wait_ge(q_lo, K * b + m - 1)
                        three_pass(nc, proj[:, m % 2, :], lambda h, k: A[:, h, k, m * P:(m + 1) * P],
                                   lambda h, k: xp[:, h, k, :], K).then_inc(q_mm, 1)
                    if not first:
                        turn_x1(b - 1)
                    pe.wait_ge(q_lo, K * b + K)
                    for i in range(T):
                        if i < 2:
                            if not first:
                                pe.wait_ge(cut, T * b - 2 + i + 1)
                        else:
                            pe.wait_ge(cut, T * b + i - 1)
                        three_pass(nc, spsum[:, i % 2, i * P:], lambda h, k: qp[:, h, k, i * P:(i + 1) * P],
                                   lambda h, k: xp[:, h, k, i * P:], K).then_inc(s_mm, 1)
                    for i in range(T):
                        if i >= 2:
                            pe.wait_ge(v_lo, T * b + i - 1)
                        three_pass(nc, proj[:, i % 2, :], lambda h, k: xp[:, h, k, i * P:(i + 1) * P],
                                   lambda h, k: WV[:, h, k, :], K).then_inc(v_mm, 1)
                    for k in range(T):
                        if k < 2:
                            if not first:
                                pe.wait_ge(x1t_out, K * b)
                        else:
                            pe.wait_ge(pt_lo, T * b + k - 1)
                        for i in range(T):
                            if k == 0:
                                pe.wait_ge(prob_ready, T * b + i + 1)
                            t = nc.tensor.transpose(tpsum[:, k % 2, i * P:(i + 1) * P],
                                                    prob[:, i, k * P:(k + 1) * P], ident[:, :])
                        t.then_inc(t_mm, 1)
                    pe.wait_ge(v_lo, T * b + T)
                    pe.wait_ge(pt_lo, T * b + T)
                    for i in range(T):
                        if i < 2:
                            if not first:
                                pe.wait_ge(norm.summed, T * b - 2 + i + 1)
                        else:
                            pe.wait_ge(norm.summed, T * b + i - 1)
                        three_pass(nc, opsum[:, i % 2, :], lambda h, k: pt[:, h, k, i * P:(i + 1) * P],
                                   lambda h, k: vp[:, h, k, :], T).then_inc(av_mm, 1)

                batches(pe, body)
                turn_x1(NB - 1)


def cross_attention(nc, y_steps, xparts, cparts, wqparts, wkparts, wvparts, woparts, bq, bk, bv, ident, NB, S, D, H, DK):
    T, K = S // P, D // P
    HALVES, HH = 2, H // 2
    GROUPS = HALVES * NB
    PAIRS = HH // 2
    CH = HH * DK
    TILES, LEAD = T * HH, 5
    assert 2 * DK == P and CH == 512 and S == 512 and PAIRS == 4 and T == 4 and GROUPS % 2 == 0

    SLOTS = ["V3", "O0", "K2", "Q2", "O1", "O2", "K3", "Q3", "O3", "V0+", "K0+", "Q0+", "V1+", "V2+", "K1+", "Q1+"]
    assert 2 * len(SLOTS) == TILES
    FIRST_AHEAD = SLOTS.index("V0+")
    MADE = [name for name in SLOTS if name[0] != "O"]
    AHEAD = MADE[MADE.index("V0+"):]

    def pieces(name):
        return 1 if name[0] == "V" else 2

    def made(g, name):
        return len(MADE) * g + len(AHEAD) + MADE.index(name) + 1

    def split(g, name, head=1):
        n = MADE.index(name)
        return (sum(map(pieces, MADE)) * g + sum(map(pieces, AHEAD)) + sum(map(pieces, MADE[:n + 1]))
                - (1 - head if name[0] != "V" else 0))

    def pair_slot(g, letter, j):
        return (g - 1, f"{letter}{j}+") if j < 2 else (g, f"{letter}{j}")

    def wait(eng, sem, n):
        if not (isinstance(n, int) and n <= 0):
            eng.wait_ge(sem, n)

    def groups(eng, body):
        body(0, 0, True, False)
        with eng.Fori(0, GROUPS // 2 - 1) as c:
            body(c * 2 + 1, 1, False, False)
            body(c * 2 + 2, 0, False, False)
        body(GROUPS - 1, 1, False, True)

    def ahead(g, t, last):
        return [(g, t)] if t < TILES else [] if last else [(g + 1, t - TILES)]

    def slot(t, first, last):
        name = SLOTS[t // 2]
        return None if (first and name[0] == "O") or (last and name[-1] == "+") else name

    def head_before(g, t, first):
        return [(g, t // T - 1)] if t else [] if first else [(g - 1, HH - 1)]

    with ExitStack() as ctx:
        sc = Scope(nc, ctx, "c")
        WV = sc.sb("WV", [P, 2, K, CH], F32R)
        WO = sc.sb("WO", [P, 2, PAIRS, D], F32R)
        xp = sc.sb("xp", [P, 2, K, S], F32R)
        cp = sc.sb("cp", [P, K, 2, S], F32R)
        wk, wq = sc.sb("wk", [P, 2, K, P], F32R), sc.sb("wq", [P, 2, K, P], F32R)
        qs = sc.sb("qs", [P, 2, 2, S], F32R)
        ks = sc.sb("ks", [P, 2, 2, 2, S], F32R)
        vs = sc.sb("vs", [P, 2, T, HH, 2 * DK], F32R)
        prob = sc.sb("prob", [P, 2, T, S])
        pt = sc.sb("pt", [P, 2, 2, S], F32R)
        opart, osum = sc.sb("opart", [P, S]), sc.sb("osum", [P, 2, S])
        op = sc.sb("op", [P, 2, PAIRS, S], F32R)
        y = sc.sb("y", [P, T, D])
        negmax, den, rden = sc.sb("negmax", [P, 2, T]), sc.sb("den", [P, 2, T]), sc.sb("rden", [P, 2, T])
        raw_b = [sc.sb("raw_bk", [P, H // 2]), sc.sb("raw_bq", [P, H // 2]), sc.sb("raw_bv", [DK, H])]
        bks, bqs, bvs = (sc.sb("bk", [P, GROUPS * PAIRS]), sc.sb("bq", [P, GROUPS * PAIRS]),
                         sc.sb("bv", [DK, GROUPS * HH]))
        projp, spsum = sc.ps("proj", [P, 2, 512]), sc.ps("score", [P, 2, 512])
        tpsum, opsum = sc.ps("turned", [P, 2, 512]), sc.ps("av", [P, 2, 512])

        (b_loaded, bias_ready, x_loaded, wk_loaded, wq_loaded, wv_loaded, wo_loaded, wv_ready, wo_ready, proj_mm,
         proj_hi, proj_lo, s_mm, smax, p_exp, have_rden, p_ready, t_mm, pt_hi, pt_lo, av_mm, o_part, o_sum, op_hi,
         op_lo, wo_mm, wo_out, y_loaded, y_stored, passed) = (sc.sem(n) for n in (
             "b_loaded", "bias_ready", "x_loaded", "wk_loaded", "wq_loaded", "wv_loaded", "wo_loaded", "wv_ready",
             "wo_ready", "proj_mm", "proj_hi", "proj_lo", "s_mm", "smax", "p_exp", "have_rden", "p_ready", "t_mm",
             "pt_hi", "pt_lo", "av_mm", "o_part", "o_sum", "op_hi", "op_lo", "wo_mm", "wo_out", "y_loaded", "y_stored",
             "passed"))
        k_doubled = [sc.sem(f"k_doubled{n}") for n in range(2)]
        c_loaded = [sc.sem(f"c_loaded{n}") for n in range(K)]

        def sides(e):
            own, other = slice(0, DK), slice(DK, P)
            return (own, other) if e == 0 else (other, own)

        with nc.Block() as block:

            @block.sync
            def _(sp):
                def load_ctx(b):
                    for k in range(K):
                        sp.dma_start(as_f32(cp[:, k, :, :]),
                                     cparts[b, :, k * 2 * S:(k + 1) * 2 * S].rearrange("p (a n) -> p a n",
                                                                                       a=2)).then_inc(c_loaded[k], 16)

                def load_x(b):
                    sp.dma_start(as_f32(xp[:, :, :, :]), xparts[b]).then_inc(x_loaded, 16)

                def load_pair(dst, parts, pair, loaded):
                    sp.dma_start(as_f32(dst[:, :, :, :]), parts[pair]).then_inc(loaded, 16)

                def load_half(dst, parts, h, loaded):
                    for k in range(K):
                        sp.dma_start(as_f32(dst[:, :, k, :]),
                                     parts[h * K + k].rearrange("p (a n) -> p a n", a=2)).then_inc(loaded, 16)

                def load_y(g):
                    sp.dma_start(y[:, :, :], y_steps[g].rearrange("(t p) d -> p t d", p=P)).then_inc(y_loaded, 16)

                def store_y(g):
                    sp.wait_ge(wo_out, T * g + T)
                    sp.dma_start(y_steps[g + NB].rearrange("(t p) d -> p t d", p=P), y[:, :, :]).then_inc(y_stored, 16)
                    sp.wait_ge(y_stored, 16 * g + 16)

                def double_k(g, name):
                    ring = int(name[1]) % 2
                    for e in range(2):
                        own, other = sides(e)
                        sp.wait_ge(proj_lo, split(g, name, e))
                        sp.dma_start(as_f32(ks[other, ring, e, :, :]),
                                     as_f32(ks[own, ring, e, :, :])).then_inc(k_doubled[e], 16)

                load_ctx(0)
                load_half(WV, wvparts, 0, wv_loaded)
                load_pair(wk, wkparts, 0, wk_loaded)
                load_pair(wq, wqparts, 0, wq_loaded)
                load_x(0)
                for dst, src in zip(raw_b, (bk, bq, bv)):
                    sp.dma_start(dst[:, :], src).then_inc(b_loaded, 16)
                load_y(0)
                sp.wait_ge(wv_loaded, 16 * K)
                sp.sem_inc(wv_ready, 1)
                sp.wait_ge(proj_mm, made(-1, "K0+"))
                load_pair(wk, wkparts, 1, wk_loaded)
                double_k(-1, "K0+")
                sp.wait_ge(proj_mm, made(-1, "Q0+"))
                load_pair(wq, wqparts, 1, wq_loaded)
                sp.wait_ge(proj_mm, made(-1, "K1+"))
                load_pair(wk, wkparts, 2, wk_loaded)
                double_k(-1, "K1+")
                sp.wait_ge(proj_mm, made(-1, "Q1+"))
                load_pair(wq, wqparts, 2, wq_loaded)

                def body(g, b, h, opens, closes):
                    last = closes and h == HALVES - 1
                    nb, nh = (0, h + 1) if closes else (b + 1, h)
                    if closes and not last:
                        sp.wait_ge(proj_mm, made(g, "V3"))
                        load_half(WV, wvparts, nh, wv_loaded)
                    for name, following in (("K2", (h, 3)), ("K3", (nh, 0))):
                        final = last and following[1] == 0
                        sp.wait_ge(proj_mm, made(g, name))
                        if not final:
                            load_pair(wk, wkparts, following[0] * PAIRS + following[1], wk_loaded)
                        if name == "K3" and not last:
                            load_ctx(nb)
                        double_k(g, name)
                        if not final:
                            sp.wait_ge(proj_mm, made(g, "Q" + name[1]))
                            load_pair(wq, wqparts, following[0] * PAIRS + following[1], wq_loaded)
                        if name == "K3" and not last:
                            load_x(nb)
                    if not last:
                        if closes:
                            sp.wait_ge(wv_loaded, 16 * K * (nh + 1))
                        sp.sem_inc(wv_ready, 1)
                    if not (opens and h == 0):
                        store_y(g - 1)
                        load_y(g)
                    if opens:
                        wait(sp, wo_mm, T * g)
                        load_half(WO, woparts, h, wo_loaded)
                    if not last:
                        for name, j in (("K0+", 1), ("K1+", 2)):
                            sp.wait_ge(proj_mm, made(g, name))
                            load_pair(wk, wkparts, nh * PAIRS + j, wk_loaded)
                            double_k(g, name)
                            sp.wait_ge(proj_mm, made(g, "Q" + name[1:]))
                            load_pair(wq, wqparts, nh * PAIRS + j, wq_loaded)
                    if opens:
                        sp.wait_ge(wo_loaded, 16 * K * (h + 1))
                    sp.sem_inc(wo_ready, 1)

                for h in range(HALVES):
                    body(NB * h, 0, h, True, False)
                    with sp.Fori(1, NB - 1) as b:
                        body(b + NB * h, b, h, False, False)
                    body(NB * h + NB - 1, NB - 1, h, False, True)
                store_y(GROUPS - 1)

            @block.gpsimd
            def _(pool):
                def norm_tile(g, t):
                    n, i = divmod(t, T)
                    pool.wait_ge(have_rden, TILES * g + t + 1)
                    pool.sem_inc(passed, 1)
                    nc.gpsimd.tensor_scalar(prob[:, n % 2, i, :], prob[:, n % 2, i, :], rden[:, n % 2, i:i + 1], 1.0,
                                            ALU.mult, ALU.mult).then_inc(p_ready, 1)

                def split_hi(g, j):
                    pool.wait_ge(o_sum, HH * g + 2 * j + 2)
                    if j == 0:
                        wait(pool, wo_mm, T * g)
                    pool.sem_inc(passed, 1)
                    nc.gpsimd.tensor_scalar(op[:, HI, j, :], osum[:, j % 2, :], 1.0, 1.0, ALU.mult,
                                            ALU.mult).then_inc(op_hi, 1)

                def split_lo(g, j):
                    pool.wait_ge(op_hi, PAIRS * g + j + 1)
                    nc.gpsimd.tensor_tensor(op[:, LO, j, :], osum[:, j % 2, :], as_f32(op[:, HI, j, :]),
                                            ALU.subtract).then_inc(op_lo, 1)

                SPLIT_AT = {18: 0, 20: 1, 25: 2}

                def body(g, u, first, last):
                    for t in range(TILES):
                        if t == 1 and not first:
                            split_hi(g - 1, PAIRS - 1)
                            split_lo(g - 1, PAIRS - 1)
                        for tile in ahead(g, t + LEAD, last):
                            norm_tile(*tile)
                        if t in SPLIT_AT:
                            split_hi(g, SPLIT_AT[t])
                        if t - 1 in SPLIT_AT:
                            split_lo(g, SPLIT_AT[t - 1])

                for t in range(LEAD):
                    norm_tile(0, t)
                groups(pool, body)
                split_hi(GROUPS - 1, PAIRS - 1)
                split_lo(GROUPS - 1, PAIRS - 1)

            @block.scalar
            def _(act):
                def exp_tile(g, t):
                    n, i = divmod(t, T)
                    head = HH * g + n
                    act.wait_ge(smax, T * head + i + 1)
                    if i == 0:
                        wait(act, t_mm, T * head - T)
                    nc.scalar.activation(prob[:, n % 2, i, :], spsum[:, i % 2, :], ACT.Exp,
                                         bias=negmax[:, n % 2, i:i + 1], scale=1.0,
                                         accum_out=den[:, n % 2, i:i + 1]).then_inc(p_exp, 1)

                def proj_hi_part(g, name, u):
                    bank, j = projp[:, SLOTS.index(name) % 2, :], int(name[1])
                    G = g + 1 if name[-1] == "+" else g
                    act.wait_ge(proj_mm, made(g, name))
                    if name[0] == "V":
                        if j == 0:
                            wait(act, av_mm, TILES * (G - 1))
                        ring = 1 - u if name[-1] == "+" else u
                        nc.scalar.copy(vs[:, ring, j, :, 0:DK],
                                       bank.rearrange("p (h d) -> p h d", d=DK)).then_inc(proj_hi, 1)
                        return
                    bias = bks if name[0] == "K" else bqs
                    wait(act, s_mm, T * (HH * G + 2 * j - 2))
                    for e in range(2):
                        rows = sides(e)[0]
                        dst = ks[rows, j % 2, e, HI, :] if name[0] == "K" else qs[rows, j % 2, e, :]
                        nc.scalar.activation(dst, bank[rows, :], ACT.Identity,
                                             bias=bias[rows, bass.ds(G * PAIRS + j, 1)], scale=1.0).then_inc(proj_hi, 1)

                def pt_tile(g, t):
                    act.wait_ge(t_mm, TILES * g + t + 1)
                    wait(act, av_mm, TILES * g + t - 1)
                    nc.scalar.copy(pt[:, t % 2, HI, :], tpsum[:, t % 2, :]).then_inc(pt_hi, 1)

                def o_first(g, n):
                    head = HH * g + n
                    act.wait_ge(av_mm, T * head + T)
                    wait(act, o_sum, head - 1)
                    nc.scalar.activation(opart[sides(n % 2)[0], :], opsum[0:DK, n % 2, :], ACT.Identity,
                                         bias=bvs[:, bass.ds(head, 1)], scale=1.0).then_inc(o_part, 1)

                def body(g, u, first, last):
                    for t in range(TILES):
                        for tile in ahead(g, t + LEAD, last):
                            exp_tile(*tile)
                        pt_tile(g, t)
                        if t % T == 0:
                            for head in head_before(g, t, first):
                                o_first(*head)
                        name = slot(t, first, last)
                        if t % 2 == 1 and name and name[0] != "O":
                            proj_hi_part(g, name, u)

                act.wait_ge(bias_ready, 3 * NB)
                for name in AHEAD:
                    proj_hi_part(-1, name, 1)
                    if name == "V2+":
                        for t in range(2):
                            exp_tile(0, t)
                for t in range(2, LEAD):
                    exp_tile(0, t)
                groups(act, body)
                o_first(GROUPS - 1, HH - 1)

            @block.vector
            def _(dve):
                def max_tile(g, t):
                    n, i = divmod(t, T)
                    dve.wait_ge(s_mm, TILES * g + t + 1)
                    nc.vector.tensor_reduce(negmax[:, n % 2, i:i + 1], spsum[:, i % 2, :], AX.X, ALU.max,
                                            negate=True).then_inc(smax, 1)

                def recip(g, t):
                    n, i = divmod(t, T)
                    dve.wait_ge(p_exp, TILES * g + t + 1)
                    nc.vector.reciprocal(rden[:, n % 2, i:i + 1], den[:, n % 2, i:i + 1]).then_inc(have_rden, 1)

                def proj_lo_part(g, name, u, heads=(0, 1)):
                    bank, j = projp[:, SLOTS.index(name) % 2, :], int(name[1])
                    G = g + 1 if name[-1] == "+" else g
                    if name[0] == "V":
                        ring = 1 - u if name[-1] == "+" else u
                        dve.wait_ge(proj_hi, split(g, name))
                        nc.vector.tensor_tensor(vs[:, ring, j, :, DK:], bank.rearrange("p (h d) -> p h d", d=DK),
                                                as_f32(vs[:, ring, j, :, 0:DK]), ALU.subtract).then_inc(proj_lo, 1)
                        return
                    bias = bks if name[0] == "K" else bqs
                    for e in heads:
                        rows, other = sides(e)
                        dve.wait_ge(proj_hi, split(g, name, e))
                        if name[0] == "K":
                            hi, lo = ks[rows, j % 2, e, HI, :], ks[rows, j % 2, e, LO, :]
                        else:
                            hi, lo = qs[rows, j % 2, e, :], qs[other, j % 2, e, :]
                        nc.vector.scalar_tensor_tensor(out=lo, in0=bank[rows, :],
                                                       scalar=bias[rows, bass.ds(G * PAIRS + j, 1)], in1=as_f32(hi),
                                                       op0=ALU.add, op1=ALU.subtract).then_inc(proj_lo, 1)

                def add_out(g, name):
                    i = int(name[1])
                    if i == 0:
                        dve.wait_ge(y_loaded, 16 * g)
                    dve.wait_ge(wo_mm, T * (g - 1) + i + 1)
                    nc.vector.tensor_tensor(y[:, i, :], projp[:, SLOTS.index(name) % 2, :], y[:, i, :],
                                            ALU.add).then_inc(wo_out, 1)

                def pt_tile(g, t):
                    dve.wait_ge(pt_hi, TILES * g + t + 1)
                    nc.vector.tensor_tensor(pt[:, t % 2, LO, :], tpsum[:, t % 2, :], as_f32(pt[:, t % 2, HI, :]),
                                            ALU.subtract).then_inc(pt_lo, 1)

                def o_second(g, n):
                    head = HH * g + n
                    dve.wait_ge(o_part, head + 1)
                    wait(dve, op_lo, PAIRS * g + n // 2 - 1)
                    rows = sides(n % 2)[0]
                    nc.vector.tensor_tensor(osum[rows, n // 2 % 2, :], opsum[DK:P, n % 2, :], opart[rows, :],
                                            ALU.add).then_inc(o_sum, 1)

                def finish_slot(g, u, t, first, last):
                    if t < 2:
                        return proj_lo_part(g - 1, SLOTS[-1], 1 - u, (t,))
                    name = slot(t - 2, first, last)
                    if name and name[0] in "KQ":
                        proj_lo_part(g, name, u, (t % 2,))
                    elif name and t % 2 == 0:
                        add_out(g, name) if name[0] == "O" else proj_lo_part(g, name, u)

                def body(g, u, first, last):
                    for t in range(TILES):
                        for tile in ahead(g, t + LEAD, last):
                            max_tile(*tile)
                        finish_slot(g, u, t, first, last)
                        if t % T == 1:
                            for head in head_before(g, t - 1, first):
                                o_second(*head)
                        for tile in ahead(g, t + LEAD, last):
                            recip(*tile)
                        pt_tile(g, t)

                dve.wait_ge(b_loaded, 48)
                for raw, dst, scale in zip(raw_b, (bks, bqs, bvs), (1.0, float(NB) ** -0.5, 1.0)):
                    halves = dst[:, :].rearrange("p (h b j) -> p h b j", h=HALVES, b=NB)
                    for b in range(NB):
                        nc.vector.tensor_scalar(halves[:, :, b, :], raw[:, :].rearrange("p (h j) -> p h j", h=HALVES),
                                                scale, None, ALU.mult).then_inc(bias_ready, 1)
                dve.wait_ge(bias_ready, 3 * NB)
                for name in AHEAD:
                    if name != AHEAD[-1]:
                        proj_lo_part(-1, name, 1)
                    if name == "V2+":
                        for t in range(2):
                            max_tile(0, t)
                for t in range(2):
                    recip(0, t)
                for t in range(2, LEAD):
                    max_tile(0, t)
                    recip(0, t)
                groups(dve, body)
                o_second(GROUPS - 1, HH - 1)
                for i in range(T):
                    add_out(GROUPS, f"O{i}")

            @block.tensor
            def _(pe):
                def bank_free(g, name, first, before=True):
                    s = SLOTS.index(name) - 2
                    if first and s >= 0 and SLOTS[s][0] == "O":
                        s -= 2
                    if s < 0:
                        g, s = g - 1, s + len(SLOTS)
                    if SLOTS[s][0] == "O":
                        pe.wait_ge(wo_out, T * (g - 1) + int(SLOTS[s][1]) + 1)
                    else:
                        pe.wait_ge(proj_lo, split(g, SLOTS[s]))

                def project(g, name, u, part=0, parts=1):
                    G, j = (g + 1 if name[-1] == "+" else g), int(name[1])
                    out = projp[:, SLOTS.index(name) % 2, :]
                    mms = [(k, s, m) for k in range(K) for s, m in TERMS]
                    lo, hi = part * len(mms) // parts, (part + 1) * len(mms) // parts
                    if part == 0:
                        if name == "V0+":
                            pe.wait_ge(wv_ready, G + 1)
                        if name[0] == "K":
                            pe.wait_ge(wk_loaded, 16 * (PAIRS * G + j + 1))
                        if name[0] == "Q":
                            pe.wait_ge(wq_loaded, 16 * (PAIRS * G + j + 1))
                        if name == "Q0+":
                            pe.wait_ge(x_loaded, 16 * G + 16)
                        if name == "O0":
                            pe.wait_ge(wo_ready, g)
                    for n, (k, s, m) in enumerate(mms[lo:hi], lo):
                        if name == "V0+" and n % len(TERMS) == 0:
                            pe.wait_ge(c_loaded[k], 16 * G + 16)
                        if name[0] == "K":
                            l, r = wk[:, s, k, :], cp[:, k, m, :]
                        elif name[0] == "Q":
                            l, r = wq[:, s, k, :], xp[:, m, k, :]
                        elif name[0] == "V":
                            l, r = cp[:, k, s, j * P:(j + 1) * P], WV[:, m, k, :]
                        else:
                            if j == 0 and n % len(TERMS) == 0:
                                pe.wait_ge(op_lo, PAIRS * (g - 1) + k + 1)
                            l, r = op[:, s, k, j * P:(j + 1) * P], WO[:, m, k, :]
                        ins = nc.tensor.matmul(out, l, r, start=(n == 0), stop=(n == len(mms) - 1))
                    if part == parts - 1:
                        ins.then_inc(wo_mm if name[0] == "O" else proj_mm, 1)

                def scores(g, t):
                    n, i = divmod(t, T)
                    head, j, e = HH * g + n, n // 2, n % 2
                    if i == 0:
                        pe.wait_ge(proj_lo, split(*pair_slot(g, "Q", j), e))
                        pe.wait_ge(k_doubled[e], 16 * (PAIRS * g + j + 1))
                    wait(pe, p_exp, T * head + i - 1)
                    for m in (HI, LO):
                        ins = nc.tensor.matmul(spsum[:, i % 2, :], qs[:, j % 2, e, i * P:(i + 1) * P],
                                               ks[:, j % 2, e, m, :], start=(m == HI), stop=(m == LO))
                    ins.then_inc(s_mm, 1)

                def turn(g, t):
                    n, k = divmod(t, T)
                    head = HH * g + n
                    wait(pe, pt_lo, T * head + k - 1)
                    for i in range(T):
                        if k == 0:
                            pe.wait_ge(p_ready, T * head + i + 1)
                        ins = nc.tensor.transpose(tpsum[:, k % 2, i * P:(i + 1) * P],
                                                  prob[:, n % 2, i, k * P:(k + 1) * P], ident[:, :])
                    ins.then_inc(t_mm, 1)

                def values(g, t, u):
                    n, k = divmod(t, T)
                    head = HH * g + n
                    if k == 0:
                        wait(pe, o_sum, head - 1)
                    if n == 0:
                        pe.wait_ge(proj_lo, split(g, "V3") if k == T - 1 else split(g - 1, f"V{k}+"))
                    pe.wait_ge(pt_lo, T * head + k + 1)
                    for m in (HI, LO):
                        ins = nc.tensor.matmul(opsum[:, n % 2, :], vs[:, u, k, n, :], pt[:, k % 2, m, :],
                                               start=(k == 0 and m == HI), stop=(k == T - 1 and m == LO))
                    ins.then_inc(av_mm, 1)

                def body(g, u, first, last):
                    for t in range(TILES):
                        for tile in ahead(g, t + LEAD, last):
                            scores(*tile)
                        name = slot(t, first, last)
                        if name:
                            if t % 2 == 0:
                                bank_free(g, name, first)
                            project(g, name, u, t % 2, 2)
                        turn(g, t)
                        if t:
                            values(g, t - 1, u)
                        elif not first:
                            values(g - 1, TILES - 1, 1 - u)

                for name in AHEAD:
                    if SLOTS.index(name) >= FIRST_AHEAD + 2:
                        bank_free(-1, name, False)
                    project(-1, name, 1)
                    if name == "V2+":
                        for t in range(2):
                            scores(0, t)
                for t in range(2, LEAD):
                    scores(0, t)
                groups(pe, body)
                values(GROUPS - 1, TILES - 1, 1)
                for i in range(T):
                    if i >= 2:
                        pe.wait_ge(wo_out, T * (GROUPS - 1) + i - 1)
                    project(GROUPS, f"O{i}", 0)


def feed_forward(nc, y_in, WsT, WeT, Wg, bo, bias, ident, out, NB, S, D, NG):
    T, K, RING = S // P, D // P, 2
    SHARED, EXPERT = 0, 1
    PAD = 8
    assert NB % RING == 0 and T == 4 and K == 4 and NG < PAD
    with ExitStack() as ctx:
        sc = Scope(nc, ctx, "f")
        raw = sc.sb("raw", [P, 2, K, D])
        W = sc.sb("W", [P, 2, 2, K, D], F32R)
        graw, G = sc.sb("graw", [P, K, P]), sc.sb("G", [P, 2, K, P], F32R)
        bo_all, bias_all = sc.sb("bo", [P, D]), sc.sb("bias", [P, D])
        x2 = sc.sb("x2", [P, RING, T, D])
        x2T = sc.sb("x2T", [P, RING, 2, K, S], F32R)
        z = sc.sb("z", [P, RING, T, D])
        logitT = sc.sb("logitT", [P, S])
        e = sc.sb("e", [P, T, PAD])
        gneg, den = sc.sb("gneg", [P, T]), sc.sb("den", [P, T])
        best = sc.sb("best", [P, T, PAD])
        total, route, weight = sc.sb("total", [P, T]), sc.sb("route", [P, 2, T]), sc.sb("weight", [P, T])
        prod = sc.ps("prod", [P, RING, 2, D])
        turned = sc.ps("turned", [P, 2, S])
        gateT, logit = sc.ps("gateT", [P, S]), sc.ps("logit", [P, T, P])

        (g_zero, g_loaded, w_hi, w_lo, b_loaded, xb_made, t_mm, x2_hi, x2_lo, gate_mm, gate_out, lt_mm,
         g_max, e_done, e_pad, w_step, w_done, prod_mm, z_mid) = (sc.sem(n) for n in (
             "g_zero", "g_loaded", "w_hi", "w_lo", "b_loaded", "xb_made", "t_mm", "x2_hi", "x2_lo", "gate_mm",
             "gate_out", "lt_mm", "g_max", "e_done", "e_pad", "w_step", "w_done", "prod_mm", "z_mid"))
        ranked, passed = sc.sem("ranked"), sc.sem("passed")
        w_loaded = [sc.sem(f"w_loaded{n}") for n in range(2)]
        y_loaded, z_stored = ([sc.sem(f"{n}{u}") for u in range(RING)] for n in ("y_loaded", "z_stored"))
        WEIGHT_STEPS = 1 + T + 4
        CREDIT = 16
        norm2, norm3 = Norm(sc, T, D, "norm2"), Norm(sc, T, D, "norm3", credit=CREDIT)

        def done(n):
            return n + CREDIT

        def batches(eng, step):
            if NB > RING:
                with eng.Fori(0, NB // RING - 1) as c:
                    for u in range(RING):
                        step(c * RING + u, u, c, RING)
            for u in range(RING):
                step(NB - RING + u, u, NB // RING - 1, RING - 1 - u)

        with nc.Block() as block:

            @block.sync
            def _(sp):
                def load(u, b):
                    sp.dma_start(x2[:, u, :, :], y_in[b].rearrange("(t p) d -> p t d", p=P)).then_inc(y_loaded[u], 16)

                load(0, 0)
                sp.dma_start(bo_all[:, :], bo.partition_broadcast(P)).then_inc(b_loaded, 16)
                sp.wait_ge(g_zero, 1)
                sp.dma_start(graw[:, :, :NG], Wg.rearrange("(k p) n -> p k n", p=P)).then_inc(g_loaded, 16)
                sp.dma_start(bias_all[:, :], bias.partition_broadcast(P)).then_inc(b_loaded, 16)
                for w, src in enumerate((WsT, WeT)):
                    sp.dma_start(raw[:, w, :, :], src.rearrange("(k p) n -> p k n", p=P)).then_inc(w_loaded[w], 16)
                load(1, 1)

                def step(b, u, c, more):
                    if more == RING:
                        sp.wait_ge(t_mm, K * b + K)
                        sp.wait_ge(xb_made, T * b + T)
                        load(u, b + RING)
                    sp.wait_ge(norm3.normed, T * b + T)
                    sp.dma_start(out[b].rearrange("(t p) d -> p t d", p=P), z[:, u, :, :]).then_inc(z_stored[u], 16)

                batches(sp, step)
                for u in range(RING):
                    sp.wait_ge(z_stored[u], done(16 * NB // RING))

            @block.gpsimd
            def _(pool):
                nc.gpsimd.memset(graw[:, :, :], 0.0).then_inc(g_zero, 1)
                for u in range(RING):
                    pool.sem_inc(z_stored[u], CREDIT)

                def add_bo(u, c):
                    pool.wait_ge(y_loaded[u], 16 * c + 16)
                    for i in range(T):
                        nc.gpsimd.tensor_tensor(x2[:, u, i, :], x2[:, u, i, :], bo_all[:, :],
                                                ALU.add).then_inc(norm2.summed, 1)

                def add_bias(b, u, c):
                    pool.wait_ge(norm2.normed, T * b + T)
                    pool.wait_ge(z_stored[u], 16 * c + CREDIT)
                    for i in range(T):
                        nc.gpsimd.tensor_tensor(z[:, u, i, :], x2[:, u, i, :], bias_all[:, :],
                                                ALU.add).then_inc(xb_made, 1)

                pool.wait_ge(b_loaded, 32)
                add_bo(0, 0)
                add_bias(0, 0, 0)
                add_bo(1, 0)

                def step(b, u, c, more):
                    if more:
                        add_bias(b + 1, (u + 1) % RING, c + (u + 1) // RING)
                    if more == RING:
                        add_bo(u, c + 1)

                batches(pool, step)

            @block.scalar
            def _(act):
                act.sem_inc(e_done, CREDIT)
                act.sem_inc(gate_out, CREDIT)

                def turn_hi(b, u):
                    for k in range(K):
                        act.wait_ge(t_mm, K * b + k + 1)
                        act.wait_ge(prod_mm, done(T * b - T))
                        nc.scalar.copy(x2T[:, u, HI, k, :], turned[:, k % 2, :]).then_inc(x2_hi, 1)

                def gate_copy(b):
                    act.wait_ge(gate_mm, b + 1)
                    act.wait_ge(lt_mm, done(b))
                    nc.scalar.copy(logitT[:, :], gateT[:, :]).then_inc(gate_out, 1)

                for w in range(2):
                    act.wait_ge(w_loaded[w], 16)
                    for k in range(K):
                        nc.scalar.copy(W[:, w, HI, k, :], raw[:, w, k, :]).then_inc(w_hi, 1)
                    if w == 0:
                        act.wait_ge(g_loaded, 16)
                        nc.scalar.copy(G[:, HI, :, :], graw[:, :, :]).then_inc(w_hi, 1)
                norm2.root(nc, 0)
                turn_hi(0, 0)
                gate_copy(0)

                def step(b, u, c, more):
                    act.wait_ge(g_max, b + 1)
                    act.wait_ge(w_done, done(b))
                    for i in range(T):
                        nc.scalar.activation(e[:, i, :NG], logit[:, i, :NG], ACT.Exp, bias=gneg[:, i:i + 1], scale=1.0,
                                             accum_out=den[:, i:i + 1]).then_inc(e_done, 1)
                    if more:
                        norm2.root(nc, b + 1)
                        turn_hi(b + 1, (u + 1) % RING)
                        gate_copy(b + 1)
                    norm3.root(nc, b)

                batches(act, step)

            @block.vector
            def _(dve):
                for s in (x2_lo, w_done, norm3.summed):
                    dve.sem_inc(s, CREDIT)
                nc.vector.memset(e[:, :, :], 0.0).then_inc(e_pad, 1)
                dve.wait_ge(e_pad, 1)
                v = nc.vector

                def turn_lo(b, u):
                    for k in range(K):
                        dve.wait_ge(x2_hi, K * b + k + 1)
                        v.tensor_tensor(x2T[:, u, LO, k, :], turned[:, k % 2, :], as_f32(x2T[:, u, HI, k, :]),
                                        ALU.subtract).then_inc(x2_lo, 1)

                def gate_max(b):
                    dve.wait_ge(lt_mm, done(b + 1))
                    v.tensor_reduce(gneg[:, :], logit[:, :, :NG], AX.X, ALU.max, negate=True).then_inc(g_max, 1)

                def route_weights(b):
                    count = [WEIGHT_STEPS * b]

                    def link(ins):
                        count[0] = count[0] + 1
                        ins.then_inc(w_step, 1)
                        dve.wait_ge(w_step, count[0])

                    dve.wait_ge(e_done, done(T * b + T))
                    link(v.reciprocal(den[:, :], den[:, :]))
                    for i in range(T):
                        link(v.tensor_scalar(e[:, i, :NG], e[:, i, :NG], den[:, i:i + 1], None, ALU.mult))
                    dve.sem_inc(passed, 1)
                    for i in range(T):
                        v.max(best[:, i, :], e[:, i, :]).then_inc(ranked, 1)
                    dve.wait_ge(ranked, T * b + T)
                    link(v.tensor_tensor(total[:, :], best[:, :, 0], best[:, :, 1], ALU.add))
                    link(v.reciprocal(total[:, :], total[:, :]))
                    for r in range(2):
                        link(v.tensor_tensor(route[:, r, :], best[:, :, r], total[:, :], ALU.mult))
                    v.tensor_tensor(weight[:, :], route[:, 0, :], route[:, 1, :], ALU.add).then_inc(w_done, 1)

                def finish_tile(b, u, i):
                    dve.wait_ge(prod_mm, done(T * b + i + 1))
                    dve.wait_ge(xb_made, T * b + i + 1)
                    if i == 0:
                        dve.wait_ge(w_done, done(b + 1))
                    v.scalar_tensor_tensor(out=z[:, u, i, :], in0=prod[:, i % RING, EXPERT, :], scalar=weight[:, i:i + 1],
                                           in1=z[:, u, i, :], op0=ALU.mult, op1=ALU.add).then_inc(z_mid, 1)
                    dve.wait_ge(z_mid, T * b + i + 1)
                    v.tensor_tensor(z[:, u, i, :], prod[:, i % RING, SHARED, :], z[:, u, i, :],
                                    ALU.add).then_inc(norm3.summed, 1)
                    norm3.stats(nc, b, i, z[:, u])

                for i in range(T):
                    norm2.stats(nc, 0, i, x2[:, 0])
                norm2.variance(nc, 0)
                for n in range(2):
                    for k in range(K):
                        dve.wait_ge(w_hi, (K + 1) * n + k + 1)
                        v.tensor_tensor(W[:, n, LO, k, :], raw[:, n, k, :], as_f32(W[:, n, HI, k, :]),
                                        ALU.subtract).then_inc(w_lo, 1)
                    if n == 0:
                        dve.wait_ge(w_hi, K + 1)
                        v.tensor_tensor(G[:, LO, :, :], graw[:, :, :], as_f32(G[:, HI, :, :]),
                                        ALU.subtract).then_inc(w_lo, 1)
                norm2.scale(nc, 0, x2[:, 0], x2[:, 0])
                turn_lo(0, 0)

                def step(b, u, c, more):
                    nu = (u + 1) % RING
                    if more:
                        for i in range(T):
                            norm2.stats(nc, b + 1, i, x2[:, nu])
                    gate_max(b)
                    if more:
                        norm2.variance(nc, b + 1)
                    route_weights(b)
                    finish_tile(b, u, 0)
                    if more:
                        norm2.scale(nc, b + 1, x2[:, nu], x2[:, nu])
                    finish_tile(b, u, 1)
                    finish_tile(b, u, 2)
                    if more:
                        turn_lo(b + 1, nu)
                    finish_tile(b, u, 3)
                    norm3.variance(nc, b)
                    norm3.scale(nc, b, z[:, u], z[:, u])

                batches(dve, step)

            @block.tensor
            def _(pe):
                pe.sem_inc(lt_mm, CREDIT)
                pe.sem_inc(prod_mm, CREDIT)

                def turn(b, u, ks):
                    pe.wait_ge(norm2.normed, T * b + T)
                    for k in ks:
                        pe.wait_ge(x2_lo, done(K * b + k - 1))
                        for i in range(T):
                            t = nc.tensor.transpose(turned[:, k % 2, i * P:(i + 1) * P], x2[:, u, i, k * P:(k + 1) * P],
                                                    ident[:, :])
                        t.then_inc(t_mm, 1)

                def gate(b, u):
                    pe.wait_ge(x2_lo, done(K * b + K))
                    pe.wait_ge(gate_out, done(b))
                    three_pass(nc, gateT[:, :], lambda s, k: G[:, s, k, :], lambda m, k: x2T[:, u, m, k, :],
                               K).then_inc(gate_mm, 1)

                def turn_logits(b):
                    pe.wait_ge(gate_out, done(b + 1))
                    pe.wait_ge(e_done, done(T * b))
                    for i in range(T):
                        t = nc.tensor.transpose(logit[:, i, :], logitT[:, i * P:(i + 1) * P], ident[:, :])
                    t.then_inc(lt_mm, 1)

                def product(b, u, i, which):
                    if which == SHARED:
                        pe.wait_ge(norm3.summed, done(T * b + i - 1))
                    return three_pass(nc, prod[:, i % RING, which, :], lambda s, k: x2T[:, u, s, k, i * P:(i + 1) * P],
                                      lambda m, k: W[:, which, m, k, :], K)

                turn(0, 0, range(K))
                pe.wait_ge(w_lo, 2 * K + 1)
                gate(0, 0)

                def step(b, u, c, more):
                    nu = (u + 1) % RING
                    product(b, u, 0, SHARED)
                    turn_logits(b)
                    product(b, u, 0, EXPERT).then_inc(prod_mm, 1)
                    for i in (1, 2):
                        product(b, u, i, SHARED)
                        product(b, u, i, EXPERT).then_inc(prod_mm, 1)
                    if more:
                        turn(b + 1, nu, range(0, 2))
                    product(b, u, 3, SHARED)
                    if more:
                        turn(b + 1, nu, range(2, K))
                    product(b, u, 3, EXPERT).then_inc(prod_mm, 1)
                    if more:
                        gate(b + 1, nu)

                batches(pe, step)


def decoder_layer(nc, x, xT, ctxT, wqT, wkT, wv, wpair, bq, bk, bv, bo, WsT, WeT, Wg, bias, out):
    NB, S, D = x.shape
    NPAIR, (DK, H) = wpair.shape[0], bv.shape
    y_steps = nc.dram_tensor("y_steps_scratch", [3 * NB, S, D], F32).ap()
    xparts, cparts = (nc.dram_tensor(f"{n}_scratch", [NB, P, 2 * (D // P) * S], F32).ap() for n in ("x1T", "ctxT"))
    wparts = [nc.dram_tensor(f"{n}_scratch", [NPAIR, P, 2 * D], F32).ap() for n in ("wq", "wk", "wv", "wo")]
    with ExitStack() as ctx:
        sc = Scope(nc, ctx, "all")
        ident = sc.sb("ident", [P, P])
        made = sc.sem("ident_made")
        with nc.Block() as block:
            @block.gpsimd
            def _(pool):
                nc.gpsimd.memset(ident[:, :], 0.0).then_inc(made, 1)
                pool.wait_ge(made, 1)
                nc.gpsimd.affine_select(out=ident[:, :], in_=ident[:, :], compare_op=ALU.not_equal, fill=1.0, base=0,
                                        pattern=[[-1, P]], channel_multiplier=1).then_inc(made, 1)
        with ExitStack() as first_half:
            sa = Scope(nc, first_half, "sw")
            A, WV = sa.sb("A", [P, 2, D // P, D], F32R), sa.sb("WV", [P, 2, D // P, D], F32R)
            load_weights(nc, wqT, wkT, wv, A, WV, D)
            self_attention(nc, x, xT, ctxT, wpair, A, WV, ident, y_steps, xparts, cparts, wparts, NB, S, D, float(NB) ** -0.5)
        cross_attention(nc, y_steps, xparts, cparts, *wparts, bq, bk, bv, ident, NB, S, D, H, DK)
        feed_forward(nc, y_steps[2 * NB:3 * NB], WsT, WeT, Wg, bo, bias, ident, out, NB, S, D, Wg.shape[1])


def kernel(x, ctx_1024, L0_attn_W, L0_xattn_Wq, L0_xattn_bq, L0_xattn_Wk, L0_xattn_bk, L0_xattn_Wv, L0_xattn_bv,
           L0_xattn_Wo, L0_xattn_bo, L0_ffn_cond, L0_ffn_mask, L0_ffn_W_shared, L0_ffn_W_expert, L0_ffn_W_gate,
           L0_ffn_bias):
    import numpy as np
    import concourse.bacc as bacc
    from concourse.bass_utils import run_bass_kernel_spmd

    D, H, DK = x.shape[2], 16, 64
    K, PAIRS = D // P, H * DK // P

    def pair_columns(w):
        return w.reshape(K, P, PAIRS, P).transpose(2, 1, 0, 3).reshape(PAIRS, P, K * P)

    W, Wq, Wk, Wv, Wo = (np.asarray(a) for a in (L0_attn_W, L0_xattn_Wq, L0_xattn_Wk, L0_xattn_Wv, L0_xattn_Wo))
    halves = Wv.reshape(K, P, 2, Wv.shape[1] // 2).transpose(2, 0, 1, 3).reshape(PAIRS, P, Wv.shape[1] // 2)
    arrays = {
        "x": np.asarray(x), "xT": np.asarray(x).transpose(0, 2, 1), "ctxT": np.asarray(ctx_1024).transpose(0, 2, 1),
        "wqT": W[:, :D].T, "wkT": W[:, D:2 * D].T, "wv": W[:, 2 * D:],
        "wpair": np.stack([pair_columns(Wq), pair_columns(Wk), halves, Wo.reshape(PAIRS, P, D)], axis=1),
        "bq": np.asarray(L0_xattn_bq).reshape(PAIRS, P).T, "bk": np.asarray(L0_xattn_bk).reshape(PAIRS, P).T,
        "bv": np.asarray(L0_xattn_bv).reshape(H, DK).T, "bo": np.asarray(L0_xattn_bo).reshape(1, D),
        "WsT": np.asarray(L0_ffn_W_shared).T, "WeT": np.asarray(L0_ffn_W_expert).T,
        "Wg": np.asarray(L0_ffn_W_gate), "bias": np.asarray(L0_ffn_bias).reshape(1, D)}
    arrays = {f"in_{name}": np.ascontiguousarray(a) for name, a in arrays.items()}
    nc = bacc.Bacc("TRN2", target_bir_lowering=False, num_devices=1)
    args = [nc.dram_tensor(name, a.shape, mybir.dt.from_np(a.dtype), kind="ExternalInput").ap()
            for name, a in arrays.items()]
    args.append(nc.dram_tensor("out", x.shape, F32, kind="ExternalOutput").ap())
    decoder_layer(nc, *args)
    return run_bass_kernel_spmd(nc, [arrays], core_ids=[0]).results[0]["out"]
```

```python
from contextlib import ExitStack

import concourse.bass as bass
from concourse import mybir

F32 = mybir.dt.float32
F32R = mybir.dt.float32r
ALU = mybir.AluOpType
ACT = mybir.ActivationFunctionType
AX = mybir.AxisListType

P = 128
HI, LO = 0, 1
EPS = 1e-5
NEG = 9000000000000000.0
TERMS = ((HI, HI), (HI, LO), (LO, HI))


class Scope:

    def __init__(self, nc, ctx, stage):
        self.nc, self.ctx, self.stage = nc, ctx, stage

    def sb(self, name, shape, dt=F32):
        return self.ctx.enter_context(self.nc.sbuf_tensor(f"{self.stage}_{name}", shape, dt))

    def ps(self, name, shape):
        return self.ctx.enter_context(self.nc.psum_tensor(f"{self.stage}_{name}", shape, F32))

    def sem(self, name):
        return self.ctx.enter_context(self.nc.semaphore(f"{self.stage}_{name}"))


def as_f32(ap):
    return ap.bitcast(F32)


def three_pass(nc, out, stationary, moving, depth):
    last = (depth - 1, TERMS[-1])
    for k in range(depth):
        for s, m in TERMS:
            ins = nc.tensor.matmul(out, stationary(s, k), moving(m, k), start=(k == 0 and s == m == HI),
                                   stop=((k, (s, m)) == last))
    return ins


class Norm:

    def __init__(self, sc, T, D, name="norm", credit=0):
        self.T, self.D, self.credit = T, D, credit
        self.stat = sc.sb(f"{name}_stat", [P, T, 6])
        self.mean, self.var, self.std = (sc.sb(f"{name}_{n}", [P, T]) for n in ("mean", "variance", "std"))
        self.r, self.t, self.u = (sc.sb(f"{name}_{n}", [P, T]) for n in ("r", "t", "u"))
        self.summed, self.have_stat, self.step, self.have_var, self.have_std, self.normed, self.passed = (
            sc.sem(f"{name}_{n}") for n in ("summed", "have_stat", "step", "have_var", "have_std", "normed", "passed"))

    def link(self, nc, count, ins):
        count[0] = count[0] + 1
        ins.then_inc(self.step, 1)
        nc.vector.wait_ge(self.step, count[0])

    VARIANCE_STEPS, STEPS = 6, 11

    def stats(self, nc, b, i, y):
        nc.vector.wait_ge(self.summed, self.T * b + i + 1 + self.credit)
        nc.vector.bn_stats(self.stat[:, i, :], y[:, i, :]).then_inc(self.have_stat, 1)

    def variance(self, nc, b):
        v, st, n = nc.vector, self.stat, [self.STEPS * b]
        v.wait_ge(self.have_stat, self.T * b + self.T)
        self.link(nc, n, v.tensor_tensor(self.mean[:, :], st[:, :, 1], st[:, :, 4], ALU.add))
        self.link(nc, n, v.tensor_scalar(self.mean[:, :], self.mean[:, :], 0.5, None, ALU.mult))
        self.link(nc, n, v.tensor_tensor(self.t[:, :], st[:, :, 1], st[:, :, 4], ALU.subtract))
        self.link(nc, n, v.tensor_tensor(self.t[:, :], self.t[:, :], self.t[:, :], ALU.mult))
        self.link(nc, n, v.tensor_tensor(self.u[:, :], st[:, :, 2], st[:, :, 5], ALU.add))
        self.link(nc, n, v.tensor_scalar(self.u[:, :], self.u[:, :], 1.0 / self.D, EPS, ALU.mult, ALU.add))
        v.scalar_tensor_tensor(out=self.var[:, :], in0=self.t[:, :], scalar=0.25, in1=self.u[:, :], op0=ALU.mult,
                               op1=ALU.add).then_inc(self.have_var, 1)

    def root(self, nc, b):
        nc.scalar.wait_ge(self.have_var, b + 1)
        nc.scalar.activation(self.std[:, :], self.var[:, :], ACT.Sqrt).then_inc(self.have_std, 1)

    def inverse(self, nc, b):
        v, n = nc.vector, [self.STEPS * b + self.VARIANCE_STEPS]
        v.wait_ge(self.have_std, b + 1)
        self.link(nc, n, v.reciprocal(self.r[:, :], self.std[:, :]))
        self.link(nc, n, v.tensor_tensor(self.t[:, :], self.r[:, :], self.r[:, :], ALU.mult))
        self.link(nc, n, v.tensor_tensor(self.t[:, :], self.t[:, :], self.var[:, :], ALU.mult))
        self.link(nc, n, v.tensor_scalar(self.t[:, :], self.t[:, :], -0.5, 1.5, ALU.mult, ALU.add))
        self.link(nc, n, v.tensor_tensor(self.r[:, :], self.r[:, :], self.t[:, :], ALU.mult))

    def scale_on_pool(self, nc, b, y):
        nc.gpsimd.wait_ge(self.step, self.STEPS * b + self.STEPS)
        nc.gpsimd.sem_inc(self.passed, 1)
        for i in range(self.T):
            nc.gpsimd.tensor_scalar(y[:, i, :], y[:, i, :], self.mean[:, i:i + 1], self.r[:, i:i + 1], ALU.subtract,
                                    ALU.mult).then_inc(self.normed, 1)

    def scale(self, nc, out, y):
        v = nc.vector
        for i in range(self.T):
            v.tensor_scalar(out[:, i, :], y[:, i, :], self.mean[:, i:i + 1], self.r[:, i:i + 1], ALU.subtract,
                            ALU.mult).then_inc(self.normed, 1)


class Held:

    def __init__(self, sc, D):
        self.first, self.second, self.third = (sc.sb(f"{n}_buffer", [P, 2, 4, 512], F32R)
                                               for n in ("first", "second", "third"))
        self.wv_loaded, self.c_loaded = sc.sem("wv_loaded"), [sc.sem(f"c_loaded{k}") for k in range(D // P)]
        self.x_loaded = sc.sem("x1T_loaded")

    def begin_x2(self, sc, T, D):
        self.x2, self.bo = sc.sb("x2", [P, 2, T, D]), sc.sb("bo", [P, D])
        self.bo_loaded, self.ws_loaded, self.ws_hi, self.ws_lo = (sc.sem(n) for n in (
            "bo_loaded", "ws_loaded", "ws_hi", "ws_lo"))
        self.y_loaded = [sc.sem(f"y2_loaded{u}") for u in range(2)]
        self.norm2 = Norm(sc, T, D, "norm2")


def add_bo(nc, held, u, c):
    x2, T = held.x2[:, u, :, :], held.norm2.T
    nc.gpsimd.wait_ge(held.y_loaded[u], 16 * c + 16)
    for i in range(T):
        nc.gpsimd.tensor_tensor(x2[:, i, :], x2[:, i, :], held.bo[:, :], ALU.add).then_inc(held.norm2.summed, 1)


def load_ctx(sp, held, cparts, b):
    for k, loaded in enumerate(held.c_loaded):
        n = 2 * held.second.shape[-1]
        sp.dma_start(as_f32(held.second[:, :, k, :]),
                     cparts[b, :, k * n:(k + 1) * n].rearrange("p (a n) -> p a n", a=2)).then_inc(loaded, 16)


def load_half(sp, dst, parts, h, loaded):
    pieces = dst.shape[2]
    for k in range(pieces):
        sp.dma_start(as_f32(dst[:, :, k, :]),
                     parts[h * pieces + k].rearrange("p (a n) -> p a n", a=2)).then_inc(loaded, 16)


def load_weights(nc, wqT, wkT, wv, xT, A, WV, xraw, xp, xT_loaded, x_hi, x_lo, D):
    T, K = D // P, xp.shape[2]
    with ExitStack() as ctx:
        sc = Scope(nc, ctx, "w")
        raw = sc.sb("raw", [P, 3, T, D])
        part = sc.sb("part", [P, 2, 2, T, D], F32R)
        pa = sc.ps("a", [P, T, D])
        loaded = [[sc.sem(f"loaded{w}{k}") for k in range(T)] for w in range(2)]
        (v_loaded, hi_done, lo_done, v_hi, v_lo, a_mm, a_hi, a_lo) = (sc.sem(n) for n in (
            "v_loaded", "hi_done", "lo_done", "v_hi", "v_lo", "a_mm", "a_hi", "a_lo"))

        with nc.Block() as block:

            @block.sync
            def _(sp):
                for k in range(T):
                    for w, src in enumerate((wqT, wkT)):
                        sp.dma_start(raw[:, w, k, :], src[k * P:(k + 1) * P, :]).then_inc(loaded[w][k], 16)
                sp.dma_start(xraw[:, :, :], xT[0].rearrange("(k p) n -> p k n", p=P)).then_inc(xT_loaded, 16)
                sp.dma_start(raw[:, 2, :, :], wv.rearrange("(k p) n -> p k n", p=P)).then_inc(v_loaded, 16)

            @block.scalar
            def _(act):
                for k in range(T):
                    for w in range(2):
                        act.wait_ge(loaded[w][k], 16)
                        nc.scalar.copy(part[:, w, HI, k, :], raw[:, w, k, :]).then_inc(hi_done, 1)
                act.wait_ge(xT_loaded, 16)
                for k in range(K):
                    nc.scalar.copy(xp[:, HI, k, :], xraw[:, k, :]).then_inc(x_hi, 1)
                for m in range(T):
                    act.wait_ge(a_mm, m + 1)
                    nc.scalar.activation(A[:, HI, m, :], pa[:, m, :], ACT.Copy,
                                         scale=float(D) ** -0.5).then_inc(a_hi, 1)
                act.wait_ge(v_loaded, 16)
                for k in range(T):
                    nc.scalar.copy(WV[:, HI, k, :], raw[:, 2, k, :]).then_inc(v_hi, 1)

            @block.vector
            def _(dve):
                for k in range(T):
                    for w in range(2):
                        dve.wait_ge(hi_done, 2 * k + w + 1)
                        nc.vector.tensor_tensor(part[:, w, LO, k, :], raw[:, w, k, :], as_f32(part[:, w, HI, k, :]),
                                                ALU.subtract).then_inc(lo_done, 1)
                for k in range(K):
                    dve.wait_ge(x_hi, k + 1)
                    nc.vector.tensor_tensor(xp[:, LO, k, :], xraw[:, k, :], as_f32(xp[:, HI, k, :]),
                                            ALU.subtract).then_inc(x_lo, 1)
                for m in range(T):
                    dve.wait_ge(a_hi, m + 1)
                    nc.vector.scalar_tensor_tensor(out=A[:, LO, m, :], in0=pa[:, m, :], scalar=float(D) ** -0.5,
                                                   in1=as_f32(A[:, HI, m, :]), op0=ALU.mult,
                                                   op1=ALU.subtract).then_inc(a_lo, 1)
                for k in range(T):
                    dve.wait_ge(v_hi, k + 1)
                    nc.vector.tensor_tensor(WV[:, LO, k, :], raw[:, 2, k, :], as_f32(WV[:, HI, k, :]),
                                            ALU.subtract).then_inc(v_lo, 1)

            @block.tensor
            def _(pe):
                for k in range(T):
                    pe.wait_ge(lo_done, 2 * k + 2)
                    for m in range(T):
                        for s, r in TERMS:
                            ins = nc.tensor.matmul(pa[:, m, :], part[:, 0, s, k, m * P:(m + 1) * P],
                                                   part[:, 1, r, k, :], start=(k == 0 and s == r == HI),
                                                   stop=(k == T - 1 and (s, r) == TERMS[-1]))
                        if k == T - 1:
                            ins.then_inc(a_mm, 1)


def self_attention(nc, x, xT, ctxT, wpair, held, xraw, xT_loaded, x_hi, x_lo, ident, x1, xparts, cparts, wparts,
                   NB, S, D, QSCALE):
    T, K = S // P, D // P
    with ExitStack() as ctx:
        sc = Scope(nc, ctx, "s")
        A, WV, xp = held.first, held.second, held.third
        qp = sc.sb("qp", [P, 2, K, S], F32R)
        vp = sc.sb("vp", [P, 2, T, D], F32R)
        y = sc.sb("y", [P, T, D])
        x1t = sc.sb("x1t", [P, 2, K, S], F32R)
        strip = sc.sb("strip", [P, (2 * T - 1) * P])
        upper = sc.sb("upper", [P, T, S])
        ms = sc.sb("ms", [P, T, S])
        gone = sc.sb("gone", [P, T, S])
        prob = sc.sb("prob", [P, T, S])
        pt = sc.sb("pt", [P, 2, T, S], F32R)
        negmax, den, rden = sc.sb("negmax", [P, T]), sc.sb("den", [P, T]), sc.sb("rden", [P, T])
        NWP = len(wparts)
        assert K == NWP and D == S
        wraw = sc.sb("wraw", [P, NWP, D])
        wsp = sc.sb("wsp", [P, NWP, 2, D], F32R)
        proj, spsum = sc.ps("proj", [P, 2, 512]), sc.ps("score", [P, 2, 512])
        tpsum, opsum = sc.ps("turned", [P, 2, 512]), sc.ps("av", [P, 2, 512])
        ones = sc.sb("ones", [P, P], F32R)
        norm = Norm(sc, T, D)
        left_sum = sc.sb("left_sum", [P, D])
        ones_made, sum_mm, sum_copied, sum_added, lower = (sc.sem(n) for n in (
            "ones_made", "sum_mm", "sum_copied", "sum_added", "lower"))
        passed = sc.sem("passed")

        (x_loaded, q_mm, q_hi, q_lo, s_mm, v_mm, v_hi, v_lo, t_mm, pt_hi, pt_lo, av_mm,
         x1t_mm, x1t_hi, x1t_out, strip_step, cut, is_zero, masked, prob_exp, have_rden, prob_ready, y_stored,
         x1t_stored, base, w_loaded, w_scaled, w_hi, w_lo, w_stored, c_stored) = (sc.sem(n) for n in (
             "x_loaded", "q_mm", "q_hi", "q_lo", "s_mm", "v_mm", "v_hi", "v_lo",
             "t_mm", "pt_hi", "pt_lo", "av_mm", "x1t_mm", "x1t_hi", "x1t_out", "strip_step", "cut", "is_zero", "masked",
             "prob_exp", "have_rden", "prob_ready", "y_stored", "x1t_stored", "base", "w_loaded", "w_scaled",
             "w_hi", "w_lo", "w_stored", "c_stored"))

        Q_ORDER = ["q0", "q1", "q2", "x0", "x1", "q3", "x2", "x3"]
        V_ORDER = ["v0", "v1", "v2", "s0", "s1", "p0", "p1", "s2", "v3", "p2", "p3"]
        V_ORDER_DVE = ["v0", "v1", "v2", "p0", "p1", "s0", "s1", "s2", "v3", "p2", "p3"]
        assert T == 4 and K == 4

        def weights_round(b, first):
            return 0 if first else b * 2 + 1

        def batches(eng, body):
            body(0, True, False)
            with eng.Fori(1, NB - 1) as b:
                body(b, False, False)
            body(NB - 1, False, True)

        with nc.Block() as block:

            @block.sync
            def _(sp):
                def load_xT(b):
                    sp.dma_start(xraw[:, :, :], xT[b].rearrange("(k p) n -> p k n", p=P)).then_inc(xT_loaded, 16)

                def store_x1T(b):
                    sp.wait_ge(x1t_out, K * b + K)
                    sp.dma_start(xparts[b], as_f32(x1t[:, :, :, :])).then_inc(x1t_stored, 16)

                def store_last_x1T():
                    b, dst = NB - 1, xparts[NB - 1].rearrange("p (a k n) -> p a k n", a=2, k=K)
                    for k in range(K):
                        sp.wait_ge(x1t_out, K * b + k + 1)
                        sp.dma_start(dst[:, :, k, :], as_f32(x1t[:, :, k, :])).then_inc(x1t_stored, 16)

                def load_ctx_round(b):
                    sp.dma_start(wraw[:, :, :], ctxT[b].rearrange("(k p) n -> p k n", p=P)).then_inc(w_loaded, 16)

                def store_ctx(b, n):
                    sp.wait_ge(w_lo, NWP * (n + 1))
                    sp.dma_start(cparts[b], as_f32(wsp[:, :, :, :])).then_inc(c_stored, 16)

                def body(b, first, last):
                    if not last:
                        sp.wait_ge(x_lo, K * b + K)
                        load_xT(b + 1)
                    if not first:
                        sp.wait_ge(y_stored, 16 * b)
                        sp.wait_ge(x1t_mm, K * b)
                    sp.dma_start(y[:, :, :], x[b].rearrange("(t p) d -> p t d", p=P)).then_inc(x_loaded, 16)
                    if not first:
                        store_ctx(b - 1, 2 * b)
                    sp.dma_start(wraw[:, :, :], wpair[b].rearrange("w p n -> p w n")).then_inc(w_loaded, 16)
                    if not first:
                        store_x1T(b - 1)
                    if last:
                        sp.wait_ge(w_stored, 16 * NWP * b)
                        sp.wait_ge(q_mm, K * b + K)
                        load_half(sp, held.first, wparts[2], 0, held.wv_loaded)
                    for w, dst in enumerate(wparts):
                        sp.wait_ge(w_lo, NWP * weights_round(b, first) + w + 1)
                        sp.dma_start(dst[b], as_f32(wsp[:, w, :, :])).then_inc(w_stored, 16)
                    if first:
                        load_ctx_round(NB - 1)
                        store_ctx(NB - 1, 1)
                    if not last:
                        load_ctx_round(b)
                    if last:
                        sp.wait_ge(c_stored, 16 * NB)
                        sp.wait_ge(v_mm, T * b + T)
                        load_ctx(sp, held, cparts, 0)
                        sp.wait_ge(x1t_stored, 16 * b + 16)
                    sp.wait_ge(norm.normed, T * b + T)
                    sp.dma_start(x1[b].rearrange("(t p) d -> p t d", p=P), y[:, :, :]).then_inc(y_stored, 16)

                batches(sp, body)
                store_last_x1T()
                sp.dma_start(as_f32(held.third[:, :, :, :]), xparts[0]).then_inc(held.x_loaded, 16)
                sp.wait_ge(y_stored, 16 * NB)
                sp.wait_ge(x1t_stored, 16 * (NB - 1 + K) + 16)
                sp.wait_ge(w_stored, 16 * NWP * NB)
                sp.wait_ge(c_stored, 16 * NB)

            @block.gpsimd
            def _(pool):
                nc.gpsimd.memset(strip[:, :(T - 1) * P], 0.0).then_inc(strip_step, 1)
                nc.gpsimd.memset(strip[:, (T - 1) * P:], 1.0).then_inc(strip_step, 1)
                pool.wait_ge(strip_step, 2)
                tri = strip[:, (T - 1) * P:T * P]
                nc.gpsimd.affine_select(out=tri, in_=tri, compare_op=ALU.is_ge, fill=0.0, base=0, pattern=[[1, P]],
                                        channel_multiplier=-1).then_inc(strip_step, 1)

                def split_round(n, free, stored):
                    if free is not None:
                        pool.wait_ge(stored, free)
                    for w in range(NWP):
                        pool.sem_inc(passed, 1)
                        nc.gpsimd.tensor_scalar(wsp[:, w, HI, :], wraw[:, w, :], 1.0, 1.0, ALU.mult,
                                                ALU.mult).then_inc(w_hi, 1)
                        pool.wait_ge(w_hi, NWP * n + w + 1)
                        nc.gpsimd.tensor_tensor(wsp[:, w, LO, :], wraw[:, w, :], as_f32(wsp[:, w, HI, :]),
                                                ALU.subtract).then_inc(w_lo, 1)

                def body(b, first, last):
                    for i in range(T):
                        pool.wait_ge(have_rden, T * b + i + 1)
                        pool.sem_inc(passed, 1)
                        nc.gpsimd.tensor_scalar(prob[:, i, :], prob[:, i, :], rden[:, i:i + 1], 1.0, ALU.mult,
                                                ALU.mult).then_inc(prob_ready, 1)
                    n = weights_round(b, first)
                    pool.wait_ge(w_loaded, 16 * (n + 1))
                    pool.sem_inc(passed, 1)
                    nc.gpsimd.tensor_scalar(wraw[:, 0, :], wraw[:, 0, :], QSCALE, 1.0, ALU.mult,
                                            ALU.mult).then_inc(w_scaled, 1)
                    pool.wait_ge(w_scaled, b + 1)
                    split_round(n, None if first else 16 * (b + 1), c_stored)
                    if first:
                        pool.wait_ge(w_loaded, 32)
                        split_round(1, 16 * NWP, w_stored)
                        pool.wait_ge(w_loaded, 48)
                        split_round(2, 16, c_stored)
                    elif not last:
                        pool.wait_ge(w_loaded, 16 * (n + 2))
                        split_round(n + 1, 16 * NWP * (b + 1), w_stored)

                batches(pool, body)

            @block.scalar
            def _(act):
                act.sem_inc(x1t_stored, 16)

                def x1_tile(b, k):
                    act.wait_ge(x1t_mm, K * b + k + 1)
                    act.wait_ge(x1t_stored, 16 * b + 16)
                    nc.scalar.copy(x1t[:, HI, k, :], tpsum[:, k % 2, :]).then_inc(x1t_hi, 1)

                def split_x(b):
                    act.wait_ge(xT_loaded, 16 * b + 16)
                    act.wait_ge(s_mm, T * b)
                    act.wait_ge(v_mm, T * b)
                    for k in range(K):
                        nc.scalar.copy(xp[:, HI, k, :], xraw[:, k, :]).then_inc(x_hi, 1)

                def body(b, first, last):
                    for kind, m in Q_ORDER:
                        m = int(m)
                        if kind == "q":
                            act.wait_ge(q_mm, K * b + m + 1)
                            nc.scalar.copy(qp[:, HI, m, :], proj[:, m % 2, :]).then_inc(q_hi, 1)
                        elif not first:
                            x1_tile(b - 1, m)
                    for i in range(T):
                        act.wait_ge(masked, T * b + i + 1)
                        if not first:
                            act.wait_ge(t_mm, T * b)
                            act.wait_ge(lower, (T - 1) * b)
                        nc.scalar.activation(prob[:, i, :], ms[:, i, :], ACT.Exp, bias=negmax[:, i:i + 1], scale=-1.0,
                                             accum_out=den[:, i:i + 1]).then_inc(prob_exp, 1)
                    for kind, i in V_ORDER:
                        i = int(i)
                        if kind == "v":
                            act.wait_ge(v_mm, T * b + i + 1)
                            if not first:
                                act.wait_ge(av_mm, T * b)
                            nc.scalar.copy(vp[:, HI, i, :], proj[:, i % 2, :]).then_inc(v_hi, 1)
                        elif i == 0 and kind == "s":
                            act.wait_ge(sum_mm, (T - 1) * b + 1)
                            nc.scalar.copy(left_sum[:, :], spsum[:, 0, :]).then_inc(sum_copied, 1)
                        elif kind == "p":
                            n = (i + 1) * P
                            act.wait_ge(t_mm, T * b + i + 1)
                            nc.scalar.copy(pt[:, HI, i, :n], tpsum[:, i % 2, :n]).then_inc(pt_hi, 1)
                    if not last:
                        split_x(b + 1)
                    norm.root(nc, b)

                batches(act, body)
                for k in range(K):
                    x1_tile(NB - 1, k)

            @block.vector
            def _(dve):
                dve.wait_ge(strip_step, 3)
                nc.vector.tensor_copy(ones[:, :], strip[:, T * P:(T + 1) * P]).then_inc(ones_made, 1)
                for i in range(1, T):
                    nc.vector.memset(ms[:, i, :i * P], NEG).then_inc(base, 1)

                def split_x(b, ks):
                    for k in ks:
                        dve.wait_ge(x_hi, K * b + k + 1)
                        nc.vector.tensor_tensor(xp[:, LO, k, :], xraw[:, k, :], as_f32(xp[:, HI, k, :]),
                                                ALU.subtract).then_inc(x_lo, 1)

                def q_tile(b, m):
                    dve.wait_ge(q_hi, K * b + m + 1)
                    nc.vector.tensor_tensor(qp[:, LO, m, :], proj[:, m % 2, :], as_f32(qp[:, HI, m, :]),
                                            ALU.subtract).then_inc(q_lo, 1)

                def x1_tile(b, k):
                    dve.wait_ge(x1t_hi, K * b + k + 1)
                    nc.vector.tensor_tensor(x1t[:, LO, k, :], tpsum[:, k % 2, :], as_f32(x1t[:, HI, k, :]),
                                            ALU.subtract).then_inc(x1t_out, 1)

                def cut_tile(b, i, first):
                    dve.wait_ge(s_mm, T * b + i + 1)
                    if first:
                        dve.wait_ge(strip_step, 3)
                    else:
                        dve.wait_ge(masked, T * b - T + i + 1)
                        dve.wait_ge(prob_exp, T * b - T + i + 1)
                    nc.vector.tensor_tensor(upper[:, i, i * P:], spsum[:, i % 2, i * P:],
                                            strip[:, (T - 1) * P:(2 * T - 1 - i) * P], ALU.mult).then_inc(cut, 1)

                def left_part(b, j):
                    i = j + 1
                    dve.wait_ge(sum_mm, (T - 1) * b + i)
                    if j == 0:
                        dve.wait_ge(sum_copied, b + 1)
                    if j:
                        nc.vector.tensor_tensor(left_sum[:, :], spsum[:, j % 2, :], left_sum[:, :],
                                                ALU.add).then_inc(sum_added, 1)
                        dve.wait_ge(sum_added, (T - 2) * b + j)
                    dve.wait_ge(prob_ready, T * b + i + 1)
                    nc.vector.scalar_tensor_tensor(out=y[:, i, :], in0=left_sum[:, :],
                                                   scalar=prob[:, i, 0:1], in1=y[:, i, :], op0=ALU.mult,
                                                   op1=ALU.add).then_inc(lower, 1)

                def recip(b, i):
                    dve.wait_ge(prob_exp, T * b + i + 1)
                    nc.vector.reciprocal(rden[:, i:i + 1], den[:, i:i + 1]).then_inc(have_rden, 1)

                def body(b, first, last):
                    for kind, m in Q_ORDER:
                        m = int(m)
                        if kind == "q" and (m or first):
                            q_tile(b, m)
                        elif kind == "x" and not first:
                            x1_tile(b - 1, m)
                    for i in range(T):
                        if i == 0:
                            cut_tile(b, 0, first)
                        dve.wait_ge(cut, T * b + i + 1)
                        nc.vector.tensor_scalar(gone[:, i, i * P:], upper[:, i, i * P:], 0.0, -NEG, ALU.is_equal,
                                                ALU.mult).then_inc(is_zero, 1)
                        dve.wait_ge(is_zero, T * b + i + 1)
                        if i + 1 < T:
                            cut_tile(b, i + 1, first)
                        else:
                            recip(b, i - 1)
                        if first and i == 0:
                            dve.wait_ge(base, T - 1)
                        nc.vector.tensor_tensor_reduce(ms[:, i, i * P:], upper[:, i, i * P:], gone[:, i, i * P:], -1.0,
                                                       NEG, ALU.add, ALU.min, negmax[:, i:i + 1]).then_inc(masked, 1)
                        if 0 < i < T - 1:
                            recip(b, i - 1)
                    recip(b, T - 1)
                    for kind, i in V_ORDER_DVE:
                        i = int(i)
                        if kind == "v":
                            dve.wait_ge(v_hi, T * b + i + 1)
                            nc.vector.tensor_tensor(vp[:, LO, i, :], proj[:, i % 2, :], as_f32(vp[:, HI, i, :]),
                                                    ALU.subtract).then_inc(v_lo, 1)
                        elif kind == "s":
                            if i == 0:
                                dve.wait_ge(x_loaded, 16 * b + 16)
                            left_part(b, i)
                        else:
                            n = (i + 1) * P
                            dve.wait_ge(pt_hi, T * b + i + 1)
                            nc.vector.tensor_tensor(pt[:, LO, i, :n], tpsum[:, i % 2, :n], as_f32(pt[:, HI, i, :n]),
                                                    ALU.subtract).then_inc(pt_lo, 1)
                    if not last:
                        split_x(b + 1, range(0, K // 2))
                    for i in range(T):
                        if i:
                            dve.wait_ge(lower, (T - 1) * b + i)
                        dve.wait_ge(av_mm, T * b + i + 1)
                        nc.vector.tensor_tensor(y[:, i, :], opsum[:, i % 2, :], y[:, i, :],
                                                ALU.add).then_inc(norm.summed, 1)
                        norm.stats(nc, b, i, y)
                        if i == 0 and not last:
                            split_x(b + 1, range(K // 2, K))
                    norm.variance(nc, b)
                    if not last:
                        q_tile(b + 1, 0)
                    norm.inverse(nc, b)
                    norm.scale(nc, y, y)

                batches(dve, body)
                for k in range(K):
                    x1_tile(NB - 1, k)

            @block.tensor
            def _(pe):
                def x1_tile(b, k):
                    pe.wait_ge(norm.normed, T * b + T)
                    if k < 2:
                        pe.wait_ge(pt_lo, T * b + T)
                    else:
                        pe.wait_ge(x1t_out, K * b + k - 1)
                    for i in range(T):
                        t = nc.tensor.transpose(tpsum[:, k % 2, i * P:(i + 1) * P], y[:, i, k * P:(k + 1) * P],
                                                ident[:, :])
                    t.then_inc(x1t_mm, 1)

                def q_tile(b, m, first):
                    if m >= 2:
                        pe.wait_ge(q_lo, K * b + m - 1)
                    elif not first:
                        pe.wait_ge(v_lo, T * b - 2 + m + 1)

                    def tokens(h, k):
                        if m == 0 and h == HI:
                            pe.wait_ge(x_lo, K * b + k + 1)
                        return xp[:, h, k, :]

                    three_pass(nc, proj[:, m % 2, :], lambda h, k: A[:, h, k, m * P:(m + 1) * P], tokens,
                               K).then_inc(q_mm, 1)

                def score_tile(b, i, first):
                    if i >= 2:
                        pe.wait_ge(cut, T * b + i - 1)
                    elif i == 0 and not first:
                        pe.wait_ge(lower, (T - 1) * b)
                    elif not first:
                        pe.wait_ge(cut, T * b - 2 + i + 1)

                    def queries(h, k):
                        if i == 0 and h == HI:
                            pe.wait_ge(q_lo, K * b + k + 1)
                        return qp[:, h, k, i * P:(i + 1) * P]

                    three_pass(nc, spsum[:, i % 2, i * P:], queries, lambda h, k: xp[:, h, k, i * P:],
                               K).then_inc(s_mm, 1)

                def v_tile(b, i):
                    pe.wait_ge(v_lo, T * b + i - 1) if i >= 2 else pe.wait_ge(q_lo, K * b + 3 + i)
                    three_pass(nc, proj[:, i % 2, :], lambda h, k: xp[:, h, k, i * P:(i + 1) * P],
                               lambda h, k: WV[:, h, k, :], K).then_inc(v_mm, 1)

                def turn(b, k, first):
                    if k >= 2:
                        pe.wait_ge(pt_lo, T * b + k - 1)
                    elif not first:
                        pe.wait_ge(x1t_out, K * b)
                    pe.wait_ge(prob_ready, T * b + k + 1)
                    for i in range(k + 1):
                        t = nc.tensor.transpose(tpsum[:, k % 2, i * P:(i + 1) * P],
                                                prob[:, i, k * P:(k + 1) * P], ident[:, :])
                    t.then_inc(t_mm, 1)

                def value_sum(b, j):
                    if j == 0:
                        pe.wait_ge(ones_made, 1)
                    if j < 2:
                        pe.wait_ge(cut, T * b + T - 1 + j)
                    else:
                        pe.wait_ge(sum_copied, b + 1)
                    pe.wait_ge(v_lo, T * b + j + 1)
                    for m in (HI, LO):
                        ins = nc.tensor.matmul(spsum[:, j % 2, :], ones[:, :], vp[:, m, j, :], start=(m == HI),
                                               stop=(m == LO))
                    ins.then_inc(sum_mm, 1)

                def av_tile(b, i, first):
                    if i >= 2:
                        pe.wait_ge(norm.summed, T * b + i - 1)
                    elif not first:
                        pe.wait_ge(norm.summed, T * b - 2 + i + 1)

                    def probabilities(h, k):
                        if i == 0 and h == HI:
                            pe.wait_ge(pt_lo, T * b + k + 1)
                            pe.wait_ge(v_lo, T * b + k + 1)
                        return pt[:, h, k, i * P:(i + 1) * P]

                    three_pass(nc, opsum[:, i % 2, :], lambda h, k: probabilities(h, k + i),
                               lambda h, k: vp[:, h, k + i, :], T - i).then_inc(av_mm, 1)

                def body(b, first, last):
                    for kind, m in Q_ORDER:
                        if kind == "q":
                            q_tile(b, int(m), first)
                        elif not first:
                            x1_tile(b - 1, int(m))
                    for i in range(T):
                        score_tile(b, i, first)
                    for kind, i in V_ORDER:
                        if kind == "v":
                            v_tile(b, int(i))
                        elif kind == "s":
                            value_sum(b, int(i))
                        else:
                            turn(b, int(i), first)
                    for i in range(T):
                        av_tile(b, i, first)

                batches(pe, body)
                for k in range(K):
                    x1_tile(NB - 1, k)


def cross_attention(nc, y_steps, xparts, cparts, wqparts, wkparts, wvparts, woparts, bq, bk, bv, bo, WsT, held, ident,
                    NB, S, D, H, DK):
    T, K = S // P, D // P
    HALVES, HH = 2, H // 2
    GROUPS = HALVES * NB
    PAIRS = HH // 2
    CH = HH * DK
    TILES, AHEAD_S, AHEAD_P = T * HH, 5, 4
    assert 2 * DK == P and CH == 512 and S == 512 and PAIRS == 4 and T == 4 and GROUPS % 2 == 0

    SLOTS = ["V3", "O0", "K2", "Q2", "O1", "O2", "K3", "Q3", "O3", "V0+", "K0+", "Q0+", "V1+", "V2+", "K1+", "Q1+"]
    assert 2 * len(SLOTS) == TILES
    FIRST_AHEAD = SLOTS.index("V0+")
    MADE = [name for name in SLOTS if name[0] != "O"]
    AHEAD = MADE[MADE.index("V0+"):]

    def pieces(name):
        return 1 if name[0] == "V" else 2

    def made(g, name):
        return len(MADE) * g + len(AHEAD) + MADE.index(name) + 1

    def split(g, name, head=1):
        n = MADE.index(name)
        return (sum(map(pieces, MADE)) * g + sum(map(pieces, AHEAD)) + sum(map(pieces, MADE[:n + 1]))
                - (1 - head if name[0] != "V" else 0))

    def pair_slot(g, letter, j):
        return (g - 1, f"{letter}{j}+") if j < 2 else (g, f"{letter}{j}")

    def wait(eng, sem, n):
        if not (isinstance(n, int) and n <= 0):
            eng.wait_ge(sem, n)

    def groups(eng, body):
        body(0, 0, True, False)
        with eng.Fori(0, GROUPS // 2 - 1) as c:
            body(c * 2 + 1, 1, False, False)
            body(c * 2 + 2, 0, False, False)
        body(GROUPS - 1, 1, False, True)

    def ahead(g, t, last):
        return [(g, t)] if t < TILES else [] if last else [(g + 1, t - TILES)]

    def slot(t, first, last):
        name = SLOTS[t // 2]
        return None if (first and name[0] == "O") or (last and name[-1] == "+") else name

    def head_before(g, t, first):
        return [(g, t // T - 1)] if t else [] if first else [(g - 1, HH - 1)]

    with ExitStack() as ctx:
        sc = Scope(nc, ctx, "c")
        WV, cp, xp = held.first, held.second, held.third
        WO = sc.sb("WO", [P, 2, PAIRS, D], F32R)
        wk, wq = sc.sb("wk", [P, 2, K, P], F32R), sc.sb("wq", [P, 2, K, P], F32R)
        qs = sc.sb("qs", [P, 2, 2, S], F32R)
        ks = sc.sb("ks", [P, 2, 2, 2, S], F32R)
        vs = sc.sb("vs", [P, 2, T, HH, 2 * DK], F32R)
        prob = sc.sb("prob", [P, 2, T, S])
        pt = sc.sb("pt", [P, 2, 2, S], F32R)
        opart, osum = sc.sb("opart", [P, S]), sc.sb("osum", [P, 2, S])
        op = sc.sb("op", [P, 2, PAIRS, S], F32R)
        y = sc.sb("y", [P, T, D])
        negmax, den, rden = sc.sb("negmax", [P, 2, T]), sc.sb("den", [P, 2, T]), sc.sb("rden", [P, 2, T])
        raw_b = [sc.sb("raw_bk", [P, H // 2]), sc.sb("raw_bq", [P, H // 2]), sc.sb("raw_bv", [DK, H])]
        bks, bqs, bvs = (sc.sb("bk", [P, GROUPS * PAIRS]), sc.sb("bq", [P, GROUPS * PAIRS]),
                         sc.sb("bv", [DK, GROUPS * HH]))
        projp, spsum = sc.ps("proj", [P, 2, 512]), sc.ps("score", [P, 2, 512])
        tpsum, opsum = sc.ps("turned", [P, 2, 512]), sc.ps("av", [P, 2, 512])

        (b_loaded, bias_ready, wk_loaded, wq_loaded, wo_loaded, wv_ready, wo_ready, proj_mm,
         proj_hi, proj_lo, s_mm, smax, p_exp, have_rden, p_ready, t_mm, pt_hi, pt_lo, av_mm, o_part, o_sum, op_hi,
         op_lo, wo_mm, wo_out, y_loaded, y_stored, passed) = (sc.sem(n) for n in (
             "b_loaded", "bias_ready", "wk_loaded", "wq_loaded", "wo_loaded", "wv_ready",
             "wo_ready", "proj_mm", "proj_hi", "proj_lo", "s_mm", "smax", "p_exp", "have_rden", "p_ready", "t_mm",
             "pt_hi", "pt_lo", "av_mm", "o_part", "o_sum", "op_hi", "op_lo", "wo_mm", "wo_out", "y_loaded", "y_stored",
             "passed"))
        k_doubled = [sc.sem(f"k_doubled{n}") for n in range(2)]
        wv_loaded, c_loaded, x_loaded = held.wv_loaded, held.c_loaded, held.x_loaded

        WS_AT = [TILES - 10 + 2 * k for k in range(K)]

        def sides(e):
            own, other = slice(0, DK), slice(DK, P)
            return (own, other) if e == 0 else (other, own)

        with nc.Block() as block:

            @block.sync
            def _(sp):
                def load_x(b):
                    sp.dma_start(as_f32(xp[:, :, :, :]), xparts[b]).then_inc(x_loaded, 16)

                def load_pair(dst, parts, pair, loaded):
                    sp.dma_start(as_f32(dst[:, :, :, :]), parts[pair]).then_inc(loaded, 16)

                def load_y(g):
                    sp.dma_start(y[:, :, :], y_steps[g].rearrange("(t p) d -> p t d", p=P)).then_inc(y_loaded, 16)

                def store_y(g):
                    sp.wait_ge(wo_out, T * g + T)
                    sp.dma_start(y_steps[g + NB].rearrange("(t p) d -> p t d", p=P), y[:, :, :]).then_inc(y_stored, 16)
                    sp.wait_ge(y_stored, 16 * g + 16)

                def load_x2(u):
                    sp.dma_start(held.x2[:, u, :, :], y_steps[2 * NB + u].rearrange(
                        "(t p) d -> p t d", p=P)).then_inc(held.y_loaded[u], 16)

                def double_k(g, name):
                    ring = int(name[1]) % 2
                    for e in range(2):
                        own, other = sides(e)
                        sp.wait_ge(proj_lo, split(g, name, e))
                        sp.dma_start(as_f32(ks[other, ring, e, :, :]),
                                     as_f32(ks[own, ring, e, :, :])).then_inc(k_doubled[e], 16)

                sp.wait_ge(wv_loaded, 16 * K)
                sp.sem_inc(wv_ready, 1)
                load_pair(wk, wkparts, 0, wk_loaded)
                for dst, src in zip(raw_b, (bk, bq, bv)):
                    sp.dma_start(dst[:, :], src).then_inc(b_loaded, 16)
                load_pair(wq, wqparts, 0, wq_loaded)
                load_y(0)
                sp.dma_start(held.bo[:, :], bo.partition_broadcast(P)).then_inc(held.bo_loaded, 16)
                sp.wait_ge(proj_mm, made(-1, "K0+"))
                load_pair(wk, wkparts, 1, wk_loaded)
                double_k(-1, "K0+")
                sp.wait_ge(proj_mm, made(-1, "Q0+"))
                load_pair(wq, wqparts, 1, wq_loaded)
                sp.wait_ge(proj_mm, made(-1, "K1+"))
                load_pair(wk, wkparts, 2, wk_loaded)
                double_k(-1, "K1+")
                sp.wait_ge(proj_mm, made(-1, "Q1+"))
                load_pair(wq, wqparts, 2, wq_loaded)

                def body(g, b, h, opens, closes):
                    last = closes and h == HALVES - 1
                    nb, nh = (0, h + 1) if closes else (b + 1, h)
                    if closes:
                        sp.wait_ge(proj_mm, made(g, "V3"))
                        if last:
                            load_x2(0)
                            sp.dma_start(held.x2[:, 1, :, :],
                                         WsT.rearrange("(k p) n -> p k n", p=P)).then_inc(held.ws_loaded, 16)
                        else:
                            load_half(sp, WV, wvparts, nh, wv_loaded)
                    for name, following in (("K2", (h, 3)), ("K3", (nh, 0))):
                        final = last and following[1] == 0
                        sp.wait_ge(proj_mm, made(g, name))
                        if not final:
                            load_pair(wk, wkparts, following[0] * PAIRS + following[1], wk_loaded)
                        if name == "K3" and not last:
                            load_ctx(sp, held, cparts, nb)
                        double_k(g, name)
                        if not final:
                            sp.wait_ge(proj_mm, made(g, "Q" + name[1]))
                            load_pair(wq, wqparts, following[0] * PAIRS + following[1], wq_loaded)
                        if name == "K3" and not last:
                            load_x(nb)
                    if not last:
                        if closes:
                            sp.wait_ge(wv_loaded, 16 * K * (nh + 1))
                        sp.sem_inc(wv_ready, 1)
                    if not (opens and h == 0):
                        store_y(g - 1)
                        load_y(g)
                    if opens:
                        wait(sp, wo_mm, T * g)
                        load_half(sp, WO, woparts, h, wo_loaded)
                    if not last:
                        for name, j in (("K0+", 1), ("K1+", 2)):
                            sp.wait_ge(proj_mm, made(g, name))
                            load_pair(wk, wkparts, nh * PAIRS + j, wk_loaded)
                            double_k(g, name)
                            sp.wait_ge(proj_mm, made(g, "Q" + name[1:]))
                            load_pair(wq, wqparts, nh * PAIRS + j, wq_loaded)
                    if opens:
                        sp.wait_ge(wo_loaded, 16 * K * (h + 1))
                    sp.sem_inc(wo_ready, 1)

                for h in range(HALVES):
                    body(NB * h, 0, h, True, False)
                    with sp.Fori(1, NB - 1) as b:
                        body(b + NB * h, b, h, False, False)
                    body(NB * h + NB - 1, NB - 1, h, False, True)
                sp.wait_ge(held.ws_lo, K)
                load_x2(1)
                for i in range(T):
                    sp.wait_ge(wo_out, T * (GROUPS - 1) + i + 1)
                    sp.dma_start(y_steps[GROUPS - 1 + NB, i * P:(i + 1) * P, :], y[:, i, :]).then_inc(y_stored, 16)
                sp.wait_ge(y_stored, 16 * (GROUPS - 1 + T))

            @block.gpsimd
            def _(pool):
                def norm_tile(g, t):
                    n, i = divmod(t, T)
                    pool.wait_ge(have_rden, TILES * g + t + 1)
                    pool.sem_inc(passed, 1)
                    nc.gpsimd.tensor_scalar(prob[:, n % 2, i, :], prob[:, n % 2, i, :], rden[:, n % 2, i:i + 1], 1.0,
                                            ALU.mult, ALU.mult).then_inc(p_ready, 1)

                def split_hi(g, j):
                    pool.wait_ge(o_sum, HH * g + 2 * j + 2)
                    if j == 0:
                        wait(pool, wo_mm, T * g)
                    pool.sem_inc(passed, 1)
                    nc.gpsimd.tensor_scalar(op[:, HI, j, :], osum[:, j % 2, :], 1.0, 1.0, ALU.mult,
                                            ALU.mult).then_inc(op_hi, 1)

                def split_lo(g, j):
                    pool.wait_ge(op_hi, PAIRS * g + j + 1)
                    nc.gpsimd.tensor_tensor(op[:, LO, j, :], osum[:, j % 2, :], as_f32(op[:, HI, j, :]),
                                            ALU.subtract).then_inc(op_lo, 1)

                SPLIT_AT = {18: 0, 20: 1, 25: 2}

                def body(g, u, first, last):
                    for t in range(TILES):
                        if t == 1 and not first:
                            split_hi(g - 1, PAIRS - 1)
                            split_lo(g - 1, PAIRS - 1)
                        for tile in ahead(g, t + AHEAD_P, last):
                            norm_tile(*tile)
                        if t in SPLIT_AT:
                            split_hi(g, SPLIT_AT[t])
                        if t - 1 in SPLIT_AT:
                            split_lo(g, SPLIT_AT[t - 1])
                        if last and t == TILES - AHEAD_P:
                            pool.wait_ge(held.bo_loaded, 16)
                            add_bo(nc, held, 0, 0)

                for t in range(AHEAD_P):
                    norm_tile(0, t)
                groups(pool, body)
                split_hi(GROUPS - 1, PAIRS - 1)
                split_lo(GROUPS - 1, PAIRS - 1)

            @block.scalar
            def _(act):
                def exp_tile(g, t):
                    n, i = divmod(t, T)
                    head = HH * g + n
                    act.wait_ge(smax, T * head + i + 1)
                    if i == 0:
                        wait(act, t_mm, T * head - T)
                    nc.scalar.activation(prob[:, n % 2, i, :], spsum[:, i % 2, :], ACT.Exp,
                                         bias=negmax[:, n % 2, i:i + 1], scale=1.0,
                                         accum_out=den[:, n % 2, i:i + 1]).then_inc(p_exp, 1)

                def proj_hi_part(g, name, u):
                    bank, j = projp[:, SLOTS.index(name) % 2, :], int(name[1])
                    G = g + 1 if name[-1] == "+" else g
                    act.wait_ge(proj_mm, made(g, name))
                    if name[0] == "V":
                        if j == 0:
                            wait(act, av_mm, TILES * (G - 1))
                        ring = 1 - u if name[-1] == "+" else u
                        nc.scalar.copy(vs[:, ring, j, :, 0:DK],
                                       bank.rearrange("p (h d) -> p h d", d=DK)).then_inc(proj_hi, 1)
                        return
                    bias = bks if name[0] == "K" else bqs
                    wait(act, s_mm, T * (HH * G + 2 * j - 2))
                    for e in range(2):
                        rows = sides(e)[0]
                        dst = ks[rows, j % 2, e, HI, :] if name[0] == "K" else qs[rows, j % 2, e, :]
                        nc.scalar.activation(dst, bank[rows, :], ACT.Identity,
                                             bias=bias[rows, bass.ds(G * PAIRS + j, 1)], scale=1.0).then_inc(proj_hi, 1)

                def pt_tile(g, t):
                    act.wait_ge(t_mm, TILES * g + t + 1)
                    wait(act, av_mm, TILES * g + t - 1)
                    nc.scalar.copy(pt[:, t % 2, HI, :], tpsum[:, t % 2, :]).then_inc(pt_hi, 1)

                def o_first(g, n):
                    head = HH * g + n
                    act.wait_ge(av_mm, T * head + T)
                    wait(act, o_sum, head - 1)
                    nc.scalar.activation(opart[sides(n % 2)[0], :], opsum[0:DK, n % 2, :], ACT.Identity,
                                         bias=bvs[:, bass.ds(head, 1)], scale=1.0).then_inc(o_part, 1)

                def body(g, u, first, last):
                    for t in range(TILES):
                        for tile in ahead(g, t + AHEAD_P, last):
                            exp_tile(*tile)
                        pt_tile(g, t)
                        if t % T == 0:
                            for head in head_before(g, t, first):
                                o_first(*head)
                        name = slot(t, first, last)
                        if t % 2 == 1 and name and name[0] != "O":
                            proj_hi_part(g, name, u)
                        if last and t in WS_AT:
                            k = WS_AT.index(t)
                            act.wait_ge(held.ws_loaded, 16)
                            act.wait_ge(proj_mm, made(g, "Q3"))
                            nc.scalar.copy(held.third[:, HI, k, :], held.x2[:, 1, k, :]).then_inc(held.ws_hi, 1)

                act.wait_ge(bias_ready, 3 * NB)
                for name in AHEAD:
                    proj_hi_part(-1, name, 1)
                    if name == "V2+":
                        for t in range(2):
                            exp_tile(0, t)
                for t in range(2, AHEAD_P):
                    exp_tile(0, t)
                groups(act, body)
                o_first(GROUPS - 1, HH - 1)
                held.norm2.root(nc, 0)

            @block.vector
            def _(dve):
                def max_tile(g, t):
                    n, i = divmod(t, T)
                    dve.wait_ge(s_mm, TILES * g + t + 1)
                    nc.vector.tensor_reduce(negmax[:, n % 2, i:i + 1], spsum[:, i % 2, :], AX.X, ALU.max,
                                            negate=True).then_inc(smax, 1)

                def recip(g, t):
                    n, i = divmod(t, T)
                    dve.wait_ge(p_exp, TILES * g + t + 1)
                    nc.vector.reciprocal(rden[:, n % 2, i:i + 1], den[:, n % 2, i:i + 1]).then_inc(have_rden, 1)

                def proj_lo_part(g, name, u, heads=(0, 1)):
                    bank, j = projp[:, SLOTS.index(name) % 2, :], int(name[1])
                    G = g + 1 if name[-1] == "+" else g
                    if name[0] == "V":
                        ring = 1 - u if name[-1] == "+" else u
                        dve.wait_ge(proj_hi, split(g, name))
                        nc.vector.tensor_tensor(vs[:, ring, j, :, DK:], bank.rearrange("p (h d) -> p h d", d=DK),
                                                as_f32(vs[:, ring, j, :, 0:DK]), ALU.subtract).then_inc(proj_lo, 1)
                        return
                    bias = bks if name[0] == "K" else bqs
                    for e in heads:
                        rows, other = sides(e)
                        dve.wait_ge(proj_hi, split(g, name, e))
                        if name[0] == "K":
                            hi, lo = ks[rows, j % 2, e, HI, :], ks[rows, j % 2, e, LO, :]
                        else:
                            hi, lo = qs[rows, j % 2, e, :], qs[other, j % 2, e, :]
                        nc.vector.scalar_tensor_tensor(out=lo, in0=bank[rows, :],
                                                       scalar=bias[rows, bass.ds(G * PAIRS + j, 1)], in1=as_f32(hi),
                                                       op0=ALU.add, op1=ALU.subtract).then_inc(proj_lo, 1)

                def add_out(g, name):
                    i = int(name[1])
                    if i == 0:
                        dve.wait_ge(y_loaded, 16 * g)
                    dve.wait_ge(wo_mm, T * (g - 1) + i + 1)
                    nc.vector.tensor_tensor(y[:, i, :], projp[:, SLOTS.index(name) % 2, :], y[:, i, :],
                                            ALU.add).then_inc(wo_out, 1)

                def pt_tile(g, t):
                    dve.wait_ge(pt_hi, TILES * g + t + 1)
                    nc.vector.tensor_tensor(pt[:, t % 2, LO, :], tpsum[:, t % 2, :], as_f32(pt[:, t % 2, HI, :]),
                                            ALU.subtract).then_inc(pt_lo, 1)

                def o_second(g, n):
                    head = HH * g + n
                    dve.wait_ge(o_part, head + 1)
                    wait(dve, op_lo, PAIRS * g + n // 2 - 1)
                    rows = sides(n % 2)[0]
                    nc.vector.tensor_tensor(osum[rows, n // 2 % 2, :], opsum[DK:P, n % 2, :], opart[rows, :],
                                            ALU.add).then_inc(o_sum, 1)

                def finish_slot(g, u, t, first, last):
                    if t < 2:
                        return proj_lo_part(g - 1, SLOTS[-1], 1 - u, (t,))
                    name = slot(t - 2, first, last)
                    if name and name[0] in "KQ":
                        proj_lo_part(g, name, u, (t % 2,))
                    elif name and t % 2 == 0:
                        add_out(g, name) if name[0] == "O" else proj_lo_part(g, name, u)

                def body(g, u, first, last):
                    for t in range(TILES):
                        for tile in ahead(g, t + AHEAD_S, last):
                            max_tile(*tile)
                        finish_slot(g, u, t, first, last)
                        if t % T == 1:
                            for head in head_before(g, t - 1, first):
                                o_second(*head)
                        for tile in ahead(g, t + AHEAD_P, last):
                            recip(*tile)
                        if last and t - 1 in WS_AT:
                            k = WS_AT.index(t - 1)
                            dve.wait_ge(held.ws_hi, k + 1)
                            nc.vector.tensor_tensor(held.third[:, LO, k, :], held.x2[:, 1, k, :],
                                                    as_f32(held.third[:, HI, k, :]),
                                                    ALU.subtract).then_inc(held.ws_lo, 1)
                        pt_tile(g, t)

                dve.wait_ge(b_loaded, 48)
                for raw, dst, scale in zip(raw_b, (bks, bqs, bvs), (1.0, float(NB) ** -0.5, 1.0)):
                    halves = dst[:, :].rearrange("p (h b j) -> p h b j", h=HALVES, b=NB)
                    for b in range(NB):
                        nc.vector.tensor_scalar(halves[:, :, b, :], raw[:, :].rearrange("p (h j) -> p h j", h=HALVES),
                                                scale, None, ALU.mult).then_inc(bias_ready, 1)
                dve.wait_ge(bias_ready, 3 * NB)
                for name in AHEAD:
                    if name != AHEAD[-1]:
                        proj_lo_part(-1, name, 1)
                    if name == "V2+":
                        for t in range(2):
                            max_tile(0, t)
                for t in range(2, AHEAD_S):
                    max_tile(0, t)
                    recip(0, t - 2)
                recip(0, AHEAD_P - 1)
                groups(dve, body)
                o_second(GROUPS - 1, HH - 1)
                x2, norm2 = held.x2[:, 0, :, :], held.norm2
                for i in range(T):
                    norm2.stats(nc, 0, i, x2)
                add_out(GROUPS, "O0")
                norm2.variance(nc, 0)
                add_out(GROUPS, "O1")
                norm2.inverse(nc, 0)
                norm2.scale(nc, x2, x2)
                add_out(GROUPS, "O2")
                add_out(GROUPS, "O3")

            @block.tensor
            def _(pe):
                def bank_free(g, name, first):
                    s = SLOTS.index(name) - 2
                    if first and s >= 0 and SLOTS[s][0] == "O":
                        s -= 2
                    if s < 0:
                        g, s = g - 1, s + len(SLOTS)
                    if SLOTS[s][0] == "O":
                        pe.wait_ge(wo_out, T * (g - 1) + int(SLOTS[s][1]) + 1)
                    else:
                        pe.wait_ge(proj_lo, split(g, SLOTS[s]))

                def project(g, name, u, part=0, parts=1):
                    G, j = (g + 1 if name[-1] == "+" else g), int(name[1])
                    out = projp[:, SLOTS.index(name) % 2, :]
                    mms = [(k, s, m) for k in range(K) for s, m in TERMS]
                    lo, hi = part * len(mms) // parts, (part + 1) * len(mms) // parts
                    if part == 0:
                        if name == "V0+":
                            pe.wait_ge(wv_ready, G + 1)
                        if name[0] == "K":
                            pe.wait_ge(wk_loaded, 16 * (PAIRS * G + j + 1))
                        if name[0] == "Q":
                            pe.wait_ge(wq_loaded, 16 * (PAIRS * G + j + 1))
                        if name == "Q0+":
                            pe.wait_ge(x_loaded, 16 * G + 16)
                        if name == "O0":
                            pe.wait_ge(wo_ready, g)
                    for n, (k, s, m) in enumerate(mms[lo:hi], lo):
                        if name == "V0+" and n % len(TERMS) == 0:
                            pe.wait_ge(c_loaded[k], 16 * G + 16)
                        if name[0] == "K":
                            l, r = wk[:, s, k, :], cp[:, m, k, :]
                        elif name[0] == "Q":
                            l, r = wq[:, s, k, :], xp[:, m, k, :]
                        elif name[0] == "V":
                            l, r = cp[:, s, k, j * P:(j + 1) * P], WV[:, m, k, :]
                        else:
                            if j == 0 and n % len(TERMS) == 0:
                                pe.wait_ge(op_lo, PAIRS * (g - 1) + k + 1)
                            l, r = op[:, s, k, j * P:(j + 1) * P], WO[:, m, k, :]
                        ins = nc.tensor.matmul(out, l, r, start=(n == 0), stop=(n == len(mms) - 1))
                    if part == parts - 1:
                        ins.then_inc(wo_mm if name[0] == "O" else proj_mm, 1)

                def scores(g, t):
                    n, i = divmod(t, T)
                    head, j, e = HH * g + n, n // 2, n % 2
                    if i == 0:
                        pe.wait_ge(proj_lo, split(*pair_slot(g, "Q", j), e))
                        pe.wait_ge(k_doubled[e], 16 * (PAIRS * g + j + 1))
                    wait(pe, p_exp, T * head + i - 1)
                    for m in (HI, LO):
                        ins = nc.tensor.matmul(spsum[:, i % 2, :], qs[:, j % 2, e, i * P:(i + 1) * P],
                                               ks[:, j % 2, e, m, :], start=(m == HI), stop=(m == LO))
                    ins.then_inc(s_mm, 1)

                def turn(g, t):
                    n, k = divmod(t, T)
                    head = HH * g + n
                    wait(pe, pt_lo, T * head + k - 1)
                    for i in range(T):
                        if k == 0:
                            pe.wait_ge(p_ready, T * head + i + 1)
                        ins = nc.tensor.transpose(tpsum[:, k % 2, i * P:(i + 1) * P],
                                                  prob[:, n % 2, i, k * P:(k + 1) * P], ident[:, :])
                    ins.then_inc(t_mm, 1)

                def values(g, t, u):
                    n, k = divmod(t, T)
                    head = HH * g + n
                    if k == 0:
                        wait(pe, o_sum, head - 1)
                    if n == 0:
                        pe.wait_ge(proj_lo, split(g, "V3") if k == T - 1 else split(g - 1, f"V{k}+"))
                    pe.wait_ge(pt_lo, T * head + k + 1)
                    for m in (HI, LO):
                        ins = nc.tensor.matmul(opsum[:, n % 2, :], vs[:, u, k, n, :], pt[:, k % 2, m, :],
                                               start=(k == 0 and m == HI), stop=(k == T - 1 and m == LO))
                    ins.then_inc(av_mm, 1)

                def body(g, u, first, last):
                    for t in range(TILES):
                        for tile in ahead(g, t + AHEAD_S, last):
                            scores(*tile)
                        name = slot(t, first, last)
                        if name:
                            if t % 2 == 0:
                                bank_free(g, name, first)
                            project(g, name, u, t % 2, 2)
                        turn(g, t)
                        if t:
                            values(g, t - 1, u)
                        elif not first:
                            values(g - 1, TILES - 1, 1 - u)

                for name in AHEAD:
                    if SLOTS.index(name) >= FIRST_AHEAD + 2:
                        bank_free(-1, name, False)
                    project(-1, name, 1)
                    if name == "V2+":
                        for t in range(2):
                            scores(0, t)
                for t in range(2, AHEAD_S):
                    scores(0, t)
                groups(pe, body)
                values(GROUPS - 1, TILES - 1, 1)
                for i in range(T):
                    if i >= 2:
                        pe.wait_ge(wo_out, T * (GROUPS - 1) + i - 1)
                    project(GROUPS, f"O{i}", 0)


def feed_forward(nc, y_in, WeT, Wg, bias, held, ident, out, NB, S, D, NG):
    T, K, RING = S // P, D // P, 2
    SHARED, EXPERT = 0, 1
    PAD = 8
    assert NB % RING == 0 and T == 4 and K == 4 and NG < PAD
    with ExitStack() as ctx:
        sc = Scope(nc, ctx, "f")
        x2, raw = held.x2, sc.sb("raw", [P, K, D])
        W = [held.third, sc.sb("We", [P, 2, K, D], F32R)]
        graw, G = sc.sb("graw", [P, K, P]), sc.sb("G", [P, 2, K, P], F32R)
        bias_all = sc.sb("bias", [P, D])
        x2T = sc.sb("x2T", [P, RING, 2, K, S], F32R)
        z = sc.sb("z", [P, RING, T, D])
        logitT = sc.sb("logitT", [P, S])
        e = sc.sb("e", [P, T, PAD])
        gneg, den = sc.sb("gneg", [P, T]), sc.sb("den", [P, T])
        best = sc.sb("best", [P, T, PAD])
        total, route, weight = sc.sb("total", [P, T]), sc.sb("route", [P, 2, T]), sc.sb("weight", [P, T])
        prod = sc.ps("prod", [P, RING, 2, D])
        turned = sc.ps("turned", [P, 2, S])
        gateT, logit = sc.ps("gateT", [P, S]), sc.ps("logit", [P, T, P])

        (we_loaded, g_zero, g_loaded, w_hi, w_lo, b_loaded, xb_made, t_mm, x2_hi, x2_lo, gate_mm, gate_out, lt_mm,
         g_max, e_done, e_pad, w_step, w_done, prod_mm, z_mid) = (sc.sem(n) for n in (
             "we_loaded", "g_zero", "g_loaded", "w_hi", "w_lo", "b_loaded", "xb_made", "t_mm", "x2_hi", "x2_lo",
             "gate_mm", "gate_out", "lt_mm", "g_max", "e_done", "e_pad", "w_step", "w_done", "prod_mm", "z_mid"))
        ranked, passed = sc.sem("ranked"), sc.sem("passed")
        y_loaded, z_stored = held.y_loaded, [sc.sem(f"z_stored{u}") for u in range(RING)]
        WEIGHT_STEPS = 1 + T + 4
        CREDIT = 16
        norm2, norm3 = held.norm2, Norm(sc, T, D, "norm3", credit=CREDIT)

        def done(n):
            return n + CREDIT

        def batches(eng, step):
            if NB > RING:
                with eng.Fori(0, NB // RING - 1) as c:
                    for u in range(RING):
                        step(c * RING + u, u, c, RING)
            for u in range(RING):
                step(NB - RING + u, u, NB // RING - 1, RING - 1 - u)

        with nc.Block() as block:

            @block.sync
            def _(sp):
                def load(u, b):
                    sp.dma_start(x2[:, u, :, :], y_in[b].rearrange("(t p) d -> p t d", p=P)).then_inc(y_loaded[u], 16)

                sp.dma_start(raw[:, :, :], WeT.rearrange("(k p) n -> p k n", p=P)).then_inc(we_loaded, 16)
                sp.wait_ge(g_zero, 1)
                sp.dma_start(graw[:, :, :NG], Wg.rearrange("(k p) n -> p k n", p=P)).then_inc(g_loaded, 16)
                sp.dma_start(bias_all[:, :], bias.partition_broadcast(P)).then_inc(b_loaded, 16)

                def step(b, u, c, more):
                    if more == RING:
                        sp.wait_ge(t_mm, K * b + K)
                        sp.wait_ge(xb_made, T * b + T)
                        load(u, b + RING)
                    if more:
                        sp.wait_ge(norm3.normed, done(T * b + T))
                        sp.dma_start(out[b].rearrange("(t p) d -> p t d", p=P), z[:, u, :, :]).then_inc(z_stored[u], 16)
                    else:
                        for i in range(T):
                            sp.wait_ge(norm3.normed, done(T * b + i + 1))
                            sp.dma_start(out[b, i * P:(i + 1) * P, :], z[:, u, i, :]).then_inc(z_stored[u], 16)

                batches(sp, step)
                sp.wait_ge(z_stored[0], done(16 * NB // RING))
                sp.wait_ge(z_stored[1], done(16 * (NB // RING - 1 + T)))

            @block.gpsimd
            def _(pool):
                nc.gpsimd.memset(graw[:, :, :], 0.0).then_inc(g_zero, 1)
                for u in range(RING):
                    pool.sem_inc(z_stored[u], CREDIT)

                def add_bias(b, u, c):
                    pool.wait_ge(norm2.normed, T * b + T)
                    pool.wait_ge(z_stored[u], 16 * c + CREDIT)
                    for i in range(T):
                        nc.gpsimd.tensor_tensor(z[:, u, i, :], x2[:, u, i, :], bias_all[:, :],
                                                ALU.add).then_inc(xb_made, 1)

                add_bo(nc, held, 1, 0)
                pool.wait_ge(b_loaded, 16)
                add_bias(0, 0, 0)

                def step(b, u, c, more):
                    if more:
                        add_bias(b + 1, (u + 1) % RING, c + (u + 1) // RING)
                    if more == RING:
                        add_bo(nc, held, u, c + 1)
                    if more:
                        norm3.scale_on_pool(nc, b, z[:, u])

                batches(pool, step)

            @block.scalar
            def _(act):
                act.sem_inc(e_done, CREDIT)
                act.sem_inc(gate_out, CREDIT)

                def turn_hi(b, u):
                    for k in range(K):
                        act.wait_ge(t_mm, K * b + k + 1)
                        act.wait_ge(prod_mm, done(T * b - T))
                        nc.scalar.copy(x2T[:, u, HI, k, :], turned[:, k % 2, :]).then_inc(x2_hi, 1)

                def gate_copy(b):
                    act.wait_ge(gate_mm, b + 1)
                    act.wait_ge(lt_mm, done(b))
                    nc.scalar.copy(logitT[:, :], gateT[:, :]).then_inc(gate_out, 1)

                turn_hi(0, 0)
                act.wait_ge(g_loaded, 16)
                nc.scalar.copy(G[:, HI, :, :], graw[:, :, :]).then_inc(w_hi, 1)
                act.wait_ge(we_loaded, 16)
                for k in range(K):
                    nc.scalar.copy(W[EXPERT][:, HI, k, :], raw[:, k, :]).then_inc(w_hi, 1)
                gate_copy(0)

                def step(b, u, c, more):
                    act.wait_ge(g_max, b + 1)
                    act.wait_ge(w_done, done(b))
                    for i in range(T):
                        nc.scalar.activation(e[:, i, :NG], logit[:, i, :NG], ACT.Exp, bias=gneg[:, i:i + 1], scale=1.0,
                                             accum_out=den[:, i:i + 1]).then_inc(e_done, 1)
                    if more:
                        norm2.root(nc, b + 1)
                        turn_hi(b + 1, (u + 1) % RING)
                        gate_copy(b + 1)
                    norm3.root(nc, b)

                batches(act, step)

            @block.vector
            def _(dve):
                for s in (x2_lo, w_done, norm3.summed, norm3.normed):
                    dve.sem_inc(s, CREDIT)
                nc.vector.memset(e[:, :, :], 0.0).then_inc(e_pad, 1)
                dve.wait_ge(e_pad, 1)
                v = nc.vector

                def turn_lo(b, u):
                    for k in range(K):
                        dve.wait_ge(x2_hi, K * b + k + 1)
                        v.tensor_tensor(x2T[:, u, LO, k, :], turned[:, k % 2, :], as_f32(x2T[:, u, HI, k, :]),
                                        ALU.subtract).then_inc(x2_lo, 1)

                def gate_max(b):
                    dve.wait_ge(lt_mm, done(b + 1))
                    v.tensor_reduce(gneg[:, :], logit[:, :, :NG], AX.X, ALU.max, negate=True).then_inc(g_max, 1)

                def route_weights(b):
                    count = [WEIGHT_STEPS * b]

                    def link(ins):
                        count[0] = count[0] + 1
                        ins.then_inc(w_step, 1)
                        dve.wait_ge(w_step, count[0])

                    dve.wait_ge(e_done, done(T * b + T))
                    link(v.reciprocal(den[:, :], den[:, :]))
                    for i in range(T):
                        link(v.tensor_scalar(e[:, i, :NG], e[:, i, :NG], den[:, i:i + 1], None, ALU.mult))
                    dve.sem_inc(passed, 1)
                    for i in range(T):
                        v.max(best[:, i, :], e[:, i, :]).then_inc(ranked, 1)
                    dve.wait_ge(ranked, T * b + T)
                    link(v.tensor_tensor(total[:, :], best[:, :, 0], best[:, :, 1], ALU.add))
                    link(v.reciprocal(total[:, :], total[:, :]))
                    for r in range(2):
                        link(v.tensor_tensor(route[:, r, :], best[:, :, r], total[:, :], ALU.mult))
                    v.tensor_tensor(weight[:, :], route[:, 0, :], route[:, 1, :], ALU.add).then_inc(w_done, 1)

                def finish_tile(b, u, i):
                    dve.wait_ge(prod_mm, done(T * b + i + 1))
                    dve.wait_ge(xb_made, T * b + i + 1)
                    if i == 0:
                        dve.wait_ge(w_done, done(b + 1))
                    v.scalar_tensor_tensor(out=z[:, u, i, :], in0=prod[:, i % RING, EXPERT, :],
                                           scalar=weight[:, i:i + 1], in1=z[:, u, i, :], op0=ALU.mult, op1=ALU.add).then_inc(z_mid, 1)
                    dve.wait_ge(z_mid, T * b + i + 1)
                    v.tensor_tensor(z[:, u, i, :], prod[:, i % RING, SHARED, :], z[:, u, i, :],
                                    ALU.add).then_inc(norm3.summed, 1)
                    norm3.stats(nc, b, i, z[:, u])

                turn_lo(0, 0)
                dve.wait_ge(w_hi, 1)
                v.tensor_tensor(G[:, LO, :, :], graw[:, :, :], as_f32(G[:, HI, :, :]), ALU.subtract).then_inc(w_lo, 1)
                for k in range(K):
                    dve.wait_ge(w_hi, k + 2)
                    v.tensor_tensor(W[EXPERT][:, LO, k, :], raw[:, k, :], as_f32(W[EXPERT][:, HI, k, :]),
                                    ALU.subtract).then_inc(w_lo, 1)

                def step(b, u, c, more):
                    nu = (u + 1) % RING
                    gate_max(b)
                    if more:
                        for i in range(T):
                            norm2.stats(nc, b + 1, i, x2[:, nu])
                    route_weights(b)
                    finish_tile(b, u, 0)
                    if more:
                        norm2.variance(nc, b + 1)
                        norm2.inverse(nc, b + 1)
                        norm2.scale(nc, x2[:, nu], x2[:, nu])
                    finish_tile(b, u, 1)
                    finish_tile(b, u, 2)
                    if more:
                        turn_lo(b + 1, nu)
                    finish_tile(b, u, 3)
                    dve.wait_ge(norm3.normed, done(T * b))
                    norm3.variance(nc, b)
                    norm3.inverse(nc, b)
                    if not more:
                        norm3.scale(nc, z[:, u], z[:, u])

                batches(dve, step)

            @block.tensor
            def _(pe):
                pe.sem_inc(lt_mm, CREDIT)
                pe.sem_inc(prod_mm, CREDIT)

                def turn(b, u, ks):
                    pe.wait_ge(norm2.normed, T * b + T)
                    for k in ks:
                        pe.wait_ge(x2_lo, done(K * b + k - 1))
                        for i in range(T):
                            t = nc.tensor.transpose(turned[:, k % 2, i * P:(i + 1) * P], x2[:, u, i, k * P:(k + 1) * P],
                                                    ident[:, :])
                        t.then_inc(t_mm, 1)

                def gate(b, u):
                    pe.wait_ge(x2_lo, done(K * b + K))
                    pe.wait_ge(gate_out, done(b))
                    three_pass(nc, gateT[:, :], lambda s, k: G[:, s, k, :], lambda m, k: x2T[:, u, m, k, :],
                               K).then_inc(gate_mm, 1)

                def turn_logits(b):
                    pe.wait_ge(gate_out, done(b + 1))
                    pe.wait_ge(e_done, done(T * b))
                    for i in range(T):
                        t = nc.tensor.transpose(logit[:, i, :], logitT[:, i * P:(i + 1) * P], ident[:, :])
                    t.then_inc(lt_mm, 1)

                def product(b, u, i, which):
                    pe.wait_ge(held.ws_lo, K) if which == SHARED else pe.wait_ge(w_lo, K + 1)
                    if which == SHARED:
                        pe.wait_ge(norm3.summed, done(T * b + i - 1))
                    return three_pass(nc, prod[:, i % RING, which, :], lambda s, k: x2T[:, u, s, k, i * P:(i + 1) * P],
                                      lambda m, k: W[which][:, m, k, :], K)

                turn(0, 0, range(K))
                pe.wait_ge(w_lo, 1)
                gate(0, 0)

                def step(b, u, c, more):
                    nu = (u + 1) % RING
                    product(b, u, 0, SHARED)
                    turn_logits(b)
                    product(b, u, 0, EXPERT).then_inc(prod_mm, 1)
                    for i in (1, 2):
                        product(b, u, i, SHARED)
                        product(b, u, i, EXPERT).then_inc(prod_mm, 1)
                    if more:
                        turn(b + 1, nu, range(0, 2))
                    product(b, u, 3, SHARED)
                    if more:
                        turn(b + 1, nu, range(2, K))
                    product(b, u, 3, EXPERT).then_inc(prod_mm, 1)
                    if more:
                        gate(b + 1, nu)

                batches(pe, step)


def decoder_layer(nc, x, xT, ctxT, wqT, wkT, wv, wpair, bq, bk, bv, bo, WsT, WeT, Wg, bias, out):
    NB, S, D = x.shape
    NPAIR, (DK, H) = wpair.shape[0], bv.shape
    y_steps = nc.dram_tensor("y_steps_scratch", [3 * NB, S, D], F32).ap()
    xparts, cparts = (nc.dram_tensor(f"{n}_scratch", [NB, P, 2 * (D // P) * S], F32).ap() for n in ("x1T", "ctxT"))
    wparts = [nc.dram_tensor(f"{n}_scratch", [NPAIR, P, 2 * D], F32).ap() for n in ("wq", "wk", "wv", "wo")]
    with ExitStack() as ctx:
        sc = Scope(nc, ctx, "all")
        ident = sc.sb("ident", [P, P])
        made = sc.sem("ident_made")
        with nc.Block() as block:
            @block.gpsimd
            def _(pool):
                nc.gpsimd.memset(ident[:, :], 0.0).then_inc(made, 1)
                pool.wait_ge(made, 1)
                nc.gpsimd.affine_select(out=ident[:, :], in_=ident[:, :], compare_op=ALU.not_equal, fill=1.0, base=0,
                                        pattern=[[-1, P]], channel_multiplier=1).then_inc(made, 1)
        held = Held(sc, D)
        with ExitStack() as first_half:
            sx = Scope(nc, first_half, "x")
            xraw = sx.sb("raw", [P, D // P, S])
            xT_loaded, x_hi, x_lo = (sx.sem(n) for n in ("T_loaded", "hi", "lo"))
            load_weights(nc, wqT, wkT, wv, xT, held.first, held.second, xraw, held.third, xT_loaded, x_hi, x_lo, D)
            self_attention(nc, x, xT, ctxT, wpair, held, xraw, xT_loaded, x_hi, x_lo, ident, y_steps, xparts, cparts,
                           wparts, NB, S, D, float(NB) ** -0.5)
        held.begin_x2(sc, S // P, D)
        cross_attention(nc, y_steps, xparts, cparts, *wparts, bq, bk, bv, bo, WsT, held, ident, NB, S, D, H, DK)
        feed_forward(nc, y_steps[2 * NB:3 * NB], WeT, Wg, bias, held, ident, out, NB, S, D, Wg.shape[1])


def kernel(x, ctx_1024, L0_attn_W, L0_xattn_Wq, L0_xattn_bq, L0_xattn_Wk, L0_xattn_bk, L0_xattn_Wv, L0_xattn_bv,
           L0_xattn_Wo, L0_xattn_bo, L0_ffn_cond, L0_ffn_mask, L0_ffn_W_shared, L0_ffn_W_expert, L0_ffn_W_gate,
           L0_ffn_bias):
    import numpy as np
    import concourse.bacc as bacc
    from concourse.bass_utils import run_bass_kernel_spmd

    D, H, DK = x.shape[2], 16, 64
    K, PAIRS = D // P, H * DK // P

    def pair_columns(w):
        return w.reshape(K, P, PAIRS, P).transpose(2, 1, 0, 3).reshape(PAIRS, P, K * P)

    W, Wq, Wk, Wv, Wo = (np.asarray(a) for a in (L0_attn_W, L0_xattn_Wq, L0_xattn_Wk, L0_xattn_Wv, L0_xattn_Wo))
    halves = Wv.reshape(K, P, 2, Wv.shape[1] // 2).transpose(2, 0, 1, 3).reshape(PAIRS, P, Wv.shape[1] // 2)
    arrays = {
        "x": np.asarray(x), "xT": np.asarray(x).transpose(0, 2, 1), "ctxT": np.asarray(ctx_1024).transpose(0, 2, 1),
        "wqT": W[:, :D].T, "wkT": W[:, D:2 * D].T, "wv": W[:, 2 * D:],
        "wpair": np.stack([pair_columns(Wq), pair_columns(Wk), halves, Wo.reshape(PAIRS, P, D)], axis=1),
        "bq": np.asarray(L0_xattn_bq).reshape(PAIRS, P).T, "bk": np.asarray(L0_xattn_bk).reshape(PAIRS, P).T,
        "bv": np.asarray(L0_xattn_bv).reshape(H, DK).T, "bo": np.asarray(L0_xattn_bo).reshape(1, D),
        "WsT": np.asarray(L0_ffn_W_shared).T, "WeT": np.asarray(L0_ffn_W_expert).T,
        "Wg": np.asarray(L0_ffn_W_gate), "bias": np.asarray(L0_ffn_bias).reshape(1, D)}
    arrays = {f"in_{name}": np.ascontiguousarray(a) for name, a in arrays.items()}
    nc = bacc.Bacc("TRN2", target_bir_lowering=False, num_devices=1)
    args = [nc.dram_tensor(name, a.shape, mybir.dt.from_np(a.dtype), kind="ExternalInput").ap()
            for name, a in arrays.items()]
    args.append(nc.dram_tensor("out", x.shape, F32, kind="ExternalOutput").ap())
    decoder_layer(nc, *args)
    return run_bass_kernel_spmd(nc, [arrays], core_ids=[0]).results[0]["out"]
```
